# Optimizing a Trainium2 kernel written in Bass

```python
import numpy as np
import jax
import jax.numpy as jnp

def _softmax(x, axis=-1):
    return jax.nn.softmax(x, axis=axis)

def _gelu(x):
    return jax.nn.gelu(x, approximate=True)

def _silu(x):
    return jax.nn.silu(x)

def _sigmoid(x):
    return jax.nn.sigmoid(x)

def _layernorm(x, axis=-1, eps=1e-05):
    m = jnp.mean(x, axis=axis, keepdims=True)
    v = jnp.var(x, axis=axis, keepdims=True)
    return (x - m) / jnp.sqrt(v + eps)

def _scatter_add(tgt, idx, src, axis=0):
    return tgt.at[idx].add(src)

def _segment_sum(src, seg, n):
    return jax.ops.segment_sum(src, seg, n)
kernel_name = 'mk_decoder_preln_d4_seqx_r8_628816'

def setup_inputs(seed: int=0):
    np.random.seed(seed)
    _w = jnp.asarray

    def _rec_inputs():
        import jax
        import jax.numpy as jnp
        _rk = jax.random.key(seed)
        x = 7.22e-05 + 1 * jax.random.normal(jax.random.fold_in(_rk, 1), (4, 512, 128), jnp.float32)
        _lenS = 512 - jax.random.randint(jax.random.fold_in(_rk, 7), (4,), 0, max(1, 512 // 4) + 1, jnp.int32)
        _lenS2 = 77 - jax.random.randint(jax.random.fold_in(_rk, 8), (4,), 0, max(1, 77 // 4) + 1, jnp.int32)
        _ctx_1024P = jax.random.normal(jax.random.fold_in(_rk, 11), (4, 16, 128), jnp.float32)
        _ctx_1024c = jax.random.dirichlet(jax.random.fold_in(_rk, 511), 0.3 * jnp.ones((16,), jnp.float32), (4, 77))
        _ctx_1024t = jnp.einsum('bsk,bkd->bsd', _ctx_1024c, _ctx_1024P)
        _ctx_1024t = _ctx_1024t * jax.lax.rsqrt(jnp.mean(jnp.square(_ctx_1024t)) + 1e-12) * 0.953939
        ctx_1024 = 4.13588e-05 + 0.999923 * (_ctx_1024t + 0.3 * jax.random.normal(jax.random.fold_in(_rk, 611), (4, 77, 128), jnp.float32))
        _validS = jnp.arange(512)[None, :] < _lenS[:, None]
        _validS2 = jnp.arange(77)[None, :] < _lenS2[:, None]
        _causal = jnp.tril(jnp.ones((512, 512), dtype=bool))
        mask_BxS2_bf0 = jnp.logical_not(jnp.ones((4, 77), dtype=bool))
        return (x, ctx_1024, mask_BxS2_bf0)
    x, ctx_1024, mask_BxS2_bf0 = _rec_inputs()

    def _L0_attn_setup():
        import jax, jax.numpy as jnp
        import numpy as np
        import math
        N_HEADS = 16
        FACTOR = 5
        key = jax.random.key(seed)
        ks = jax.random.split(key, 9)
        B, T, D = (2, 256, 128)
        s = D ** (-0.5)
        return {'x': jax.random.normal(ks[0], (B, T, D), dtype=jnp.float32), 'Wq': jax.random.normal(ks[1], (D, D), dtype=jnp.float32) * s, 'bq': jnp.zeros((D,), dtype=jnp.float32), 'Wk': jax.random.normal(ks[2], (D, D), dtype=jnp.float32) * s, 'bk': jnp.zeros((D,), dtype=jnp.float32), 'Wv': jax.random.normal(ks[3], (D, D), dtype=jnp.float32) * s, 'bv': jnp.zeros((D,), dtype=jnp.float32), 'Wo': jax.random.normal(ks[4], (D, D), dtype=jnp.float32) * s, 'bo': jnp.zeros((D,), dtype=jnp.float32)}
    _L0_attn_all = _L0_attn_setup()
    _L0_attn_in = {k: v for k, v in _L0_attn_all.items() if k in ('Wq', 'bq', 'Wk', 'bk', 'Wv', 'bv', 'Wo', 'bo')}
    del _L0_attn_all

    def _L0_xattn_setup():
        import jax, jax.numpy as jnp
        import numpy as np
        EMBED = 128
        B, S = (4, 256)
        key = jax.random.key(seed)
        k1, k2, k3, k4, k5, k6 = jax.random.split(key, 6)
        scale = 1.0 / np.sqrt(EMBED)
        return {'query': jax.random.normal(k1, (B, S, EMBED), dtype=jnp.float32), 'key': jax.random.normal(k2, (B, S, EMBED), dtype=jnp.float32), 'value': jax.random.normal(k3, (B, S, EMBED), dtype=jnp.float32), 'Q_W': jax.random.normal(k4, (EMBED, EMBED), dtype=jnp.float32) * scale, 'K_W': jax.random.normal(k5, (EMBED, EMBED), dtype=jnp.float32) * scale, 'V_W': jax.random.normal(k6, (EMBED, EMBED), dtype=jnp.float32) * scale}
    _L0_xattn_all = _L0_xattn_setup()
    _L0_xattn_in = {k: v for k, v in _L0_xattn_all.items() if k in ('Q_W', 'K_W', 'V_W')}
    del _L0_xattn_all

    def _L0_ffn_setup():
        import jax, jax.numpy as jnp
        import numpy as np
        DIM = 128
        DEPTH = 2
        HEADS = 8
        DIM_HEAD = 64
        WINDOW = 64
        INNER = HEADS * DIM_HEAD
        HID = int(DIM * 4 * 2 / 3)
        B, N = (2, 1024)
        QK_SCALE = 8.0

        def shift_token(t):
            t1, t2 = jnp.split(t, 2, axis=-1)
            t2 = jnp.pad(t2, ((0, 0), (1, 0), (0, 0)))[:, :-1]
            return jnp.concatenate([t1, t2], axis=-1)

        def l2norm(t):
            return t / jnp.clip(jnp.linalg.norm(t, axis=-1, keepdims=True), 1e-12)

        def rotate_half(x):
            x1, x2 = jnp.split(x, 2, axis=-1)
            return jnp.concatenate([-x2, x1], axis=-1)

        def rotary_xpos(q, k):
            n = q.shape[-2]
            half_idx = jnp.arange(0, DIM_HEAD, 2, dtype=jnp.float32)
            inv_freq = 1.0 / 10000.0 ** (half_idx / DIM_HEAD)
            t = jnp.arange(n, dtype=jnp.float32)
            freqs = t[:, None] * inv_freq[None, :]
            freqs = jnp.concatenate([freqs, freqs], axis=-1)
            base = (half_idx + 0.4 * DIM_HEAD) / (1.4 * DIM_HEAD)
            power = (t - n // 2) / float(WINDOW // 2)
            scale = base[None, :] ** power[:, None]
            scale = jnp.concatenate([scale, scale], axis=-1)
            cos, sin = (jnp.cos(freqs), jnp.sin(freqs))
            q = q * cos * scale + rotate_half(q) * sin * scale
            k = k * cos / scale + rotate_half(k) * sin / scale
            return (q, k)

        def local_attention(q, k, v):
            b, h, n, d = q.shape
            w = n // WINDOW
            bq = q.reshape(b, h, w, WINDOW, d) * QK_SCALE
            bk = k.reshape(b, h, w, WINDOW, d)
            bv = v.reshape(b, h, w, WINDOW, d)

            def look_around(t):
                p = jnp.pad(t, ((0, 0), (0, 0), (1, 0), (0, 0), (0, 0)))
                return jnp.concatenate([p[:, :, :w], p[:, :, 1:]], axis=3)
            bk, bv = (look_around(bk), look_around(bv))
            bt = jnp.arange(n).reshape(w, WINDOW)
            btp = jnp.pad(bt, ((1, 0), (0, 0)), constant_values=-1)
            btk = jnp.concatenate([btp[:w], btp[1:]], axis=1)
            sim = jnp.einsum('bhwid,bhwjd->bhwij', bq, bk)
            i = bt[:, :, None]
            j = btk[:, None, :]
            mask = (i < j) | (i > j + WINDOW) | (j == -1)
            sim = jnp.where(mask, -jnp.finfo(sim.dtype).max, sim)
            attn = jax.nn.softmax(sim, axis=-1)
            out = jnp.einsum('bhwij,bhwjd->bhwid', attn, bv)
            return out.reshape(b, h, n, d)

        def _layer(x, wqkv, qs, ksc, wo, lg, lb, w1, b1, w2, b2):
            b, n, _ = x.shape
            h = shift_token(x)
            qkv = h @ wqkv
            q, k, v = jnp.split(qkv, 3, axis=-1)
            to_heads = lambda t: t.reshape(b, n, HEADS, DIM_HEAD).transpose(0, 2, 1, 3)
            q, k, v = (to_heads(q), to_heads(k), to_heads(v))
            q = l2norm(q) * qs
            k = l2norm(k) * ksc
            q, k = rotary_xpos(q, k)
            o = local_attention(q, k, v)
            o = o.transpose(0, 2, 1, 3).reshape(b, n, INNER)
            x = x + o @ wo
            h = shift_token(x)
            mu = h.mean(-1, keepdims=True)
            var = h.var(-1, keepdims=True)
            h = (h - mu) / jnp.sqrt(var + 1e-05) * lg + lb
            h = h @ w1 + b1
            a, g = jnp.split(h, 2, axis=-1)
            h = a * jax.nn.gelu(g, approximate=False)
            x = x + h @ w2 + b2
            return x
        key = jax.random.key(seed)
        ks = jax.random.split(key, 6)
        return {'x': jax.random.normal(ks[0], (B, N, DIM), jnp.float32), 'wqkv': jax.random.normal(ks[1], (DEPTH, DIM, 3 * INNER), jnp.float32) * 0.02, 'q_scale': jnp.ones((DEPTH, DIM_HEAD), jnp.float32), 'k_scale': jnp.ones((DEPTH, DIM_HEAD), jnp.float32), 'wo': jax.random.normal(ks[2], (DEPTH, INNER, DIM), jnp.float32) * 0.02, 'ln_g': jnp.ones((DEPTH, DIM), jnp.float32), 'ln_b': jnp.zeros((DEPTH, DIM), jnp.float32), 'w1': jax.random.normal(ks[3], (DEPTH, DIM, 2 * HID), jnp.float32) * 0.02, 'b1': jnp.zeros((DEPTH, 2 * HID), jnp.float32), 'w2': jax.random.normal(ks[4], (DEPTH, HID, DIM), jnp.float32) * 0.02, 'b2': jnp.zeros((DEPTH, DIM), jnp.float32)}
    _L0_ffn_all = _L0_ffn_setup()
    _L0_ffn_in = {k: v for k, v in _L0_ffn_all.items() if k in ('wqkv', 'q_scale', 'k_scale', 'wo', 'ln_g', 'ln_b', 'w1', 'b1', 'w2', 'b2')}
    del _L0_ffn_all

    def _L1_attn_setup():
        import jax, jax.numpy as jnp
        import numpy as np
        B, S, E, H = (4, 128, 128, 16)
        D = E // H
        NEG_INF = -1000000000.0

        def _xavier(key, shape, fan_in, fan_out):
            a = (6.0 / (fan_in + fan_out)) ** 0.5
            return jax.random.uniform(key, shape, jnp.float32, -a, a)
        key = jax.random.key(seed)
        kx, kq, kk, kv, ko = jax.random.split(key, 5)
        x = jax.random.normal(kx, (B, S, E), jnp.float32)
        Wq = _xavier(kq, (H, D, D), D, D)
        Wk = _xavier(kk, (H, D, D), D, D)
        Wv = _xavier(kv, (H, D, D), D, D)
        W_O = _xavier(ko, (E, E), E, E)
        return {'x': x, 'Wq': Wq, 'Wk': Wk, 'Wv': Wv, 'W_O': W_O}
    _L1_attn_all = _L1_attn_setup()
    _L1_attn_in = {k: v for k, v in _L1_attn_all.items() if k in ('Wq', 'Wk', 'Wv', 'W_O')}
    del _L1_attn_all

    def _L1_xattn_setup():
        import jax, jax.numpy as jnp
        import numpy as np
        D_MODEL = 128
        B, S = (4, 256)
        key = jax.random.key(seed)
        ks = jax.random.split(key, 10)
        s = 1.0 / np.sqrt(D_MODEL)
        return {'k': jax.random.normal(ks[0], (B, S, D_MODEL), jnp.float32), 'v': jax.random.normal(ks[1], (B, S, D_MODEL), jnp.float32), 'q': jax.random.normal(ks[2], (B, S, D_MODEL), jnp.float32), 'Wk': jax.random.normal(ks[3], (D_MODEL, D_MODEL), jnp.float32) * s, 'Wv': jax.random.normal(ks[4], (D_MODEL, D_MODEL), jnp.float32) * s, 'bv': jnp.zeros((D_MODEL,), jnp.float32), 'Wq': jax.random.normal(ks[5], (D_MODEL, D_MODEL), jnp.float32) * s, 'bq': jnp.zeros((D_MODEL,), jnp.float32), 'Wo': jax.random.normal(ks[6], (D_MODEL, D_MODEL), jnp.float32) * s, 'bo': jnp.zeros((D_MODEL,), jnp.float32)}
    _L1_xattn_all = _L1_xattn_setup()
    _L1_xattn_in = {k: v for k, v in _L1_xattn_all.items() if k in ('Wk', 'Wv', 'bv', 'Wq', 'bq', 'Wo', 'bo')}
    del _L1_xattn_all

    def _L1_ffn_setup():
        import jax, jax.numpy as jnp
        import numpy as np
        D = 128
        E = 8
        H = 256
        TOP_K = 2
        ALPHA = 0.5
        LN_EPS = 1e-05

        def _experts_all(x, W1, b1, W2, b2):
            h = jax.nn.relu(jnp.einsum('bld,edh->eblh', x, W1) + b1[:, None, None, :])
            return jnp.einsum('eblh,ehd->ebld', h, W2) + b2[:, None, None, :]

        def _selected_expert(x, expert_idx, W1, b1, W2, b2):
            oh = jax.nn.one_hot(expert_idx, E, dtype=x.dtype)
            return jnp.einsum('ebld,ble->bld', _experts_all(x, W1, b1, W2, b2), oh)

        def _layer_norm(x, gamma, beta):
            mu = jnp.mean(x, axis=-1, keepdims=True)
            var = jnp.mean(jnp.square(x - mu), axis=-1, keepdims=True)
            return (x - mu) * jax.lax.rsqrt(var + LN_EPS) * gamma + beta
        key = jax.random.key(seed)
        ks = jax.random.split(key, 8)
        x = jax.random.normal(ks[0], (2, 256, D), dtype=jnp.float32)
        gate_W = jax.random.normal(ks[1], (D, E), dtype=jnp.float32) * 0.02
        gate_b = jnp.zeros((E,), dtype=jnp.float32)
        W1 = jax.random.normal(ks[2], (E, D, H), dtype=jnp.float32) * 0.02
        b1 = jnp.zeros((E, H), dtype=jnp.float32)
        W2 = jax.random.normal(ks[3], (E, H, D), dtype=jnp.float32) * 0.02
        b2 = jnp.zeros((E, D), dtype=jnp.float32)
        ln_gamma = jnp.ones((D,), dtype=jnp.float32)
        ln_beta = jnp.zeros((D,), dtype=jnp.float32)
        return {'x': x, 'gate_W': gate_W, 'gate_b': gate_b, 'W1': W1, 'b1': b1, 'W2': W2, 'b2': b2, 'ln_gamma': ln_gamma, 'ln_beta': ln_beta}
    _L1_ffn_all = _L1_ffn_setup()
    _L1_ffn_in = {k: v for k, v in _L1_ffn_all.items() if k in ('gate_W', 'gate_b', 'W1', 'b1', 'W2', 'b2', 'ln_gamma', 'ln_beta')}
    del _L1_ffn_all

    def _L2_attn_setup():
        import jax, jax.numpy as jnp
        import numpy as np
        B, S, DIN, DOUT, H, KVH = (2, 256, 128, 128, 16, 16)
        HD = DOUT // H
        CB = 16
        CS = 16
        SB = 8
        TOPK = 2
        WIN = 32
        SCALE = 1.0 / np.sqrt(HD)

        def _rope(x, hd):
            b, s, d = x.shape
            xh = x.reshape(b, s, d // hd, hd)
            half = hd // 2
            inv = 1.0 / 10000.0 ** (jnp.arange(half, dtype=jnp.float32) * 2.0 / hd)
            ang = jnp.arange(s, dtype=jnp.float32)[:, None] * inv[None, :]
            cos = jnp.cos(ang)[None, :, None, :]
            sin = jnp.sin(ang)[None, :, None, :]
            x1, x2 = (xh[..., 0::2], xh[..., 1::2])
            out = jnp.stack([x1 * cos - x2 * sin, x1 * sin + x2 * cos], axis=-1)
            return out.reshape(b, s, d)

        def _masked_softmax(scores, mask):
            s = jnp.where(mask, scores, -jnp.inf)
            m = jnp.max(s, axis=-1, keepdims=True)
            m = jnp.where(jnp.isfinite(m), m, jnp.zeros_like(m))
            e = jnp.exp(s - m)
            den = jnp.sum(e, axis=-1, keepdims=True)
            return jnp.where(den > 0, e / jnp.where(den > 0, den, 1.0), jnp.zeros_like(e))
        key = jax.random.key(seed)
        ks = jax.random.split(key, 12)
        sc_in = 1.0 / np.sqrt(DIN)
        sc_out = 1.0 / np.sqrt(DOUT)
        return {'x': jax.random.normal(ks[0], (B, S, DIN), jnp.float32), 'Wq': jax.random.normal(ks[1], (DIN, DOUT), jnp.float32) * sc_in, 'Wk': jax.random.normal(ks[2], (DIN, KVH * HD), jnp.float32) * sc_in, 'Wv': jax.random.normal(ks[3], (DIN, KVH * HD), jnp.float32) * sc_in, 'Wo': jax.random.normal(ks[4], (DOUT, DOUT), jnp.float32) * sc_out, 'bo': jnp.zeros((DOUT,), jnp.float32), 'wk_comp': jax.random.normal(ks[5], (CB,), jnp.float32), 'wv_comp': jax.random.normal(ks[6], (CB,), jnp.float32), 'pe': jax.random.normal(ks[7], (CB, KVH * HD), jnp.float32), 'Wg': jax.random.normal(ks[8], (DIN, 3), jnp.float32) * sc_in, 'bg': jnp.zeros((3,), jnp.float32)}
    _L2_attn_all = _L2_attn_setup()
    _L2_attn_in = {k: v for k, v in _L2_attn_all.items() if k in ('Wq', 'Wk', 'Wv', 'Wo', 'bo', 'wk_comp', 'wv_comp', 'pe', 'Wg', 'bg')}
    del _L2_attn_all

    def _L2_xattn_setup():
        import jax, jax.numpy as jnp
        import numpy as np
        B, L1, L2, FULL, H = (8, 256, 256, 128, 128)
        NEG_INF = -1e+30
        key = jax.random.key(seed)
        k1, k2, k3, k4, k5 = jax.random.split(key, 5)
        xh1 = jax.random.normal(k1, (B, L1, FULL), dtype=jnp.float32)
        xh2 = jax.random.normal(k2, (B, L2, FULL), dtype=jnp.float32)
        x2 = jax.random.normal(k3, (B, L2, H), dtype=jnp.float32)
        x2_mask = jnp.zeros((B, L2), dtype=bool)
        W = jax.random.normal(k4, (FULL, FULL), dtype=jnp.float32) / np.sqrt(FULL)
        b = jnp.zeros((FULL,), dtype=jnp.float32)
        D = jnp.ones((1, FULL), dtype=jnp.float32)
        return {'xh1': xh1, 'xh2': xh2, 'x2': x2, 'x2_mask': x2_mask, 'W': W, 'b': b, 'D': D}
    _L2_xattn_all = _L2_xattn_setup()
    _L2_xattn_in = {k: v for k, v in _L2_xattn_all.items() if k in ('W', 'b', 'D')}
    del _L2_xattn_all

    def _L2_ffn_setup():
        import jax, jax.numpy as jnp
        import numpy as np
        D_MODEL = 128
        N_EXPERTS = 8
        TOP_K = 2
        BOTTLENECK = 64
        B, S = (2, 512)
        ADAPTER_SCALE = 0.5

        def _moe_forward(x, w_gate, w_noise, Wd, bd, Wu, bu):
            b, s, d = x.shape
            xf = x.reshape(-1, d)
            T = xf.shape[0]
            clean_logits = xf @ w_gate
            logits = clean_logits
            k1 = min(TOP_K + 1, N_EXPERTS)
            top_logits, top_idx = jax.lax.top_k(logits, k1)
            top_k_logits = top_logits[:, :TOP_K]
            top_k_idx = top_idx[:, :TOP_K]
            top_k_gates = jax.nn.softmax(top_k_logits, axis=-1)
            rows = jnp.arange(T)[:, None]
            gates = jnp.zeros((T, N_EXPERTS), dtype=top_k_gates.dtype)
            gates = gates.at[rows, top_k_idx].set(top_k_gates)
            h = jax.nn.relu(jnp.einsum('td,edb->teb', xf, Wd) + bd[None, :, :])
            y = jnp.einsum('teb,ebd->ted', h, Wu) + bu[None, :, :]
            y = ADAPTER_SCALE * y
            out = jnp.einsum('te,ted->td', gates, y)
            return out.reshape(b, s, d)
        key = jax.random.key(seed)
        ks = jax.random.split(key, 8)
        sd = 0.02
        x = jax.random.normal(ks[0], (B, S, D_MODEL), dtype=jnp.float32)
        w_gate = jax.random.normal(ks[1], (D_MODEL, N_EXPERTS), dtype=jnp.float32) * sd
        w_noise = jax.random.normal(ks[2], (D_MODEL, N_EXPERTS), dtype=jnp.float32) * sd
        Wd = jax.random.normal(ks[3], (N_EXPERTS, D_MODEL, BOTTLENECK), dtype=jnp.float32) * sd
        bd = jnp.zeros((N_EXPERTS, BOTTLENECK), dtype=jnp.float32)
        Wu = jax.random.normal(ks[4], (N_EXPERTS, BOTTLENECK, D_MODEL), dtype=jnp.float32) * sd
        bu = jnp.zeros((N_EXPERTS, D_MODEL), dtype=jnp.float32)
        return {'x': x, 'w_gate': w_gate, 'w_noise': w_noise, 'Wd': Wd, 'bd': bd, 'Wu': Wu, 'bu': bu}
    _L2_ffn_all = _L2_ffn_setup()
    _L2_ffn_in = {k: v for k, v in _L2_ffn_all.items() if k in ('w_gate', 'w_noise', 'Wd', 'bd', 'Wu', 'bu')}
    del _L2_ffn_all

    def _L3_attn_setup():
        import jax, jax.numpy as jnp
        import numpy as np
        H = 128
        E = 256
        N = 16
        R = 64
        K = 4
        B = 2
        L = 256
        EPS = 1e-05

        def _layernorm(x, w, b):
            mu = jnp.mean(x, axis=-1, keepdims=True)
            var = jnp.mean(jnp.square(x - mu), axis=-1, keepdims=True)
            return (x - mu) * jax.lax.rsqrt(var + EPS) * w + b

        def _causal_dw_conv(x, conv_w, conv_b):
            xc = jnp.transpose(x, (0, 2, 1))
            kern = conv_w[:, None, :]
            y = jax.lax.conv_general_dilated(xc, kern, window_strides=(1,), padding=[(K - 1, 0)], feature_group_count=E, dimension_numbers=('NCH', 'OIH', 'NCH'))
            y = y + conv_b[None, :, None]
            return jnp.transpose(y, (0, 2, 1))

        def _selective_scan(x, x_proj_w, dt_proj_w, dt_proj_b, A_log, D):
            dbc = jnp.einsum('ble,ep->blp', x, x_proj_w)
            dt_r, Bm, Cm = jnp.split(dbc, [R, R + N], axis=-1)
            dt = jax.nn.softplus(jnp.einsum('blr,re->ble', dt_r, dt_proj_w) + dt_proj_b)
            A = -jnp.exp(A_log)

            def step(h, inp):
                x_t, dt_t, B_t, C_t = inp
                dA = jnp.exp(dt_t[..., None] * A)
                h = dA * h + dt_t[..., None] * B_t[:, None, :] * x_t[..., None]
                y = jnp.einsum('ben,bn->be', h, C_t)
                return (h, y)
            xs = (jnp.transpose(x, (1, 0, 2)), jnp.transpose(dt, (1, 0, 2)), jnp.transpose(Bm, (1, 0, 2)), jnp.transpose(Cm, (1, 0, 2)))
            h0 = jnp.zeros((x.shape[0], E, N), x.dtype)
            _, ys = jax.lax.scan(step, h0, xs)
            y = jnp.transpose(ys, (1, 0, 2))
            return y + x * D
        key = jax.random.key(seed)
        ks = jax.random.split(key, 8)
        s = 0.02
        return {'hidden_states': jax.random.normal(ks[0], (B, L, H), jnp.float32), 'ln_w': jnp.ones((H,), jnp.float32), 'ln_b': jnp.zeros((H,), jnp.float32), 'in_proj_w': jax.random.normal(ks[1], (H, 2 * E), jnp.float32) * s, 'in_proj_b': jnp.zeros((2 * E,), jnp.float32), 'conv_w': jax.random.normal(ks[2], (E, K), jnp.float32) * s, 'conv_b': jnp.zeros((E,), jnp.float32), 'x_proj_w': jax.random.normal(ks[3], (E, R + 2 * N), jnp.float32) * s, 'dt_proj_w': jax.random.normal(ks[4], (R, E), jnp.float32) * s, 'dt_proj_b': jax.random.uniform(ks[5], (E,), jnp.float32, -5.0, -3.0), 'A_log': jnp.log(jnp.broadcast_to(jnp.arange(1, N + 1, dtype=jnp.float32), (E, N))), 'D': jnp.ones((E,), jnp.float32), 'out_proj_w': jax.random.normal(ks[6], (E, H), jnp.float32) * s, 'out_proj_b': jnp.zeros((H,), jnp.float32)}
    _L3_attn_all = _L3_attn_setup()
    _L3_attn_in = {k: v for k, v in _L3_attn_all.items() if k in ('ln_w', 'ln_b', 'in_proj_w', 'in_proj_b', 'conv_w', 'conv_b', 'x_proj_w', 'dt_proj_w', 'dt_proj_b', 'A_log', 'D', 'out_proj_w', 'out_proj_b')}
    del _L3_attn_all

    def _L3_xattn_setup():
        import jax, jax.numpy as jnp
        import numpy as np
        import math
        EMBED_DIM = 128
        NUM_HEADS = 16
        HEAD_DIM = EMBED_DIM // NUM_HEADS
        SUB_HEAD_DIM = HEAD_DIM // 2
        SCALING = 1.0 / math.sqrt(SUB_HEAD_DIM)
        LAMBDA_INIT = 0.8 - 0.6 * math.exp(-0.3 * 0)
        key = jax.random.key(seed)
        ks = jax.random.split(key, 10)
        B, T, D = (2, 256, EMBED_DIM)
        xav = math.sqrt(6.0 / (D + D))
        return {'query': jax.random.normal(ks[0], (B, T, D), jnp.float32), 'key': jax.random.normal(ks[1], (B, T, D), jnp.float32), 'value': jax.random.normal(ks[2], (B, T, D), jnp.float32), 'in_proj_weight': jax.random.uniform(ks[3], (3 * D, D), jnp.float32, -xav, xav), 'in_proj_bias': jnp.zeros((3 * D,), jnp.float32), 'out_proj_weight': jax.random.uniform(ks[4], (D, D), jnp.float32, -xav, xav), 'out_proj_bias': jnp.zeros((D,), jnp.float32), 'lambda_q1': 0.1 * jax.random.normal(ks[5], (SUB_HEAD_DIM,), jnp.float32), 'lambda_k1': 0.1 * jax.random.normal(ks[6], (SUB_HEAD_DIM,), jnp.float32), 'lambda_q2': 0.1 * jax.random.normal(ks[7], (SUB_HEAD_DIM,), jnp.float32), 'lambda_k2': 0.1 * jax.random.normal(ks[8], (SUB_HEAD_DIM,), jnp.float32)}
    _L3_xattn_all = _L3_xattn_setup()
    _L3_xattn_in = {k: v for k, v in _L3_xattn_all.items() if k in ('in_proj_weight', 'in_proj_bias', 'out_proj_weight', 'out_proj_bias', 'lambda_q1', 'lambda_k1', 'lambda_q2', 'lambda_k2')}
    del _L3_xattn_all

    def _L3_ffn_setup():
        import jax, jax.numpy as jnp
        import numpy as np
        HIDDEN = 128
        INNER = 512

        def _weight_quant(w):
            scale = 1.0 / jnp.clip(jnp.mean(jnp.abs(w)), 1e-05)
            wq = jnp.clip(jnp.round(w * scale), -1.0, 1.0) / scale
            return w + jax.lax.stop_gradient(wq - w)

        def _act_quant(x):
            scale = 127.0 / jnp.clip(jnp.max(jnp.abs(x), axis=-1, keepdims=True), 1e-05)
            xq = jnp.clip(jnp.round(x * scale), -128.0, 127.0) / scale
            return x + jax.lax.stop_gradient(xq - x)

        def _bitlinear(x, w):
            return jnp.einsum('bsi,oi->bso', _act_quant(x), _weight_quant(w))
        key = jax.random.key(seed)
        k0, k1, k2, k3 = jax.random.split(key, 4)
        x = jax.random.normal(k0, (4, 256, HIDDEN), dtype=jnp.float32)
        w_gate = jax.random.normal(k1, (INNER, HIDDEN), dtype=jnp.float32) / np.sqrt(HIDDEN)
        w_up = jax.random.normal(k2, (INNER, HIDDEN), dtype=jnp.float32) / np.sqrt(HIDDEN)
        w_down = jax.random.normal(k3, (HIDDEN, INNER), dtype=jnp.float32) / np.sqrt(INNER)
        return {'x': x, 'w_gate': w_gate, 'w_up': w_up, 'w_down': w_down}
    _L3_ffn_all = _L3_ffn_setup()
    _L3_ffn_in = {k: v for k, v in _L3_ffn_all.items() if k in ('w_gate', 'w_up', 'w_down')}
    del _L3_ffn_all
    return {'x': x, 'ctx_1024': ctx_1024, 'mask_BxS2_bf0': mask_BxS2_bf0, 'L0_attn_Wq': _L0_attn_in['Wq'], 'L0_attn_bq': _L0_attn_in['bq'], 'L0_attn_Wk': _L0_attn_in['Wk'], 'L0_attn_bk': _L0_attn_in['bk'], 'L0_attn_Wv': _L0_attn_in['Wv'], 'L0_attn_bv': _L0_attn_in['bv'], 'L0_attn_Wo': _L0_attn_in['Wo'], 'L0_attn_bo': _L0_attn_in['bo'], 'L0_xattn_Q_W': _L0_xattn_in['Q_W'], 'L0_xattn_K_W': _L0_xattn_in['K_W'], 'L0_xattn_V_W': _L0_xattn_in['V_W'], 'L0_ffn_wqkv': _L0_ffn_in['wqkv'], 'L0_ffn_q_scale': _L0_ffn_in['q_scale'], 'L0_ffn_k_scale': _L0_ffn_in['k_scale'], 'L0_ffn_wo': _L0_ffn_in['wo'], 'L0_ffn_ln_g': _L0_ffn_in['ln_g'], 'L0_ffn_ln_b': _L0_ffn_in['ln_b'], 'L0_ffn_w1': _L0_ffn_in['w1'], 'L0_ffn_b1': _L0_ffn_in['b1'], 'L0_ffn_w2': _L0_ffn_in['w2'], 'L0_ffn_b2': _L0_ffn_in['b2'], 'L1_attn_Wq': _L1_attn_in['Wq'], 'L1_attn_Wk': _L1_attn_in['Wk'], 'L1_attn_Wv': _L1_attn_in['Wv'], 'L1_attn_W_O': _L1_attn_in['W_O'], 'L1_xattn_Wk': _L1_xattn_in['Wk'], 'L1_xattn_Wv': _L1_xattn_in['Wv'], 'L1_xattn_bv': _L1_xattn_in['bv'], 'L1_xattn_Wq': _L1_xattn_in['Wq'], 'L1_xattn_bq': _L1_xattn_in['bq'], 'L1_xattn_Wo': _L1_xattn_in['Wo'], 'L1_xattn_bo': _L1_xattn_in['bo'], 'L1_ffn_gate_W': _L1_ffn_in['gate_W'], 'L1_ffn_gate_b': _L1_ffn_in['gate_b'], 'L1_ffn_W1': _L1_ffn_in['W1'], 'L1_ffn_b1': _L1_ffn_in['b1'], 'L1_ffn_W2': _L1_ffn_in['W2'], 'L1_ffn_b2': _L1_ffn_in['b2'], 'L1_ffn_ln_gamma': _L1_ffn_in['ln_gamma'], 'L1_ffn_ln_beta': _L1_ffn_in['ln_beta'], 'L2_attn_Wq': _L2_attn_in['Wq'], 'L2_attn_Wk': _L2_attn_in['Wk'], 'L2_attn_Wv': _L2_attn_in['Wv'], 'L2_attn_Wo': _L2_attn_in['Wo'], 'L2_attn_bo': _L2_attn_in['bo'], 'L2_attn_wk_comp': _L2_attn_in['wk_comp'], 'L2_attn_wv_comp': _L2_attn_in['wv_comp'], 'L2_attn_pe': _L2_attn_in['pe'], 'L2_attn_Wg': _L2_attn_in['Wg'], 'L2_attn_bg': _L2_attn_in['bg'], 'L2_xattn_W': _L2_xattn_in['W'], 'L2_xattn_b': _L2_xattn_in['b'], 'L2_xattn_D': _L2_xattn_in['D'], 'L2_ffn_w_gate': _L2_ffn_in['w_gate'], 'L2_ffn_w_noise': _L2_ffn_in['w_noise'], 'L2_ffn_Wd': _L2_ffn_in['Wd'], 'L2_ffn_bd': _L2_ffn_in['bd'], 'L2_ffn_Wu': _L2_ffn_in['Wu'], 'L2_ffn_bu': _L2_ffn_in['bu'], 'L3_attn_ln_w': _L3_attn_in['ln_w'], 'L3_attn_ln_b': _L3_attn_in['ln_b'], 'L3_attn_in_proj_w': _L3_attn_in['in_proj_w'], 'L3_attn_in_proj_b': _L3_attn_in['in_proj_b'], 'L3_attn_conv_w': _L3_attn_in['conv_w'], 'L3_attn_conv_b': _L3_attn_in['conv_b'], 'L3_attn_x_proj_w': _L3_attn_in['x_proj_w'], 'L3_attn_dt_proj_w': _L3_attn_in['dt_proj_w'], 'L3_attn_dt_proj_b': _L3_attn_in['dt_proj_b'], 'L3_attn_A_log': _L3_attn_in['A_log'], 'L3_attn_D': _L3_attn_in['D'], 'L3_attn_out_proj_w': _L3_attn_in['out_proj_w'], 'L3_attn_out_proj_b': _L3_attn_in['out_proj_b'], 'L3_xattn_in_proj_weight': _L3_xattn_in['in_proj_weight'], 'L3_xattn_in_proj_bias': _L3_xattn_in['in_proj_bias'], 'L3_xattn_out_proj_weight': _L3_xattn_in['out_proj_weight'], 'L3_xattn_out_proj_bias': _L3_xattn_in['out_proj_bias'], 'L3_xattn_lambda_q1': _L3_xattn_in['lambda_q1'], 'L3_xattn_lambda_k1': _L3_xattn_in['lambda_k1'], 'L3_xattn_lambda_q2': _L3_xattn_in['lambda_q2'], 'L3_xattn_lambda_k2': _L3_xattn_in['lambda_k2'], 'L3_ffn_w_gate': _L3_ffn_in['w_gate'], 'L3_ffn_w_up': _L3_ffn_in['w_up'], 'L3_ffn_w_down': _L3_ffn_in['w_down']}

def reference(x, ctx_1024, mask_BxS2_bf0, L0_attn_Wq, L0_attn_bq, L0_attn_Wk, L0_attn_bk, L0_attn_Wv, L0_attn_bv, L0_attn_Wo, L0_attn_bo, L0_xattn_Q_W, L0_xattn_K_W, L0_xattn_V_W, L0_ffn_wqkv, L0_ffn_q_scale, L0_ffn_k_scale, L0_ffn_wo, L0_ffn_ln_g, L0_ffn_ln_b, L0_ffn_w1, L0_ffn_b1, L0_ffn_w2, L0_ffn_b2, L1_attn_Wq, L1_attn_Wk, L1_attn_Wv, L1_attn_W_O, L1_xattn_Wk, L1_xattn_Wv, L1_xattn_bv, L1_xattn_Wq, L1_xattn_bq, L1_xattn_Wo, L1_xattn_bo, L1_ffn_gate_W, L1_ffn_gate_b, L1_ffn_W1, L1_ffn_b1, L1_ffn_W2, L1_ffn_b2, L1_ffn_ln_gamma, L1_ffn_ln_beta, L2_attn_Wq, L2_attn_Wk, L2_attn_Wv, L2_attn_Wo, L2_attn_bo, L2_attn_wk_comp, L2_attn_wv_comp, L2_attn_pe, L2_attn_Wg, L2_attn_bg, L2_xattn_W, L2_xattn_b, L2_xattn_D, L2_ffn_w_gate, L2_ffn_w_noise, L2_ffn_Wd, L2_ffn_bd, L2_ffn_Wu, L2_ffn_bu, L3_attn_ln_w, L3_attn_ln_b, L3_attn_in_proj_w, L3_attn_in_proj_b, L3_attn_conv_w, L3_attn_conv_b, L3_attn_x_proj_w, L3_attn_dt_proj_w, L3_attn_dt_proj_b, L3_attn_A_log, L3_attn_D, L3_attn_out_proj_w, L3_attn_out_proj_b, L3_xattn_in_proj_weight, L3_xattn_in_proj_bias, L3_xattn_out_proj_weight, L3_xattn_out_proj_bias, L3_xattn_lambda_q1, L3_xattn_lambda_k1, L3_xattn_lambda_q2, L3_xattn_lambda_k2, L3_ffn_w_gate, L3_ffn_w_up, L3_ffn_w_down):
    import jax
    import jax.numpy as jnp

    def _L0_attn_ref(x, Wq, bq, Wk, bk, Wv, bv, Wo, bo):
        import jax, jax.numpy as jnp
        import numpy as np
        import math
        N_HEADS = 16
        FACTOR = 5
        B, T, D = x.shape
        H = N_HEADS
        Hd = D // H
        scale = Hd ** (-0.5)

        def proj(W, b):
            return (x @ W + b).reshape(B, T, H, Hd).transpose(0, 2, 1, 3)
        q = proj(Wq, bq)
        k = proj(Wk, bk)
        v = proj(Wv, bv)
        q_norm = jnp.sum(jnp.abs(q), axis=-1)
        u = min(int(FACTOR * math.log(T)), T)
        _, index = jax.lax.top_k(q_norm, u)
        scores = jnp.einsum('bhqd,bhkd->bhqk', q, k) * scale
        causal = jnp.tril(jnp.ones((T, T), dtype=bool))
        scores = jnp.where(causal, scores, -jnp.inf)
        sel_scores = jnp.take_along_axis(scores, index[..., None], axis=2)
        sel_attn = jax.nn.softmax(sel_scores, axis=-1)
        sel_out = jnp.einsum('bhut,bhtd->bhud', sel_attn, v)
        attn_output = jnp.zeros_like(q)
        bI = jnp.arange(B)[:, None, None]
        hI = jnp.arange(H)[None, :, None]
        attn_output = attn_output.at[bI, hI, index].set(sel_out)
        out = attn_output.transpose(0, 2, 1, 3).reshape(B, T, D)
        return out @ Wo + bo

    def _L0_xattn_ref(query, key, value, Q_W, K_W, V_W):
        import jax, jax.numpy as jnp
        import numpy as np
        EMBED = 128
        B, S = (4, 256)
        q = jnp.einsum('bse,oe->bso', query, Q_W)
        k = jnp.einsum('bse,oe->bso', key, K_W)
        v = jnp.einsum('bse,oe->bso', value, V_W)
        scores = jnp.einsum('bqe,bke->bqk', q, k) / jnp.sqrt(jnp.asarray(q.shape[-1], q.dtype))
        attn = jax.nn.softmax(scores, axis=-1)
        out = jnp.einsum('bqs,bse->bqe', attn, v)
        return out

    def _L0_ffn_ref(x, wqkv, q_scale, k_scale, wo, ln_g, ln_b, w1, b1, w2, b2):
        import jax, jax.numpy as jnp
        import numpy as np
        DIM = 128
        DEPTH = 2
        HEADS = 8
        DIM_HEAD = 64
        WINDOW = 64
        INNER = HEADS * DIM_HEAD
        HID = int(DIM * 4 * 2 / 3)
        B, N = (2, 1024)
        QK_SCALE = 8.0

        def shift_token(t):
            t1, t2 = jnp.split(t, 2, axis=-1)
            t2 = jnp.pad(t2, ((0, 0), (1, 0), (0, 0)))[:, :-1]
            return jnp.concatenate([t1, t2], axis=-1)

        def l2norm(t):
            return t / jnp.clip(jnp.linalg.norm(t, axis=-1, keepdims=True), 1e-12)

        def rotate_half(x):
            x1, x2 = jnp.split(x, 2, axis=-1)
            return jnp.concatenate([-x2, x1], axis=-1)

        def rotary_xpos(q, k):
            n = q.shape[-2]
            half_idx = jnp.arange(0, DIM_HEAD, 2, dtype=jnp.float32)
            inv_freq = 1.0 / 10000.0 ** (half_idx / DIM_HEAD)
            t = jnp.arange(n, dtype=jnp.float32)
            freqs = t[:, None] * inv_freq[None, :]
            freqs = jnp.concatenate([freqs, freqs], axis=-1)
            base = (half_idx + 0.4 * DIM_HEAD) / (1.4 * DIM_HEAD)
            power = (t - n // 2) / float(WINDOW // 2)
            scale = base[None, :] ** power[:, None]
            scale = jnp.concatenate([scale, scale], axis=-1)
            cos, sin = (jnp.cos(freqs), jnp.sin(freqs))
            q = q * cos * scale + rotate_half(q) * sin * scale
            k = k * cos / scale + rotate_half(k) * sin / scale
            return (q, k)

        def local_attention(q, k, v):
            b, h, n, d = q.shape
            w = n // WINDOW
            bq = q.reshape(b, h, w, WINDOW, d) * QK_SCALE
            bk = k.reshape(b, h, w, WINDOW, d)
            bv = v.reshape(b, h, w, WINDOW, d)

            def look_around(t):
                p = jnp.pad(t, ((0, 0), (0, 0), (1, 0), (0, 0), (0, 0)))
                return jnp.concatenate([p[:, :, :w], p[:, :, 1:]], axis=3)
            bk, bv = (look_around(bk), look_around(bv))
            bt = jnp.arange(n).reshape(w, WINDOW)
            btp = jnp.pad(bt, ((1, 0), (0, 0)), constant_values=-1)
            btk = jnp.concatenate([btp[:w], btp[1:]], axis=1)
            sim = jnp.einsum('bhwid,bhwjd->bhwij', bq, bk)
            i = bt[:, :, None]
            j = btk[:, None, :]
            mask = (i < j) | (i > j + WINDOW) | (j == -1)
            sim = jnp.where(mask, -jnp.finfo(sim.dtype).max, sim)
            attn = jax.nn.softmax(sim, axis=-1)
            out = jnp.einsum('bhwij,bhwjd->bhwid', attn, bv)
            return out.reshape(b, h, n, d)

        def _layer(x, wqkv, qs, ksc, wo, lg, lb, w1, b1, w2, b2):
            b, n, _ = x.shape
            h = shift_token(x)
            qkv = h @ wqkv
            q, k, v = jnp.split(qkv, 3, axis=-1)
            to_heads = lambda t: t.reshape(b, n, HEADS, DIM_HEAD).transpose(0, 2, 1, 3)
            q, k, v = (to_heads(q), to_heads(k), to_heads(v))
            q = l2norm(q) * qs
            k = l2norm(k) * ksc
            q, k = rotary_xpos(q, k)
            o = local_attention(q, k, v)
            o = o.transpose(0, 2, 1, 3).reshape(b, n, INNER)
            x = x + o @ wo
            h = shift_token(x)
            mu = h.mean(-1, keepdims=True)
            var = h.var(-1, keepdims=True)
            h = (h - mu) / jnp.sqrt(var + 1e-05) * lg + lb
            h = h @ w1 + b1
            a, g = jnp.split(h, 2, axis=-1)
            h = a * jax.nn.gelu(g, approximate=False)
            x = x + h @ w2 + b2
            return x
        for l in range(DEPTH):
            x = _layer(x, wqkv[l], q_scale[l], k_scale[l], wo[l], ln_g[l], ln_b[l], w1[l], b1[l], w2[l], b2[l])
        return x

    def _L1_attn_ref(x, Wq, Wk, Wv, W_O):
        import jax, jax.numpy as jnp
        import numpy as np
        B, S, E, H = (4, 128, 128, 16)
        D = E // H
        NEG_INF = -1000000000.0

        def _xavier(key, shape, fan_in, fan_out):
            a = (6.0 / (fan_in + fan_out)) ** 0.5
            return jax.random.uniform(key, shape, jnp.float32, -a, a)
        b, s, e = x.shape
        h = Wq.shape[0]
        d = e // h
        xh = x.reshape(b, s, h, d).transpose(0, 2, 1, 3)
        Q = jnp.einsum('bhsd,hde->bhse', xh, Wq)
        K = jnp.einsum('bhsd,hde->bhse', xh, Wk)
        V = jnp.einsum('bhsd,hde->bhse', xh, Wv)
        scale = 1.0 / jnp.sqrt(jnp.asarray(d, x.dtype))
        scores = jnp.einsum('bhsd,bhtd->bhst', Q, K) * scale
        causal = jnp.tril(jnp.ones((s, s), bool))
        scores = jnp.where(causal, scores, NEG_INF)
        attn = jax.nn.softmax(scores, axis=-1)
        out = jnp.einsum('bhst,bhtd->bhsd', attn, V)
        cat = out.transpose(0, 2, 1, 3).reshape(b, s, e)
        scrambled = cat.transpose(0, 2, 1).reshape(b, s, e)
        return scrambled @ W_O

    def _L1_xattn_ref(k, v, q, Wk, Wv, bv, Wq, bq, Wo, bo):
        import jax, jax.numpy as jnp
        import numpy as np
        D_MODEL = 128
        B, S = (4, 256)
        kp = jnp.einsum('bsd,ed->bse', k, Wk)
        vp = jnp.einsum('bsd,ed->bse', v, Wv) + bv
        qp = jnp.einsum('bsd,ed->bse', q, Wq) + bq
        scale = 1.0 / jnp.sqrt(jnp.float32(kp.shape[-1]))
        scores = jnp.einsum('bqd,bkd->bqk', qp, kp) * scale
        probs = jax.nn.softmax(scores, axis=-1)
        ctx = jnp.einsum('bqk,bkd->bqd', probs, vp)
        return jnp.einsum('bqd,ed->bqe', ctx, Wo) + bo

    def _L1_ffn_ref(x, gate_W, gate_b, W1, b1, W2, b2, ln_gamma, ln_beta):
        import jax, jax.numpy as jnp
        import numpy as np
        D = 128
        E = 8
        H = 256
        TOP_K = 2
        ALPHA = 0.5
        LN_EPS = 1e-05

        def _experts_all(x, W1, b1, W2, b2):
            h = jax.nn.relu(jnp.einsum('bld,edh->eblh', x, W1) + b1[:, None, None, :])
            return jnp.einsum('eblh,ehd->ebld', h, W2) + b2[:, None, None, :]

        def _selected_expert(x, expert_idx, W1, b1, W2, b2):
            oh = jax.nn.one_hot(expert_idx, E, dtype=x.dtype)
            return jnp.einsum('ebld,ble->bld', _experts_all(x, W1, b1, W2, b2), oh)

        def _layer_norm(x, gamma, beta):
            mu = jnp.mean(x, axis=-1, keepdims=True)
            var = jnp.mean(jnp.square(x - mu), axis=-1, keepdims=True)
            return (x - mu) * jax.lax.rsqrt(var + LN_EPS) * gamma + beta
        residual = x
        gate_logits = jnp.einsum('bld,de->ble', x, gate_W) + gate_b
        gate_weights = jax.nn.softmax(gate_logits, axis=-1)
        topk_vals, topk_idx = jax.lax.top_k(gate_weights, TOP_K)
        boost = jax.lax.stop_gradient(x)
        outs = []
        for i in range(TOP_K):
            eo = _selected_expert(boost, topk_idx[:, :, i], W1, b1, W2, b2)
            outs.append(eo)
            if i < TOP_K - 1:
                boost = boost + ALPHA * jax.lax.stop_gradient(eo)
        fused = sum((topk_vals[:, :, i:i + 1] * outs[i] for i in range(TOP_K)))
        return _layer_norm(residual + fused, ln_gamma, ln_beta)

    def _L2_attn_ref(x, Wq, Wk, Wv, Wo, bo, wk_comp, wv_comp, pe, Wg, bg):
        import jax, jax.numpy as jnp
        import numpy as np
        B, S, DIN, DOUT, H, KVH = (2, 256, 128, 128, 16, 16)
        HD = DOUT // H
        CB = 16
        CS = 16
        SB = 8
        TOPK = 2
        WIN = 32
        SCALE = 1.0 / np.sqrt(HD)

        def _rope(x, hd):
            b, s, d = x.shape
            xh = x.reshape(b, s, d // hd, hd)
            half = hd // 2
            inv = 1.0 / 10000.0 ** (jnp.arange(half, dtype=jnp.float32) * 2.0 / hd)
            ang = jnp.arange(s, dtype=jnp.float32)[:, None] * inv[None, :]
            cos = jnp.cos(ang)[None, :, None, :]
            sin = jnp.sin(ang)[None, :, None, :]
            x1, x2 = (xh[..., 0::2], xh[..., 1::2])
            out = jnp.stack([x1 * cos - x2 * sin, x1 * sin + x2 * cos], axis=-1)
            return out.reshape(b, s, d)

        def _masked_softmax(scores, mask):
            s = jnp.where(mask, scores, -jnp.inf)
            m = jnp.max(s, axis=-1, keepdims=True)
            m = jnp.where(jnp.isfinite(m), m, jnp.zeros_like(m))
            e = jnp.exp(s - m)
            den = jnp.sum(e, axis=-1, keepdims=True)
            return jnp.where(den > 0, e / jnp.where(den > 0, den, 1.0), jnp.zeros_like(e))
        b, s, _ = x.shape
        q = _rope(x @ Wq, HD)
        k = _rope(x @ Wk, HD)
        v = x @ Wv
        nb = (s - CB) // CS + 1
        kb = k[:, :nb * CS].reshape(b, nb, CB, -1) + pe[None, None]
        vb = v[:, :nb * CS].reshape(b, nb, CB, -1) + pe[None, None]
        ck = jnp.einsum('bnkd,k->bnd', kb, wk_comp)
        cv = jnp.einsum('bnkd,k->bnd', vb, wv_comp)
        q4 = q.reshape(b, s, H, HD).transpose(0, 2, 1, 3)
        k4 = k.reshape(b, s, KVH, HD).transpose(0, 2, 1, 3)
        v4 = v.reshape(b, s, KVH, HD).transpose(0, 2, 1, 3)
        ck4 = ck.reshape(b, nb, KVH, HD).transpose(0, 2, 1, 3)
        cv4 = cv.reshape(b, nb, KVH, HD).transpose(0, 2, 1, 3)
        sc = jnp.einsum('bhsd,bhnd->bhsn', q4, ck4) * SCALE
        comp_mask = (jnp.arange(nb) + 1) * CS <= jnp.arange(s)[:, None]
        a_comp = _masked_softmax(sc, comp_mask[None, None])
        out_comp = jnp.einsum('bhsn,bhnd->bhsd', a_comp, cv4).transpose(0, 2, 1, 3).reshape(b, s, DOUT)
        imp = sc.mean(axis=(1, 2))
        _, top_idx = jax.lax.top_k(imp, TOPK)
        pos = (top_idx * CS)[:, :, None] + jnp.arange(SB)[None, None, :]
        pos = pos.reshape(b, TOPK * SB)
        valid = pos < s
        posc = jnp.minimum(pos, s - 1)
        sel_k = jnp.take_along_axis(k, posc[..., None], axis=1) * valid[..., None]
        sel_v = jnp.take_along_axis(v, posc[..., None], axis=1) * valid[..., None]
        M = TOPK * SB
        ks4 = sel_k.reshape(b, M, KVH, HD).transpose(0, 2, 1, 3)
        vs4 = sel_v.reshape(b, M, KVH, HD).transpose(0, 2, 1, 3)
        ss = jnp.einsum('bhsd,bhmd->bhsm', q4, ks4) * SCALE
        causal_sel = jnp.arange(s)[None, :, None] >= pos[:, None, :]
        a_sel = _masked_softmax(ss, (causal_sel & valid[:, None, :])[:, None])
        out_sel = jnp.einsum('bhsm,bhmd->bhsd', a_sel, vs4).transpose(0, 2, 1, 3).reshape(b, s, DOUT)
        sw = jnp.einsum('bhsd,bhtd->bhst', q4, k4) * SCALE
        rows = jnp.arange(s)[:, None]
        cols = jnp.arange(s)[None, :]
        wmask = (cols <= rows) & (cols > rows - WIN)
        a_win = _masked_softmax(sw, wmask[None, None])
        out_win = jnp.einsum('bhst,bhtd->bhsd', a_win, v4).transpose(0, 2, 1, 3).reshape(b, s, DOUT)
        g = jax.nn.softmax(x @ Wg + bg, axis=-1)
        out = g[..., 0:1] * out_comp + g[..., 1:2] * out_sel + g[..., 2:3] * out_win
        return out @ Wo + bo

    def _L2_xattn_ref(xh1, xh2, x2, x2_mask, W, b, D):
        import jax, jax.numpy as jnp
        import numpy as np
        B, L1, L2, FULL, H = (8, 256, 256, 128, 128)
        NEG_INF = -1e+30
        x1_key = jax.nn.relu(jnp.einsum('bsf,fg->bsg', xh1, W.T) + b)
        x2_key = jax.nn.relu(jnp.einsum('btf,fg->btg', xh2, W.T) + b)
        x2_key = x2_key * D[None, :, :]
        scores = jnp.einsum('bsf,btf->bst', x1_key, x2_key)
        scores = jnp.where(x2_mask[:, None, :], NEG_INF, scores)
        alpha = jax.nn.softmax(scores, axis=-1)
        seq_ave = jnp.einsum('bst,bth->bsh', alpha, x2)
        return seq_ave

    def _L2_ffn_ref(x, w_gate, w_noise, Wd, bd, Wu, bu):
        import jax, jax.numpy as jnp
        import numpy as np
        D_MODEL = 128
        N_EXPERTS = 8
        TOP_K = 2
        BOTTLENECK = 64
        B, S = (2, 512)
        ADAPTER_SCALE = 0.5

        def _moe_forward(x, w_gate, w_noise, Wd, bd, Wu, bu):
            b, s, d = x.shape
            xf = x.reshape(-1, d)
            T = xf.shape[0]
            clean_logits = xf @ w_gate
            logits = clean_logits
            k1 = min(TOP_K + 1, N_EXPERTS)
            top_logits, top_idx = jax.lax.top_k(logits, k1)
            top_k_logits = top_logits[:, :TOP_K]
            top_k_idx = top_idx[:, :TOP_K]
            top_k_gates = jax.nn.softmax(top_k_logits, axis=-1)
            rows = jnp.arange(T)[:, None]
            gates = jnp.zeros((T, N_EXPERTS), dtype=top_k_gates.dtype)
            gates = gates.at[rows, top_k_idx].set(top_k_gates)
            h = jax.nn.relu(jnp.einsum('td,edb->teb', xf, Wd) + bd[None, :, :])
            y = jnp.einsum('teb,ebd->ted', h, Wu) + bu[None, :, :]
            y = ADAPTER_SCALE * y
            out = jnp.einsum('te,ted->td', gates, y)
            return out.reshape(b, s, d)
        return _moe_forward(x, w_gate, w_noise, Wd, bd, Wu, bu)

    def _L3_attn_ref(hidden_states, ln_w, ln_b, in_proj_w, in_proj_b, conv_w, conv_b, x_proj_w, dt_proj_w, dt_proj_b, A_log, D, out_proj_w, out_proj_b):
        import jax, jax.numpy as jnp
        import numpy as np
        H = 128
        E = 256
        N = 16
        R = 64
        K = 4
        B = 2
        L = 256
        EPS = 1e-05

        def _layernorm(x, w, b):
            mu = jnp.mean(x, axis=-1, keepdims=True)
            var = jnp.mean(jnp.square(x - mu), axis=-1, keepdims=True)
            return (x - mu) * jax.lax.rsqrt(var + EPS) * w + b

        def _causal_dw_conv(x, conv_w, conv_b):
            xc = jnp.transpose(x, (0, 2, 1))
            kern = conv_w[:, None, :]
            y = jax.lax.conv_general_dilated(xc, kern, window_strides=(1,), padding=[(K - 1, 0)], feature_group_count=E, dimension_numbers=('NCH', 'OIH', 'NCH'))
            y = y + conv_b[None, :, None]
            return jnp.transpose(y, (0, 2, 1))

        def _selective_scan(x, x_proj_w, dt_proj_w, dt_proj_b, A_log, D):
            dbc = jnp.einsum('ble,ep->blp', x, x_proj_w)
            dt_r, Bm, Cm = jnp.split(dbc, [R, R + N], axis=-1)
            dt = jax.nn.softplus(jnp.einsum('blr,re->ble', dt_r, dt_proj_w) + dt_proj_b)
            A = -jnp.exp(A_log)

            def step(h, inp):
                x_t, dt_t, B_t, C_t = inp
                dA = jnp.exp(dt_t[..., None] * A)
                h = dA * h + dt_t[..., None] * B_t[:, None, :] * x_t[..., None]
                y = jnp.einsum('ben,bn->be', h, C_t)
                return (h, y)
            xs = (jnp.transpose(x, (1, 0, 2)), jnp.transpose(dt, (1, 0, 2)), jnp.transpose(Bm, (1, 0, 2)), jnp.transpose(Cm, (1, 0, 2)))
            h0 = jnp.zeros((x.shape[0], E, N), x.dtype)
            _, ys = jax.lax.scan(step, h0, xs)
            y = jnp.transpose(ys, (1, 0, 2))
            return y + x * D
        residual = hidden_states
        hs = _layernorm(hidden_states, ln_w, ln_b)
        proj = hs @ in_proj_w + in_proj_b
        x, gate = jnp.split(proj, [E], axis=-1)
        x = _causal_dw_conv(x, conv_w, conv_b)
        x = jax.nn.silu(x)
        y = _selective_scan(x, x_proj_w, dt_proj_w, dt_proj_b, A_log, D)
        y = jax.nn.sigmoid(gate) * y
        out = y @ out_proj_w + out_proj_b + residual
        return out

    def _L3_xattn_ref(query, key, value, in_proj_weight, in_proj_bias, out_proj_weight, out_proj_bias, lambda_q1, lambda_k1, lambda_q2, lambda_k2):
        import jax, jax.numpy as jnp
        import numpy as np
        import math
        EMBED_DIM = 128
        NUM_HEADS = 16
        HEAD_DIM = EMBED_DIM // NUM_HEADS
        SUB_HEAD_DIM = HEAD_DIM // 2
        SCALING = 1.0 / math.sqrt(SUB_HEAD_DIM)
        LAMBDA_INIT = 0.8 - 0.6 * math.exp(-0.3 * 0)
        B, T, D = query.shape
        S = key.shape[1]
        H, hd, sd = (NUM_HEADS, HEAD_DIM, SUB_HEAD_DIM)
        qw, kw, vw = jnp.split(in_proj_weight, 3, axis=0)
        qb, kb, vb = jnp.split(in_proj_bias, 3, axis=0)
        q = query @ qw.T + qb
        k = key @ kw.T + kb
        v = value @ vw.T + vb
        q = q.reshape(B, T, H, hd).transpose(0, 2, 1, 3)
        k = k.reshape(B, S, H, hd).transpose(0, 2, 1, 3)
        v = v.reshape(B, S, H, hd).transpose(0, 2, 1, 3)
        q1, q2 = (q[..., :sd], q[..., sd:])
        k1, k2 = (k[..., :sd], k[..., sd:])
        logits_1 = jnp.einsum('bhtd,bhsd->bhts', q1, k1) * SCALING
        logits_2 = jnp.einsum('bhtd,bhsd->bhts', q2, k2) * SCALING
        a1 = jax.nn.softmax(logits_1, axis=-1)
        a2 = jax.nn.softmax(logits_2, axis=-1)
        lam = jnp.exp(jnp.dot(lambda_q1, lambda_k1)) - jnp.exp(jnp.dot(lambda_q2, lambda_k2)) + LAMBDA_INIT
        diff_weights = a1 - lam * a2
        attn_output = jnp.einsum('bhts,bhsd->bhtd', diff_weights, v)
        attn_output = attn_output * (1.0 - LAMBDA_INIT)
        attn_output = attn_output.transpose(0, 2, 1, 3).reshape(B, T, D)
        output = attn_output @ out_proj_weight.T + out_proj_bias
        return output

    def _L3_ffn_ref(x, w_gate, w_up, w_down):
        import jax, jax.numpy as jnp
        import numpy as np
        HIDDEN = 128
        INNER = 512

        def _weight_quant(w):
            scale = 1.0 / jnp.clip(jnp.mean(jnp.abs(w)), 1e-05)
            wq = jnp.clip(jnp.round(w * scale), -1.0, 1.0) / scale
            return w + jax.lax.stop_gradient(wq - w)

        def _act_quant(x):
            scale = 127.0 / jnp.clip(jnp.max(jnp.abs(x), axis=-1, keepdims=True), 1e-05)
            xq = jnp.clip(jnp.round(x * scale), -128.0, 127.0) / scale
            return x + jax.lax.stop_gradient(xq - x)

        def _bitlinear(x, w):
            return jnp.einsum('bsi,oi->bso', _act_quant(x), _weight_quant(w))
        gate = jax.nn.silu(_bitlinear(x, w_gate))
        up = _bitlinear(x, w_up)
        return _bitlinear(gate * up, w_down)
    x = x + _L0_attn_ref(_layernorm(x, axis=-1), L0_attn_Wq, L0_attn_bq, L0_attn_Wk, L0_attn_bk, L0_attn_Wv, L0_attn_bv, L0_attn_Wo, L0_attn_bo)
    x = x + _L0_xattn_ref(_layernorm(x, axis=-1), ctx_1024, ctx_1024, L0_xattn_Q_W, L0_xattn_K_W, L0_xattn_V_W)
    x = x + _L0_ffn_ref(_layernorm(x, axis=-1), L0_ffn_wqkv, L0_ffn_q_scale, L0_ffn_k_scale, L0_ffn_wo, L0_ffn_ln_g, L0_ffn_ln_b, L0_ffn_w1, L0_ffn_b1, L0_ffn_w2, L0_ffn_b2)
    x = x + _L1_attn_ref(_layernorm(x, axis=-1), L1_attn_Wq, L1_attn_Wk, L1_attn_Wv, L1_attn_W_O)
    x = x + _L1_xattn_ref(ctx_1024, ctx_1024, _layernorm(x, axis=-1), L1_xattn_Wk, L1_xattn_Wv, L1_xattn_bv, L1_xattn_Wq, L1_xattn_bq, L1_xattn_Wo, L1_xattn_bo)
    x = x + _L1_ffn_ref(_layernorm(x, axis=-1), L1_ffn_gate_W, L1_ffn_gate_b, L1_ffn_W1, L1_ffn_b1, L1_ffn_W2, L1_ffn_b2, L1_ffn_ln_gamma, L1_ffn_ln_beta)
    x = x + _L2_attn_ref(_layernorm(x, axis=-1), L2_attn_Wq, L2_attn_Wk, L2_attn_Wv, L2_attn_Wo, L2_attn_bo, L2_attn_wk_comp, L2_attn_wv_comp, L2_attn_pe, L2_attn_Wg, L2_attn_bg)
    x = x + _L2_xattn_ref(_layernorm(x, axis=-1), ctx_1024, ctx_1024, mask_BxS2_bf0, L2_xattn_W, L2_xattn_b, L2_xattn_D)
    x = x + _L2_ffn_ref(_layernorm(x, axis=-1), L2_ffn_w_gate, L2_ffn_w_noise, L2_ffn_Wd, L2_ffn_bd, L2_ffn_Wu, L2_ffn_bu)
    x = x + _L3_attn_ref(_layernorm(x, axis=-1), L3_attn_ln_w, L3_attn_ln_b, L3_attn_in_proj_w, L3_attn_in_proj_b, L3_attn_conv_w, L3_attn_conv_b, L3_attn_x_proj_w, L3_attn_dt_proj_w, L3_attn_dt_proj_b, L3_attn_A_log, L3_attn_D, L3_attn_out_proj_w, L3_attn_out_proj_b)
    x = x + _L3_xattn_ref(_layernorm(x, axis=-1), ctx_1024, ctx_1024, L3_xattn_in_proj_weight, L3_xattn_in_proj_bias, L3_xattn_out_proj_weight, L3_xattn_out_proj_bias, L3_xattn_lambda_q1, L3_xattn_lambda_k1, L3_xattn_lambda_q2, L3_xattn_lambda_k2)
    x = x + _L3_ffn_ref(_layernorm(x, axis=-1), L3_ffn_w_gate, L3_ffn_w_up, L3_ffn_w_down)
    return x

_drawn_inputs = setup_inputs


def setup_inputs(seed=0):
    import zlib

    import numpy as np

    out = dict(_drawn_inputs(seed))
    spreads = {'L0_attn_bq': (0.0, 0.268),
     'L0_attn_bk': (0.0, 0.8),
     'L0_attn_bv': (0.0, 0.33),
     'L0_attn_bo': (0.0, 0.1),
     'L0_ffn_q_scale': (1.0, 0.6),
     'L0_ffn_k_scale': (1.0, 0.6),
     'L0_ffn_ln_g': (1.0, 0.6),
     'L0_ffn_ln_b': (0.0, 0.8),
     'L0_ffn_b1': (0.0, 0.8),
     'L0_ffn_b2': (0.0, 0.1),
     'L1_xattn_bv': (0.0, 0.1),
     'L1_xattn_bq': (0.0, 0.544),
     'L1_xattn_bo': (0.0, 0.1),
     'L1_ffn_gate_b': (0.0, 0.8),
     'L1_ffn_b1': (0.0, 0.8),
     'L1_ffn_b2': (0.0, 0.8),
     'L1_ffn_ln_gamma': (1.0, 0.2),
     'L1_ffn_ln_beta': (0.0, 0.1),
     'L2_attn_bo': (0.0, 0.292),
     'L2_attn_bg': (0.0, 0.333),
     'L2_xattn_b': (0.0, 0.1),
     'L2_xattn_D': (1.0, 0.2),
     'L2_ffn_bd': (0.0, 0.8),
     'L2_ffn_bu': (0.0, 0.8),
     'L3_attn_ln_w': (1.0, 0.6),
     'L3_attn_ln_b': (0.0, 0.8),
     'L3_attn_in_proj_b': (0.0, 0.8),
     'L3_attn_conv_b': (0.0, 0.8),
     'L3_attn_D': (1.0, 0.6),
     'L3_attn_out_proj_b': (0.0, 0.423),
     'L3_xattn_in_proj_bias': (0.0, 0.613),
     'L3_xattn_out_proj_bias': (0.0, 0.391)}
    factors = {'L0_ffn_w1': 5.843,
     'L0_ffn_w2': 5.579,
     'L1_ffn_gate_W': 6.962,
     'L1_ffn_W1': 8.0,
     'L1_ffn_W2': 8.0,
     'L2_ffn_w_gate': 7.239,
     'L2_ffn_Wd': 8.0,
     'L2_ffn_Wu': 8.0,
     'L3_attn_in_proj_w': 8.0,
     'L3_attn_conv_w': 8.0,
     'L3_attn_x_proj_w': 8.0,
     'L3_attn_dt_proj_w': 8.0,
     'L3_attn_dt_proj_b': 8.0,
     'L3_attn_A_log': 8.0,
     'L3_attn_out_proj_w': 8.0,
     'L3_xattn_lambda_q1': 8.0,
     'L3_xattn_lambda_k1': 8.0,
     'L3_xattn_lambda_q2': 8.0,
     'L3_xattn_lambda_k2': 8.0}
    for name, (base, spread) in spreads.items():
        noise = np.random.default_rng([zlib.crc32(name.encode()), seed]).standard_normal(out[name].shape)
        drawn = base * np.exp(spread * noise) if base else spread * noise
        out[name] = jnp.asarray(drawn.astype(out[name].dtype))
    for name, factor in factors.items():
        out[name] = (out[name] * factor).astype(out[name].dtype)
    return out
```

```python
from contextlib import ExitStack

import numpy as np

import concourse.bass as bass
from concourse import mybir

F32 = mybir.dt.float32
BF16 = mybir.dt.bfloat16
U32 = mybir.dt.uint32
ALU = mybir.AluOpType
ACT = mybir.ActivationFunctionType
AX = mybir.AxisListType

P = 128
B = 4
T = 512
D = 128
NT = T // P
S2 = 77
NEG = -1.0e30
LN_EPS = 1e-5

A0_H, A0_HD, A0_U = 16, 8, 31
F0_H, F0_HD, F0_WIN, F0_L = 8, 64, 64, 2
F0_IN = F0_H * F0_HD
F0_HID = 341
F0_CH = [(0, 128), (128, 128), (256, 85)]
A1_H, A1_HD = 16, 8
M1_E, M1_H = 8, 256
A2_H, A2_HD, A2_CB, A2_SB, A2_TOP, A2_WIN = 16, 8, 16, 8, 2, 32
A2_NB = T // A2_CB
A2_M = A2_SB * A2_TOP
M2_E, M2_H = 8, 64
A3_E, A3_N, A3_R, A3_K = 256, 16, 64, 4
A3_C = A3_E // P
X3_H, X3_SD = 16, 4
F3_IN = 512



def rotary_tables():
    half = np.arange(0, F0_HD, 2, dtype=np.float32)
    inv = (np.float32(1.0) / np.float32(10000.0) ** (half / np.float32(F0_HD))).astype(np.float32)
    t = np.arange(T, dtype=np.float32)
    f = t[:, None] * inv[None, :]
    f = np.concatenate([f, f], -1)
    base = (half + np.float32(0.4 * F0_HD)) / np.float32(1.4 * F0_HD)
    power = (t - T // 2) / np.float32(F0_WIN // 2)
    s = (base[None, :] ** power[:, None]).astype(np.float32)
    s = np.concatenate([s, s], -1)
    sign = np.where(np.arange(F0_HD) < F0_HD // 2, -1.0, 1.0).astype(np.float32)
    c, n = np.cos(f), np.sin(f) * sign
    return [c * s, n * s, c / s, n / s]


def rope_tables():
    i = np.arange(A2_HD // 2, dtype=np.float32)
    inv = (np.float32(1.0) / np.float32(10000.0) ** (i * np.float32(2.0) / np.float32(A2_HD))).astype(np.float32)
    a = np.arange(T, dtype=np.float32)[:, None] * inv[None, :]
    f = np.arange(D)
    pair = (f % A2_HD) // 2
    c, s = np.cos(a)[:, pair].T, np.sin(a)[:, pair].T
    return c, s * np.where(f % 2 == 0, -1.0, 1.0)[:, None]


def tokens(a):
    return a.reshape(NT, P, -1).transpose(1, 0, 2).reshape(P, -1)


def constants():
    p, f = np.arange(P), np.arange(D)
    c = {}
    c["ident"] = np.eye(P)
    c["iota"] = np.broadcast_to(np.arange(T), (P, T))
    c["tokid"] = p[:, None] + P * np.arange(NT)[None, :]
    c["neghalf"] = np.full((P, 32), -0.5)
    c["ones"] = np.ones((P, P))
    c["headsum"] = (f[:, None] // 8 == np.arange(16)[None, :])
    c["headmask"] = np.repeat(f[:, None] // 8 == np.arange(16)[None, :], 32, 1)
    c["rowmask"] = (4 * np.arange(4)[None, :, None] + p[:, None, None] // 32 == f[None, None, :] // 8).reshape(P, -1)
    h16 = np.zeros((P, 512))
    h16[:16] = np.repeat(np.eye(16), 32, 1)
    c["diag16"] = h16
    m = np.zeros((P, T))
    m[:, 384:] = np.where(p[None, :] <= p[:, None], 0.0, NEG)
    c["causal"] = m
    c["causalT"] = (p[:, None] <= f[None, :])
    c["halves"] = (p[:, None] // 64 == np.arange(2)[None, :])
    c["pick"] = (p[:, None] % 4 == np.arange(4)[None, :]) & (p[:, None] < 8)
    shift = np.zeros((P, P)); shift[p[:-1], p[1:]] = 1.0
    carry = np.zeros((P, P)); carry[P - 1, 0] = 1.0
    c["shift"], c["carry"] = shift, carry
    j = np.arange(192)
    ok = (j[None, :] - 64 <= p[:, None]) & (j[None, :] >= p[:, None])
    band = np.where(ok, 0.0, NEG)
    c["band"] = band
    c["iota8"] = np.broadcast_to(np.tile(np.arange(8), NT), (P, 8 * NT))
    c["pairpick"] = np.kron(np.eye(8), np.ones((1, 64)))
    c["fourfold"] = np.tile(np.eye(32), (1, 4))
    c["rot_q"], c["rot_qs"], c["rot_k"], c["rot_ks"] = [tokens(a) for a in rotary_tables()]
    c["rope_c"], c["rope_s"] = rope_tables()
    q = p % 32
    n = np.arange(A2_NB)
    comp = [np.where((n[None, :] + 1) * A2_CB <= 32 * k + q[:, None], 0.0, NEG) for k in range(T // 32)]
    c["comp_mask"] = np.concatenate(comp, 1)
    kk = np.arange(64) - 32
    win = (kk[None, :] <= q[:, None]) & (kk[None, :] > q[:, None] - A2_WIN)
    c["win_mask"] = np.concatenate([np.where(win & (kk[None, :] >= 0), 0.0, NEG), np.where(win, 0.0, NEG)], 1)
    tok = p[:, None] + P * np.arange(NT)[None, :]
    c["block_of"] = (tok[:, :, None] // A2_CB == n[None, None, :]).reshape(P, -1)
    c["query_id"] = q[:, None] + 32 * np.arange(T // 32)[None, :]
    m = np.arange(32)
    c["submap"] = (f[:, None] // 4 == (2 * (m % 16) + m // 16)[None, :])
    return {k: np.ascontiguousarray(v, np.float32) for k, v in c.items()}


def blockdiag(w):
    out = np.zeros((D, D), w.dtype)
    for h in range(w.shape[0]):
        out[8 * h:8 * h + 8, 8 * h:8 * h + 8] = w[h]
    return out


def rows(v):
    return np.broadcast_to(np.asarray(v).reshape(1, -1), (P, np.asarray(v).size))


def column(v):
    v = np.asarray(v)
    n = -(-v.size // P)
    out = np.zeros((n * P,), v.dtype)
    out[:v.size] = v
    return out.reshape(n, P).T


def chunks(w):
    n = -(-w.shape[0] // P)
    out = np.zeros((n * P, w.shape[1]), w.dtype)
    out[:w.shape[0]] = w
    return out.reshape(n, P, -1).transpose(1, 0, 2).reshape(P, -1)


def segments(a):
    c = constants()
    seg = {}
    seg["tables"] = [(k, c[k]) for k in ("rot_q", "rot_qs", "rot_k", "rot_ks", "comp_mask", "win_mask", "block_of")] + [
        ("f3_wg", a["L3_ffn_w_gate"].T), ("f3_wu", a["L3_ffn_w_up"].T), ("f3_wd", chunks(a["L3_ffn_w_down"].T)),
        ("a2_wkt", np.tile(a["L2_attn_wk_comp"], P // A2_CB)[:, None]),
        ("a2_wvt", np.tile(a["L2_attn_wv_comp"], P // A2_CB)[:, None]),
        ("a3_alog", chunks(a["L3_attn_A_log"])),
        ("x3_l", rows(np.concatenate([a["L3_xattn_lambda_q1"], a["L3_xattn_lambda_q2"],
                                      a["L3_xattn_lambda_k1"], a["L3_xattn_lambda_k2"]])))]
    for l in range(F0_L):
        seg["tables"] += [(f"f0_qs{l}", rows(a["L0_ffn_q_scale"][l])), (f"f0_ks{l}", rows(a["L0_ffn_k_scale"][l]))]
    seg["base"] = [(k, c[k]) for k in ("ident", "iota", "tokid", "neghalf", "ones", "headsum", "pick")]
    seg["l0_attn"] = [(k, c[k]) for k in ("headmask", "rowmask", "diag16")] + [
        ("a0_wq", a["L0_attn_Wq"]), ("a0_wk", a["L0_attn_Wk"]), ("a0_wv", a["L0_attn_Wv"]), ("a0_wo", a["L0_attn_Wo"]),
        ("a0_bq", column(a["L0_attn_bq"])), ("a0_bk", column(a["L0_attn_bk"])),
        ("a0_bv", rows(a["L0_attn_bv"])), ("a0_bo", rows(a["L0_attn_bo"]))]
    seg["l0_xattn"] = [("x0_wq", a["L0_xattn_Q_W"].T), ("x0_wk", a["L0_xattn_K_W"].T), ("x0_wv", a["L0_xattn_V_W"].T)]
    f0 = [(k, c[k]) for k in ("shift", "carry", "band", "halves")]
    for l in range(F0_L):
        f0 += [(f"f0_wqkv{l}", a["L0_ffn_wqkv"][l]),
               (f"f0_wo{l}", chunks(a["L0_ffn_wo"][l])),
               (f"f0_g{l}", column(a["L0_ffn_ln_g"][l])), (f"f0_b{l}", column(a["L0_ffn_ln_b"][l])),
               (f"f0_w1{l}", a["L0_ffn_w1"][l]),
               (f"f0_b1a{l}", column(a["L0_ffn_b1"][l][:F0_HID])), (f"f0_b1g{l}", column(a["L0_ffn_b1"][l][F0_HID:])),
               (f"f0_w2{l}", chunks(a["L0_ffn_w2"][l])), (f"f0_b2{l}", rows(a["L0_ffn_b2"][l]))]
    seg["l0_ffn"] = f0
    seg["l1_attn"] = [(k, c[k]) for k in ("causal", "causalT")] + [
                      ("a1_wq", blockdiag(a["L1_attn_Wq"])), ("a1_wk", blockdiag(a["L1_attn_Wk"])),
                      ("a1_wv", blockdiag(a["L1_attn_Wv"])), ("a1_wo", a["L1_attn_W_O"])]
    seg["l1_xattn"] = [("x1_wq", a["L1_xattn_Wq"].T), ("x1_wk", a["L1_xattn_Wk"].T), ("x1_wv", a["L1_xattn_Wv"].T),
                       ("x1_wo", a["L1_xattn_Wo"].T), ("x1_bq", column(a["L1_xattn_bq"])),
                       ("x1_bv", rows(a["L1_xattn_bv"])), ("x1_bo", rows(a["L1_xattn_bo"]))]
    seg["l1_ffn"] = [("iota8", c["iota8"]), ("m1_wg", a["L1_ffn_gate_W"]), ("m1_bg", rows(a["L1_ffn_gate_b"])),
                     ("m1_w1", a["L1_ffn_W1"].transpose(1, 0, 2).reshape(D, -1)),
                     ("m1_b1", column(a["L1_ffn_b1"].reshape(-1))),
                     ("m1_w2", chunks(a["L1_ffn_W2"].reshape(-1, D))),
                     ("m1_b2", a["L1_ffn_b2"]),
                     ("m1_g", rows(a["L1_ffn_ln_gamma"])), ("m1_b", rows(a["L1_ffn_ln_beta"]))]
    seg["l2_attn"] = [(k, c[k]) for k in ("rope_c", "rope_s", "query_id", "fourfold")] + [
        ("a2_wq", a["L2_attn_Wq"]), ("a2_wqs", a["L2_attn_Wq"][:, np.arange(D) ^ 1]),
        ("a2_wk", a["L2_attn_Wk"]), ("a2_wks", a["L2_attn_Wk"][:, np.arange(D) ^ 1]),
        ("a2_wv", a["L2_attn_Wv"]), ("a2_wo", a["L2_attn_Wo"]), ("a2_bo", rows(a["L2_attn_bo"])),
        ("a2_wkc", np.broadcast_to(a["L2_attn_wk_comp"][:, None], (A2_CB, A2_NB))),
        ("a2_wvc", np.broadcast_to(a["L2_attn_wv_comp"][:, None], (A2_CB, A2_NB))),
        ("a2_pe", a["L2_attn_pe"]), ("a2_wg", a["L2_attn_Wg"]), ("a2_bg", rows(a["L2_attn_bg"]))]
    seg["l2_xattn"] = [("x2_w", a["L2_xattn_W"].T), ("x2_b", column(a["L2_xattn_b"])), ("x2_d", column(a["L2_xattn_D"]))]
    seg["l2_ffn"] = [("pairpick", c["pairpick"]), ("m2_wg", a["L2_ffn_w_gate"]),
                     ("m2_wd", a["L2_ffn_Wd"].transpose(1, 0, 2).reshape(D, -1)),
                     ("m2_bd", column(a["L2_ffn_bd"].reshape(-1))),
                     ("m2_wu", chunks(a["L2_ffn_Wu"].reshape(-1, D))), ("m2_bu", a["L2_ffn_bu"])]
    seg["l3_attn"] = [("a3_g", column(a["L3_attn_ln_w"])), ("a3_b", column(a["L3_attn_ln_b"])),
                      ("a3_win", a["L3_attn_in_proj_w"]), ("a3_bin", column(a["L3_attn_in_proj_b"])),
                      ("a3_cw", chunks(a["L3_attn_conv_w"])), ("a3_cb", column(a["L3_attn_conv_b"])),
                      ("a3_wx", chunks(a["L3_attn_x_proj_w"])), ("a3_wdt", a["L3_attn_dt_proj_w"]),
                      ("a3_bdt", column(a["L3_attn_dt_proj_b"])),
                      ("a3_d", column(a["L3_attn_D"])), ("a3_wout", chunks(a["L3_attn_out_proj_w"])),
                      ("a3_bout", rows(a["L3_attn_out_proj_b"]))]
    w, b = a["L3_xattn_in_proj_weight"], a["L3_xattn_in_proj_bias"]
    seg["l3_xattn"] = [("submap", c["submap"]), ("x3_wq", w[:D].T), ("x3_wk", w[D:2 * D].T), ("x3_wv", w[2 * D:].T),
                       ("x3_bq", column(b[:D])), ("x3_bk", column(b[D:2 * D])), ("x3_bv", rows(b[2 * D:])),
                       ("x3_wo", a["L3_xattn_out_proj_weight"].T), ("x3_bo", rows(a["L3_xattn_out_proj_bias"]))]
    return seg


def pack(a):
    seg, where, pieces, parts, at = segments(a), {}, {}, [], 0
    for name, items in seg.items():
        start = at
        for key, v in items:
            v = np.asarray(v)
            where[key] = (at, v.shape[1], v.shape[0])
            full = np.zeros((P, v.shape[1]), np.float32)
            full[:v.shape[0]] = v
            parts.append(full)
            at += v.shape[1]
        pieces[name] = (start, at)
    return np.ascontiguousarray(np.concatenate(parts, 1)), where, pieces




class Sems:

    def __init__(self, nc, stage):
        self.nc, self.stage, self.made, self.stack = nc, stage, {}, ExitStack()

    def __getitem__(self, name):
        if name not in self.made:
            self.made[name] = self.stack.enter_context(self.nc.semaphore(f"{self.stage}_{name}"))
        return self.made[name]

    def clear(self):
        for s in self.made.values():
            self.nc.gpsimd.sem_clear(s)


class Steps:

    def __init__(self, eng, sem):
        self.eng, self.sem, self.n = eng, sem, 0

    def step(self, ins):
        ins.then_inc(self.sem, 1)
        self.n += 1

    def wait(self):
        self.eng.wait_ge(self.sem, self.n)

    def link(self, ins):
        self.step(ins)
        self.wait()


class Net:

    def __init__(self, nc, ctx, where):
        self.nc, self.where, self.ctx = nc, where, ctx
        self.split = where["ident"][0]
        self.W = self.sb("weights", [P, max(at + n for at, n, _ in where.values()) - self.split])
        self.tables = None
        self.x = self.sb("x", [P, NT, D])
        self.xn = self.sb("xn", [P, NT, D])
        self.xnT = self.sb("xnT", [D, T])
        self.ctxT = self.sb("ctxT", [D, S2])
        self.ctxtok = self.sb("ctxtok", [S2, D])
        self.bias = self.sb("maskrow", [P, S2])
        self.bn = self.sb("bn", [P, NT, 6])
        self.mv = self.sb("mv", [P, NT, 2])
        self.vare = self.sb("vare", [P, NT])
        self.rstd = self.sb("rstd", [P, NT])
        self.ps = [ctx.enter_context(nc.psum_tensor(f"bank{i}", [P, 512], F32)) for i in range(8)]

    def sb(self, name, shape, dt=F32):
        return self.ctx.enter_context(self.nc.sbuf_tensor(name, shape, dt))

    def w(self, key, lo=0, hi=None):
        at, n, r = self.where[key]
        held = self.W
        if at < self.split:
            held = self.tables
        else:
            at -= self.split
        return held[0:r, at + lo:at + (n if hi is None else hi)]


def tile(t, n=P):
    return slice(t * n, (t + 1) * n)




def norm_vector(net, s, v, steps, src=None, dst=None, tag=""):
    src, dst = src or net.x, dst or net.xn
    for t in range(NT):
        steps.step(v.bn_stats(net.bn[:, t, :], src[:, t, :]))
    steps.wait()
    for t in range(NT):
        last = v.bn_aggr(net.mv[:, t, :], net.bn[:, t, :])
    last.then_inc(s[tag + "variance_ready"], 1)
    v.wait_ge(s[tag + "variance_ready"], 1)
    v.wait_ge(s[tag + "rstd_ready"], 1)
    for t in range(NT):
        last = v.tensor_scalar(dst[:, t, :], src[:, t, :], net.mv[:, t, 0:1], net.rstd[:, t:t + 1],
                               ALU.subtract, ALU.mult)
    last.then_inc(s[tag + "norm_ready"], 1)


def norm_pool(net, s, g, steps, tag=""):
    g.wait_ge(s[tag + "variance_ready"], 1)
    steps.link(g.tensor_scalar(net.vare[:, :], net.mv[:, :, 1], LN_EPS, 0.0, ALU.add, ALU.add))
    g.tensor_tensor(net.rstd[:, :], net.vare[:, :], net.w("neghalf", 0, NT), ALU.pow).then_inc(s[tag + "rstd_ready"], 1)


def transpose_tensor(net, s, pe, src, bank, signal):
    for t in range(NT):
        last = pe.transpose(bank[:, tile(t)], src[:, t, :], net.w("ident"))
    last.then_inc(s[signal], 1)


def norm_tensor(net, s, pe, bank, src=None, tag=""):
    pe.wait_ge(s[tag + "norm_ready"], 1)
    transpose_tensor(net, s, pe, src or net.xn, bank, tag + "normT_in_psum")


def norm_scalar(net, s, act, bank, tag=""):
    act.wait_ge(s[tag + "normT_in_psum"], 1)
    act.activation(net.xnT[:, :], bank[:, :], ACT.Copy).then_inc(s[tag + "normT_ready"], 1)


def bc(ap, n):
    return ap.unsqueeze(1).to_broadcast([ap.shape[0], n, ap.shape[1]])


def bci(ap, n):
    return ap.unsqueeze(2).to_broadcast([ap.shape[0], ap.shape[1], n])


def run_stage(nc, name, body, need, before=None, final=False):
    if before:
        before.clear()
    s = Sems(nc, name)
    with ExitStack() as ctx:
        def sb(n, shape, dt=F32):
            return ctx.enter_context(nc.sbuf_tensor(f"{name}_{n}", shape, dt))
        with nc.Block(no_gpsimd_drain=True) as block:
            body(s, sb, block, need)
    if before:
        before.stack.close()
    if final:
        s.clear()
        nc.all_engine_barrier()
        s.stack.close()
    return s




def l0_attn(net):
    nc, w, ps = net.nc, net.w, net.ps
    G = 4

    def body(s, sb, block, need):
        qabs = sb("qabs", [D, T])
        kT = sb("kT", [D, T])
        v = sb("v", [P, NT, D])
        qn = sb("qn", [A0_H, T])
        top = sb("top", [A0_H, 32])
        topi = sb("topi", [A0_H, 32], U32)
        topf = sb("topf", [A0_H, 32])
        idxd = sb("idxd", [A0_H, T])
        idxcol = sb("idxcol", [P, G])
        lastkey = sb("lastkey", [P, G])
        onehot = sb("onehot", [P, NT, T])
        onehotT = sb("onehotT", [P, G, T])
        forbid = sb("forbid", [P, G, T])
        xsel = sb("xsel", [D, T])
        qsel = sb("qsel", [D, T])
        a = sb("a", [P, G, T])
        sc = sb("sc", [P, G, T])
        mx = sb("mx", [P, G])
        nmx = sb("nmx", [P, G])
        den = sb("den", [P, G])
        rden = sb("rden", [P, G])
        aT = sb("aT", [P, G, T])
        osel = sb("osel", [P, G, D])
        oT = sb("oT", [D, T])
        scale = A0_HD ** -0.5

        @block.tensor
        def _(pe):
            need(pe)
            norm_tensor(net, s, pe, ps[0])
            pe.wait_ge(s["normT_ready"], 1)
            pe.matmul(ps[1][:, :], w("a0_wq"), net.xnT[:, :], start=True, stop=True).then_inc(s["q_in_psum"], 1)
            pe.matmul(ps[2][:, :], w("a0_wk"), net.xnT[:, :], start=True, stop=True).then_inc(s["k_in_psum"], 1)
            for t in range(NT):
                last = pe.matmul(ps[3][:, tile(t)], net.xnT[:, tile(t)], w("a0_wv"), start=True, stop=True)
            last.then_inc(s["v_in_psum"], 1)
            pe.wait_ge(s["qabs_ready"], 1)
            pe.matmul(ps[4][0:A0_H, :], w("headsum"), qabs[:, :], start=True, stop=True).then_inc(s["qnorm_in_psum"], 1)
            pe.wait_ge(s["idx_ready"], 1)
            pe.matmul(ps[5][:, :], w("ones")[0:A0_H, :], idxd[:, :], start=True, stop=True).then_inc(s["idxrow_in_psum"], 1)
            for g in range(G):
                last = pe.matmul(ps[6][:, g:g + 1], idxd[:, tile(g)], w("ones")[0:A0_H, 0:1], start=True, stop=True)
            last.then_inc(s["idxcol_in_psum"], 1)
            for t in range(NT):
                pe.wait_ge(s["onehot_ready"], t + 1)
                last = pe.matmul(ps[7][:, :], net.xn[:, t, :], onehot[:, t, :], start=(t == 0), stop=(t == NT - 1))
            last.then_inc(s["xsel_in_psum"], 1)
            pe.wait_ge(s["xsel_ready"], 1)
            pe.matmul(ps[1][:, :], w("a0_wq"), xsel[:, :], start=True, stop=True).then_inc(s["qsel_in_psum"], 1)
            pe.wait_ge(s["qsel_ready"], 1)
            pe.wait_ge(s["k_ready"], 1)
            for g in range(G):
                if g >= 2:
                    pe.wait_ge(s["masked_ready"], g - 1)
                if g == 1:
                    pe.wait_ge(s["onehot_ready"], NT)
                pe.matmul(ps[4 + g % 2][:, :], qsel[:, tile(g)], kT[:, :], start=True, stop=True)\
                  .then_inc(s["scores_in_psum"], 1)
            for g in range(G):
                pe.wait_ge(s["probs_ready"], g + 1)
                if g >= 2:
                    pe.wait_ge(s["aT_ready"], g - 1)
                elif g == 1:
                    pe.wait_ge(s["v_ready"], 1)
                for t in range(NT):
                    last = pe.transpose(ps[2 + g % 2][:, tile(t)], a[:, g, tile(t)], w("ident"))
                last.then_inc(s["aT_in_psum"], 1)
            pe.wait_ge(s["v_ready"], 1)
            for g in range(G):
                pe.wait_ge(s["aT_ready"], g + 1)
                for t in range(NT):
                    last = pe.matmul(ps[7][:, tile(g)], aT[:, g, tile(t)], v[:, t, :], start=(t == 0), stop=(t == NT - 1))
                last.then_inc(s["osel_in_psum"], 1)
            for g in range(G):
                pe.wait_ge(s["osel_ready"], g + 1)
                last = pe.matmul(ps[0][:, :], osel[:, g, :], onehotT[:, g, :], start=(g == 0), stop=(g == G - 1))
            last.then_inc(s["out_in_psum"], 1)
            pe.wait_ge(s["oT_ready"], 1)
            for t in range(NT):
                last = pe.matmul(ps[1][:, tile(t)], oT[:, tile(t)], w("a0_wo"), start=True, stop=True)
            last.then_inc(s["y_in_psum"], 1)

        @block.scalar
        def _(act):
            need(act)
            norm_scalar(net, s, act, ps[0])
            act.wait_ge(s["q_in_psum"], 1)
            act.activation(qabs[:, :], ps[1][:, :], ACT.Abs, bias=w("a0_bq")).then_inc(s["qabs_ready"], 1)
            act.wait_ge(s["k_in_psum"], 1)
            act.activation(kT[:, :], ps[2][:, :], ACT.Identity, bias=w("a0_bk")).then_inc(s["k_ready"], 1)
            act.wait_ge(s["xsel_in_psum"], 1)
            act.activation(xsel[:, :], ps[7][:, :], ACT.Copy).then_inc(s["xsel_ready"], 1)
            for g in range(G):
                act.wait_ge(s["max_ready"], g + 1)
                act.activation(a[:, g, :], sc[:, g, :], ACT.Exp, bias=nmx[:, g:g + 1], scale=scale,
                               accum_out=den[:, g:g + 1]).then_inc(s["probs_ready"], 1)
            for g in range(G):
                act.wait_ge(s["aT_in_psum"], g + 1)
                act.activation(aT[:, g, :], ps[2 + g % 2][:, :], ACT.Copy).then_inc(s["aT_ready"], 1)
            act.wait_ge(s["out_in_psum"], 1)
            act.activation(oT[:, :], ps[0][:, :], ACT.Copy).then_inc(s["oT_ready"], 1)

        @block.gpsimd
        def _(g_):
            need(g_)
            norm_pool(net, s, g_, Steps(g_, s["pool_step"]))

        @block.vector
        def _(v_):
            need(v_)
            st = Steps(v_, s["vector_step"])
            norm_vector(net, s, v_, st)
            v_.wait_ge(s["v_in_psum"], 1)
            v_.tensor_tensor(v[:, :, :], ps[3][:, :].rearrange("p (t d) -> p t d", t=NT), bc(w("a0_bv"), NT), ALU.add)\
              .then_inc(s["v_ready"], 1)
            v_.wait_ge(s["qnorm_in_psum"], 1)
            st.link(v_.tensor_copy(qn[:, :], ps[4][0:A0_H, :]))
            for r in range(4):
                e = slice(8 * r, 8 * r + 8)
                st.link(v_.max(top[:, e], qn[:, :]))
                st.link(v_.max_index(topi[:, e], top[:, e], qn[:, :]))
                if r < 3:
                    st.link(v_.match_replace(qn[:, :], top[:, e], qn[:, :], -1.0))
            st.link(v_.tensor_copy(topf[:, :], topi[:, :]))
            st.link(v_.memset(topf[:, A0_U:32], -1.0))
            v_.tensor_tensor(idxd[:, :].rearrange("h (a u) -> h a u", u=32), w("diag16")[0:A0_H, :].rearrange("h (a u) -> h a u", u=32),
                             bc(topf[:, :], A0_H), ALU.mult).then_inc(s["idx_ready"], 1)
            v_.wait_ge(s["idxrow_in_psum"], 1)
            for t in range(NT):
                v_.tensor_scalar(onehot[:, t, :], ps[5][:, :], w("tokid")[:, t:t + 1], None, ALU.is_equal)\
                  .then_inc(s["onehot_ready"], 1)
            v_.wait_ge(s["idxcol_in_psum"], 1)
            st.step(v_.tensor_copy(idxcol[:, :], ps[6][:, 0:G]))
            st.link(v_.tensor_scalar(lastkey[:, :], ps[6][:, 0:G], 0.0, None, ALU.max))
            for g in range(G):
                st.step(v_.tensor_scalar(onehotT[:, g, :], w("iota"), idxcol[:, g:g + 1], None, ALU.is_equal))
                st.step(v_.tensor_scalar(forbid[:, g, :], w("iota"), lastkey[:, g:g + 1], NEG, ALU.is_gt, ALU.mult))
            st.wait()
            v_.wait_ge(s["qsel_in_psum"], 1)
            v_.scalar_tensor_tensor(out=qsel[:, :], in0=ps[1][:, :], scalar=w("a0_bq"), in1=w("headmask"),
                                    op0=ALU.add, op1=ALU.mult).then_inc(s["qsel_ready"], 1)
            for g in range(G):
                v_.wait_ge(s["scores_in_psum"], g + 1)
                v_.tensor_tensor_reduce(sc[:, g, :], ps[4 + g % 2][:, :], forbid[:, g, :], 1.0, -3.0e38,
                                        ALU.add, ALU.max, mx[:, g:g + 1]).then_inc(s["masked_ready"], 1)
                v_.wait_ge(s["masked_ready"], g + 1)
                v_.tensor_scalar(nmx[:, g:g + 1], mx[:, g:g + 1], -scale, None, ALU.mult).then_inc(s["max_ready"], 1)
            v_.wait_ge(s["probs_ready"], G)
            st.link(v_.reciprocal(rden[:, :], den[:, :]))
            v_.wait_ge(s["osel_in_psum"], G)
            for g in range(G):
                v_.scalar_tensor_tensor(out=osel[:, g, :], in0=ps[7][:, tile(g)], scalar=rden[:, g:g + 1],
                                        in1=w("rowmask", g * D, (g + 1) * D), op0=ALU.mult, op1=ALU.mult)\
                  .then_inc(s["osel_ready"], 1)
            st.link(v_.tensor_tensor(net.x[:, :, :], net.x[:, :, :], bc(w("a0_bo"), NT), ALU.add))
            v_.wait_ge(s["y_in_psum"], 1)
            st.link(v_.tensor_tensor(net.x[:, :, :], net.x[:, :, :], ps[1][:, :].rearrange("p (t d) -> p t d", t=NT), ALU.add))

    return body




def xattn(net, wq, wk, wv=None, bq=None, bv=None, wo=None, bo=None, scale=1.0, relu=False, kd=None, masked=False):
    nc, w, ps = net.nc, net.w, net.ps

    def body(s, sb, block, need):
        qT = sb("qT", [D, T])
        kT = sb("kT", [D, S2])
        vt = sb("vt", [S2, D])
        sc = sb("sc", [P, NT, S2])
        a = sb("a", [P, NT, S2])
        mx = sb("mx", [P, NT])
        nmx = sb("nmx", [P, NT])
        den = sb("den", [P, NT])
        rden = sb("rden", [P, NT])
        aT = sb("aT", [S2, T])
        oT = sb("oT", [D, T])
        keep = sb("keep", [P, S2])
        value = vt if wv else net.ctxtok
        scores = ps[4][:, 0:NT * S2].rearrange("p (t k) -> p t k", t=NT)

        @block.tensor
        def _(pe):
            need(pe)
            pe.matmul(ps[1][:, 0:S2], w(wk), net.ctxT[:, :], start=True, stop=True).then_inc(s["k_in_psum"], 1)
            if wv:
                pe.matmul(ps[2][0:S2, 0:D], net.ctxT[:, :], w(wv), start=True, stop=True).then_inc(s["v_in_psum"], 1)
            norm_tensor(net, s, pe, ps[0])
            pe.wait_ge(s["normT_ready"], 1)
            pe.matmul(ps[3][:, :], w(wq), net.xnT[:, :], start=True, stop=True).then_inc(s["q_in_psum"], 1)
            pe.wait_ge(s["q_ready"], 1)
            pe.wait_ge(s["k_ready"], 1)
            for t in range(NT):
                last = pe.matmul(scores[:, t, :], qT[:, tile(t)], kT[:, :], start=True, stop=True)
            last.then_inc(s["scores_in_psum"], 1)
            for t in range(NT):
                pe.wait_ge(s["probs_ready"], t + 1)
                last = pe.transpose(ps[5][0:S2, tile(t)], a[:, t, :], w("ident"))
            last.then_inc(s["aT_in_psum"], 1)
            pe.wait_ge(s["aT_ready"], 1)
            if wv:
                pe.wait_ge(s["v_ready"], 1)
            if wo:
                pe.matmul(ps[6][:, :], value[:, :], aT[:, :], start=True, stop=True).then_inc(s["o_in_psum"], 1)
                pe.wait_ge(s["oT_ready"], 1)
                for t in range(NT):
                    last = pe.matmul(ps[7][:, tile(t)], oT[:, tile(t)], w(wo), start=True, stop=True)
            else:
                for t in range(NT):
                    last = pe.matmul(ps[7][:, tile(t)], aT[:, tile(t)], value[:, :], start=True, stop=True)
            last.then_inc(s["y_in_psum"], 1)

        @block.scalar
        def _(act):
            need(act)
            act.wait_ge(s["k_in_psum"], 1)
            if relu:
                st = Steps(act, s["scalar_step"])
                st.link(act.activation(kT[:, :], ps[1][:, 0:S2], ACT.Relu, bias=w(bq)))
                act.activation(kT[:, :], kT[:, :], ACT.Copy, scale=w(kd)).then_inc(s["k_ready"], 1)
            else:
                act.activation(kT[:, :], ps[1][:, 0:S2], ACT.Copy).then_inc(s["k_ready"], 1)
            norm_scalar(net, s, act, ps[0])
            act.wait_ge(s["q_in_psum"], 1)
            act.activation(qT[:, :], ps[3][:, :], ACT.Relu if relu else ACT.Identity,
                           bias=w(bq) if bq else 0.0).then_inc(s["q_ready"], 1)
            act.wait_ge(s["max_ready"], 1)
            for t in range(NT):
                act.activation(a[:, t, :], sc[:, t, :], ACT.Exp, bias=nmx[:, t:t + 1], scale=scale,
                               accum_out=den[:, t:t + 1]).then_inc(s["probs_ready"], 1)
            act.wait_ge(s["aT_in_psum"], 1)
            act.activation(aT[:, :], ps[5][0:S2, :], ACT.Copy).then_inc(s["aT_ready"], 1)
            if wo:
                act.wait_ge(s["o_in_psum"], 1)
                act.activation(oT[:, :], ps[6][:, :], ACT.Copy).then_inc(s["oT_ready"], 1)

        @block.gpsimd
        def _(g):
            need(g)
            norm_pool(net, s, g, Steps(g, s["pool_step"]))

        @block.vector
        def _(v):
            need(v)
            st = Steps(v, s["vector_step"])
            norm_vector(net, s, v, st)
            if wv:
                v.wait_ge(s["v_in_psum"], 1)
                if bv:
                    v.tensor_tensor(vt[:, :], ps[2][0:S2, 0:D], w(bv)[0:S2, :], ALU.add).then_inc(s["v_ready"], 1)
                else:
                    v.tensor_copy(vt[:, :], ps[2][0:S2, 0:D]).then_inc(s["v_ready"], 1)
            if masked:
                st.link(v.tensor_scalar(keep[:, :], net.bias[:, :], -1.0, 1.0, ALU.mult, ALU.add))
                v.wait_ge(s["scores_in_psum"], 1)
                st.link(v.tensor_tensor(sc[:, :, :], scores, bc(keep[:, :], NT), ALU.mult))
                st.link(v.tensor_scalar(keep[:, :], net.bias[:, :], NEG, None, ALU.mult))
                st.link(v.tensor_tensor(sc[:, :, :], sc[:, :, :], bc(keep[:, :], NT), ALU.add))
            else:
                v.wait_ge(s["scores_in_psum"], 1)
                st.link(v.tensor_copy(sc[:, :, :], scores))
            st.link(v.tensor_reduce(mx[:, :], sc[:, :, :], AX.X, ALU.max))
            v.tensor_scalar(nmx[:, :], mx[:, :], -scale, None, ALU.mult).then_inc(s["max_ready"], 1)
            v.wait_ge(s["probs_ready"], NT)
            st.link(v.reciprocal(rden[:, :], den[:, :]))
            if bo:
                st.link(v.tensor_tensor(net.x[:, :, :], net.x[:, :, :], bc(w(bo), NT), ALU.add))
            v.wait_ge(s["y_in_psum"], 1)
            for t in range(NT):
                st.step(v.scalar_tensor_tensor(out=net.x[:, t, :], in0=ps[7][:, tile(t)], scalar=rden[:, t:t + 1],
                                               in1=net.x[:, t, :], op0=ALU.mult, op1=ALU.add))
            st.wait()

    return body




def shift_tensor(net, s, pe, y, bank):
    halves = bank[:, 0:NT * 64].rearrange("p (t d) -> p t d", t=NT)
    pe.matmul(halves, net.w("shift"), y[:, :, 64:D], start=True, stop=False)
    pe.matmul(halves[:, 1:NT, :], net.w("carry"), y[:, 0:NT - 1, 64:D], start=False, stop=True)\
      .then_inc(s["shift_in_psum"], 1)


def shift_scalar(net, s, act, steps, y, h, bank):
    steps.step(act.activation(h[:, :, 0:64], y[:, :, 0:64], ACT.Copy))
    act.wait_ge(s["shift_in_psum"], 1)
    act.activation(h[:, :, 64:D], bank[:, 0:NT * 64].rearrange("p (t d) -> p t d", t=NT), ACT.Copy)\
       .then_inc(s["shifted_ready"], 1)


def f0_attn(net, l, first):
    nc, w, ps, y = net.nc, net.w, net.ps, net.y
    HB = F0_H // 2
    N = NT * HB

    def body(s, sb, block, need):
        h = sb("h", [P, NT, D])
        hT = sb("hT", [D, T])
        raw = sb("raw", [P, 2, 2, F0_IN])
        sq = sb("sq", [P, 2, F0_IN])
        ss = sb("ss", [P, 2, NT, F0_H])
        rn = sb("rn", [P, 2, NT, F0_H])
        sq8 = sb("sq8", [P, NT, F0_H])
        cs = sb("cs", [P, 2, F0_IN])
        sn = sb("sn", [P, 2, F0_IN])
        rot = sb("rot", [P, 2, 2, F0_IN])
        v = sb("v", [P, NT, F0_IN])
        qT = sb("qT", [P, HB, T])
        kT = sb("kT", [P, 2, HB, T])
        sc = sb("sc", [P, 4, 2, 192])
        a = sb("a", [P, 4, 2, 256])
        mx = sb("mx", [P, N, 2])
        nmx = sb("nmx", [P, N, 2])
        den = sb("den", [P, N, 2])
        rden = sb("rden", [P, N, 2])
        aT = sb("aT", [P, 2, 2, 256])
        oT = raw[:, :, :, :].rearrange("p a b t -> p (a b) t")
        keys = lambda t: slice(64 if t == 0 else 0, 192)

        def turn(pe, t):
            for j in range(2):
                pe.wait_ge(s["rotated"], 2 * t + j + 1)
                if t >= 1:
                    pe.wait_ge(s["qkT_ready"], 2 * t + j - 1)
                for hb in range(HB):
                    last = pe.transpose(ps[j][:, tile(hb)], rot[:, t % 2, j, tile(hb)], w("ident"))
                last.then_inc(s["qkT_in_psum"], 1)

        @block.tensor
        def _(pe):
            need(pe)
            if first:
                pe.wait_ge(s["norm_ready"], 1)
            shift_tensor(net, s, pe, y, ps[0])
            pe.wait_ge(s["shifted_ready"], 1)
            transpose_tensor(net, s, pe, h, ps[1], "hT_in_psum")
            pe.wait_ge(s["hT_ready"], 1)
            for t in range(NT):
                if t >= 2:
                    pe.wait_ge(s["raw_ready"], t - 1)
                for j in range(3):
                    last = pe.matmul(ps[2 + 3 * (t % 2) + j][:, :], hT[:, tile(t)],
                                     w(f"f0_wqkv{l}", j * F0_IN, (j + 1) * F0_IN), start=True, stop=True)
                last.then_inc(s["qkv_in_psum"], 1)
                if t >= 1:
                    turn(pe, t - 1)
            turn(pe, NT - 1)
            pe.wait_ge(s["raw_ready"], NT)
            pe.wait_ge(s["qkT_ready"], 2 * NT)
            for i in range(N + 4):
                if i < N:
                    t, hb = divmod(i, HB)
                    if i >= 2:
                        pe.wait_ge(s["masked_ready"], i - 1)
                    for e in range(2):
                        lo = max(P * t - 64, 0)
                        last = pe.matmul(ps[2 + 2 * (i % 2) + e][:, keys(t)],
                                         qT[:, hb, tile(t)], kT[:, e, hb, lo:P * t + P], start=True, stop=True)
                    last.then_inc(s["scores_in_psum"], 1)
                if 3 <= i < N + 3:
                    j = i - 3
                    t = j // HB
                    pe.wait_ge(s["probs_ready"], j + 1)
                    if j >= 2:
                        pe.wait_ge(s["aT_ready"], j - 1)
                    for e in range(2):
                        for c in range(0 if t else 1, 2):
                            last = pe.transpose(ps[6 + j % 2][:, 256 * e + P * c:256 * e + P * c + P],
                                                a[:, j % 4, e, tile(c)], w("ident"))
                    last.then_inc(s["aT_in_psum"], 1)
                if i >= 4:
                    j = i - 4
                    t, hb = divmod(j, HB)
                    pe.wait_ge(s["aT_ready"], j + 1)
                    if hb == 0 and t >= 2:
                        pe.wait_ge(s["oT_ready"], t - 1)
                    for e in range(2):
                        f = slice((2 * hb + e) * F0_HD, (2 * hb + e + 1) * F0_HD)
                        for c in range(0 if t else 1, 2):
                            last = pe.matmul(ps[t % 2][64 * e:64 * e + 64, tile(hb)], v[:, t - 1 + c, f],
                                             aT[:, j % 2, e, tile(c)], start=(c == (0 if t else 1)), stop=(c == 1))
                    last.then_inc(s["pairs_done"], 1)
            pe.wait_ge(s["oT_ready"], NT)
            for t in range(NT):
                for hb in range(HB):
                    last = pe.matmul(ps[2][:, tile(t)], oT[:, hb, tile(t)], w(f"f0_wo{l}", hb * D, (hb + 1) * D),
                                     start=(hb == 0), stop=(hb == HB - 1))
            last.then_inc(s["y_in_psum"], 1)

        @block.scalar
        def _(act):
            need(act)
            st = Steps(act, s["scalar_step"])
            if first:
                act.wait_ge(s["norm_ready"], 1)
            shift_scalar(net, s, act, st, y, h, ps[0])
            act.wait_ge(s["hT_in_psum"], 1)
            act.activation(hT[:, :], ps[1][:, :], ACT.Copy).then_inc(s["hT_ready"], 1)

            def evac_turned(t):
                act.wait_ge(s["qkT_in_psum"], 2 * t + 1)
                act.activation(qT[:, :, tile(t)], ps[0][:, :].rearrange("p (b t) -> p b t", b=HB), ACT.Copy)\
                   .then_inc(s["qkT_ready"], 1)
                act.wait_ge(s["qkT_in_psum"], 2 * t + 2)
                for e in range(2):
                    last = act.activation(kT[:, e, :, tile(t)], ps[1][:, :].rearrange("p (b t) -> p b t", b=HB), ACT.Copy,
                                          scale=w("halves", e, e + 1))
                last.then_inc(s["qkT_ready"], 1)

            for t in range(NT):
                act.wait_ge(s["qkv_in_psum"], t + 1)
                if t >= 2:
                    act.wait_ge(s["rotated"], 2 * (t - 1))
                for j in range(2):
                    st.step(act.activation(raw[:, t % 2, j, :], ps[2 + 3 * (t % 2) + j][:, :], ACT.Copy))
                    if t >= 1:
                        act.wait_ge(s["squares_summed"], 2 * t + j - 1)
                    act.activation(sq[:, j, :], ps[2 + 3 * (t % 2) + j][:, :], ACT.Square).then_inc(s["squares_ready"], 1)
                act.activation(v[:, t, :], ps[4 + 3 * (t % 2)][:, :], ACT.Copy).then_inc(s["raw_ready"], 1)
                if t >= 1:
                    evac_turned(t - 1)
            evac_turned(NT - 1)
            for i in range(N + 4):
                if i < N:
                    t = i // HB
                    act.wait_ge(s["max_ready"], i + 1)
                    if i >= 4:
                        act.wait_ge(s["aT_in_psum"], i - 3)
                    for e in range(2):
                        k = keys(t)
                        last = act.activation(a[:, i % 4, e, 64 + k.start:256], sc[:, i % 4, e, k], ACT.Exp,
                                              bias=nmx[:, i, e:e + 1], scale=sq8[:, t, 2 * (i % HB) + e:2 * (i % HB) + e + 1],
                                              accum_out=den[:, i, e:e + 1])
                    last.then_inc(s["exp_ready"], 1)
                if 3 <= i < N + 3:
                    j = i - 3
                    act.wait_ge(s["aT_in_psum"], j + 1)
                    if j >= 2:
                        act.wait_ge(s["pairs_done"], j - 1)
                    k = slice(0 if j >= HB else P, 256)
                    act.activation(aT[:, j % 2, :, k], ps[6 + j % 2][:, :].rearrange("p (e k) -> p e k", e=2)[:, :, k],
                                   ACT.Copy).then_inc(s["aT_ready"], 1)
                if i >= 4 and (i - 4) % HB == HB - 1:
                    t = (i - 4) // HB
                    act.wait_ge(s["pairs_done"], HB * (t + 1))
                    act.activation(oT[:, :, tile(t)], ps[t % 2][:, :].rearrange("p (b t) -> p b t", b=HB), ACT.Copy)\
                       .then_inc(s["oT_ready"], 1)

        @block.gpsimd
        def _(g):
            need(g)
            st = Steps(g, s["pool_step"])
            g.memset(a[:, :, :, 0:64], 0.0).then_inc(s["pad_ready"], 1)
            if first:
                norm_pool(net, s, g, st)
            for t in range(NT):
                for j in range(2):
                    g.wait_ge(s["squares_summed"], 2 * t + j + 1)
                    st.link(g.tensor_scalar(ss[:, j, t, :], ss[:, j, t, :], 1e-24, 1.0, ALU.max, ALU.mult))
                    g.tensor_tensor(rn[:, j, t, :], ss[:, j, t, :], net.w("neghalf", 0, F0_H), ALU.pow)\
                     .then_inc(s["norms_ready"], 1)

        @block.vector
        def _(v_):
            need(v_)
            st = Steps(v_, s["vector_step"])
            if first:
                norm_vector(net, s, v_, st, dst=y)
            for t in range(NT):
                for j in range(2):
                    src = raw[:, t % 2, j, :].rearrange("p (h d) -> p h d", h=F0_H)
                    co = cs[:, j, :].rearrange("p (h d) -> p h d", h=F0_H)
                    si = sn[:, j, :].rearrange("p (h d) -> p h d", h=F0_H)
                    ro = rot[:, t % 2, j, :].rearrange("p (h d) -> p h d", h=F0_H)
                    C, S = net.rot[:, l, j, 0, t, :], net.rot[:, l, j, 1, t, :]
                    v_.wait_ge(s["squares_ready"], 2 * t + j + 1)
                    v_.tensor_reduce(ss[:, j, t, :], sq[:, j, :].rearrange("p (h d) -> p h d", h=F0_H), AX.X, ALU.add)\
                      .then_inc(s["squares_summed"], 1)
                    st.step(v_.tensor_tensor(co, src, bc(C, F0_H), ALU.mult))
                    st.step(v_.tensor_tensor(si[:, :, 0:32], src[:, :, 32:64], bc(S[:, 0:32], F0_H), ALU.mult))
                    st.link(v_.tensor_tensor(si[:, :, 32:64], src[:, :, 0:32], bc(S[:, 32:64], F0_H), ALU.mult))
                    if t >= 2:
                        v_.wait_ge(s["qkT_in_psum"], 2 * (t - 2) + j + 1)
                    if j == 0:
                        v_.tensor_tensor(ro, co, si, ALU.add).then_inc(s["rotated"], 1)
                    else:
                        st.link(v_.tensor_tensor(co, co, si, ALU.add))
                        v_.wait_ge(s["norms_ready"], 2 * t + 2)
                        v_.tensor_tensor(ro, co, bci(rn[:, 1, t, :], F0_HD), ALU.mult).then_inc(s["rotated"], 1)
            st.link(v_.tensor_scalar(sq8[:, :, :], rn[:, 0, :, :], 8.0, None, ALU.mult))
            v_.wait_ge(s["pad_ready"], 1)
            for i in range(N + 1):
                if i < N:
                    t, hb = divmod(i, HB)
                    v_.wait_ge(s["scores_in_psum"], i + 1)
                    if i >= 4:
                        v_.wait_ge(s["exp_ready"], i - 3)
                    for e in range(2):
                        k = keys(t)
                        last = v_.tensor_tensor_reduce(sc[:, i % 4, e, k], ps[2 + 2 * (i % 2) + e][:, k],
                                                       w("band", k.start, 192), 1.0, -3.0e38, ALU.add, ALU.max,
                                                       mx[:, i, e:e + 1])
                    last.then_inc(s["masked_ready"], 1)
                    v_.wait_ge(s["masked_ready"], i + 1)
                    v_.scalar_tensor_tensor(out=nmx[:, i, :], in0=mx[:, i, :], scalar=-1.0, in1=sq8[:, t, 2 * hb:2 * hb + 2],
                                            op0=ALU.mult, op1=ALU.mult).then_inc(s["max_ready"], 1)
                if i >= 1:
                    j = i - 1
                    k = slice(64 + keys(j // HB).start, 256)
                    v_.wait_ge(s["exp_ready"], j + 1)
                    st.link(v_.reciprocal(rden[:, j, :], den[:, j, :]))
                    for e in range(2):
                        last = v_.tensor_scalar(a[:, j % 4, e, k], a[:, j % 4, e, k], rden[:, j, e:e + 1], None, ALU.mult)
                    last.then_inc(s["probs_ready"], 1)
            v_.wait_ge(s["y_in_psum"], 1)
            st.link(v_.tensor_tensor(y[:, :, :], y[:, :, :], ps[2][:, :].rearrange("p (t d) -> p t d", t=NT), ALU.add))

    return body


def f0_mlp(net, l, last_layer):
    nc, w, ps, y = net.nc, net.w, net.ps, net.y
    C = len(F0_CH)

    def body(s, sb, block, need):
        h = sb("h", [P, NT, D])
        hn = sb("hn", [P, NT, D])
        hT = sb("hT", [D, T])
        gate = sb("gate", [P, C, T])
        u = sb("u", [P, C, T])

        @block.tensor
        def _(pe):
            need(pe)
            shift_tensor(net, s, pe, y, ps[0])
            pe.wait_ge(s["shifted_ready"], 1)
            norm_tensor(net, s, pe, ps[0], src=hn)
            pe.wait_ge(s["hT_ready"], 1)
            for c, (lo, n) in enumerate(F0_CH):
                pe.matmul(ps[4 + c][0:n, :], w(f"f0_w1{l}", F0_HID + lo, F0_HID + lo + n), hT[:, :], start=True, stop=True)\
                  .then_inc(s["gate_in_psum"], 1)
                pe.matmul(ps[1 + c][0:n, :], w(f"f0_w1{l}", lo, lo + n), hT[:, :], start=True, stop=True)\
                  .then_inc(s["up_in_psum"], 1)
            pe.wait_ge(s["u_ready"], C)
            for t in range(NT):
                for c, (_, n) in enumerate(F0_CH):
                    last = pe.matmul(ps[7][:, tile(t)], u[0:n, c, tile(t)], w(f"f0_w2{l}", c * D, (c + 1) * D)[0:n, :],
                                     start=(c == 0), stop=(c == C - 1))
            last.then_inc(s["y_in_psum"], 1)

        @block.scalar
        def _(act):
            need(act)
            shift_scalar(net, s, act, Steps(act, s["scalar_step"]), y, h, ps[0])
            act.wait_ge(s["normT_in_psum"], 1)
            act.activation(hT[:, :], ps[0][:, :], ACT.Identity, bias=w(f"f0_b{l}"), scale=w(f"f0_g{l}")).then_inc(s["hT_ready"], 1)
            for c, (_, n) in enumerate(F0_CH):
                act.wait_ge(s["gate_in_psum"], c + 1)
                act.activation(gate[0:n, c, :], ps[4 + c][0:n, :], ACT.Gelu, bias=w(f"f0_b1g{l}", c, c + 1)[0:n, :])\
                   .then_inc(s["gate_ready"], 1)

        @block.gpsimd
        def _(g):
            need(g)
            norm_pool(net, s, g, Steps(g, s["pool_step"]))

        @block.vector
        def _(v):
            need(v)
            st = Steps(v, s["vector_step"])
            v.wait_ge(s["shifted_ready"], 1)
            norm_vector(net, s, v, st, src=h, dst=hn)
            for c, (_, n) in enumerate(F0_CH):
                v.wait_ge(s["up_in_psum"], c + 1)
                v.wait_ge(s["gate_ready"], c + 1)
                v.scalar_tensor_tensor(out=u[0:n, c, :], in0=ps[1 + c][0:n, :], scalar=w(f"f0_b1a{l}", c, c + 1)[0:n, :],
                                       in1=gate[0:n, c, :], op0=ALU.add, op1=ALU.mult).then_inc(s["u_ready"], 1)
            st.link(v.tensor_tensor(y[:, :, :], y[:, :, :], bc(w(f"f0_b2{l}"), NT), ALU.add))
            v.wait_ge(s["y_in_psum"], 1)
            st.link(v.tensor_tensor(y[:, :, :], y[:, :, :], ps[7][:, :].rearrange("p (t d) -> p t d", t=NT), ALU.add))
            if last_layer:
                st.link(v.tensor_tensor(net.x[:, :, :], net.x[:, :, :], y[:, :, :], ALU.add))

    return body


def l0_ffn(net):
    parts = []
    for l in range(F0_L):
        parts += [f0_attn(net, l, l == 0), f0_mlp(net, l, l == F0_L - 1)]
    return parts




def l1_attn(net):
    nc, w, ps = net.nc, net.w, net.ps
    SETS, R = A1_H // 4, 4
    ORDER = list(range(NT))[::-1]
    scale = A1_HD ** -0.5
    OUT, MISC = ps[6], ps[7]

    def body(s, sb, block, need):
        qT = sb("qT", [D, T])
        kT = sb("kT", [D, T])
        km = sb("km", [D, A1_H, T])
        mT = sb("mT", [P, 2, T], BF16)
        va = sb("va", [P, NT, A1_H, 32])
        junk = sb("junk", [P, 2, T])
        mx = sb("mx", [P, SETS, NT, R])
        mp = sb("mp", [P, SETS, NT, P], BF16)
        ex = sb("ex", [P, 2, R, T])
        oS = sb("oS", [P, T])
        rden = sb("rden", [P, SETS, NT, R])
        cat = sb("cat", [P, D, NT])
        rowgroup = [slice(32 * r, 32 * r + 32) for r in range(R)]

        def pass1_tensor(pe, j, i, k):
            u = (j * NT + i) * R + k
            t = ORDER[i]
            if u >= 2:
                pe.wait_ge(s["row_max"], u - 1)
            pe.matmul(ps[u % 2][:, 0:P * (t + 1)], qT[:, tile(t)], km[:, R * j + k, 0:P * (t + 1)],
                      start=True, stop=True).then_inc(s["scores_in_psum"], 1)

        def maxima_tensor(pe, j):
            pe.wait_ge(s["mp_ready"], j + 1)
            if j >= 2:
                pe.wait_ge(s["cat_ready"], j - 1)
            elif j == 1:
                pe.wait_ge(s["mT_ready"], 1)
            for t in range(NT):
                last = pe.transpose(MISC[:, :].bitcast(BF16)[:, tile(t)], mp[:, j, t, :], net.ident16[:, :])
            last.then_inc(s["maxima_in_psum"], 1)

        def apply_tensor(pe, g):
            j, kt = divmod(g, NT)
            pe.wait_ge(s["ex_ready"], g + 1)
            if kt == 0 and j >= 1:
                pe.wait_ge(s["oS_ready"], j)
            for r in range(R):
                last = pe.matmul(OUT[rowgroup[r], P * kt:T], va[:, kt, R * j + r, :], ex[:, g % 2, r, 0:T - P * kt],
                                 start=(kt == 0), stop=(kt == NT - 1))
            last.then_inc(s["applied"], 1)

        def heads_tensor(pe, j):
            pe.wait_ge(s["oS_ready"], j + 1)
            pe.wait_ge(s["mT_ready"], min(j + 2, SETS))
            if j == SETS - 1:
                pe.wait_ge(s["cat_ready"], j)
            for t in range(NT):
                last = pe.transpose(MISC[:, tile(t)], oS[:, tile(t)], w("ident"))
            last.then_inc(s["heads_in_psum"], 1)

        @block.tensor
        def _(pe):
            need(pe)
            norm_tensor(net, s, pe, ps[0])
            pe.wait_ge(s["normT_ready"], 1)
            pe.matmul(ps[2][:, :], w("a1_wk"), net.xnT[:, :], start=True, stop=True).then_inc(s["k_in_psum"], 1)
            pe.matmul(ps[3][:, :], w("a1_wq"), net.xnT[:, :], start=True, stop=True).then_inc(s["q_in_psum"], 1)
            for t in range(NT):
                last = pe.matmul(ps[4][:, tile(t)], net.xnT[:, tile(t)], w("a1_wv"), start=True, stop=True)
            last.then_inc(s["v_in_psum"], 1)
            pe.wait_ge(s["q_ready"], 1)
            for i in range(NT):
                for r in range(R):
                    if i == 0:
                        pe.wait_ge(s["km_ready"], r + 1)
                    pass1_tensor(pe, 0, i, r)
            maxima_tensor(pe, 0)
            pe.wait_ge(s["va_ready"], 1)
            for j in range(SETS):
                pe.wait_ge(s["mT_ready"], j + 1)
                if j == 0:
                    pe.wait_ge(s["km_ready"], 2 * R)
                    pe.wait_ge(s["more_km_ready"], 2 * R)
                for kt in range(NT):
                    g = j * NT + kt
                    if kt == 3 and j >= 1:
                        heads_tensor(pe, j - 1)
                    for r in range(R):
                        if g >= 1:
                            pe.wait_ge(s["exp_done"], R * (g - 1) + r + 1)
                        pe.matmul(ps[2 + r][:, 0:T - P * kt], km[:, R * j + r, tile(kt)], qT[:, P * kt:T], start=True, stop=False)
                        pe.matmul(ps[2 + r][:, 0:T - P * kt], net.pick16[:, r:r + 1].to_broadcast([P, P]), mT[:, j % 2, P * kt:T],
                                  start=False, stop=True).then_inc(s["keyed_in_psum"], 1)
                        if j + 1 < SETS:
                            pass1_tensor(pe, j + 1, kt, r)
                    if g >= 1:
                        apply_tensor(pe, g - 1)
                if j + 1 < SETS:
                    maxima_tensor(pe, j + 1)
            apply_tensor(pe, SETS * NT - 1)
            heads_tensor(pe, SETS - 1)
            pe.wait_ge(s["cat_ready"], SETS)
            for t in range(NT):
                last = pe.matmul(ps[0][:, tile(t)], cat[:, 32 * t:32 * t + 32, :].rearrange("p e c -> p (e c)"),
                                 w("a1_wo"), start=True, stop=True)
            last.then_inc(s["y_in_psum"], 1)

        @block.scalar
        def _(act):
            need(act)
            norm_scalar(net, s, act, ps[0])
            act.wait_ge(s["k_in_psum"], 1)
            act.activation(kT[:, :], ps[2][:, :], ACT.Copy).then_inc(s["k_ready"], 1)
            act.wait_ge(s["q_in_psum"], 1)
            act.activation(qT[:, :], ps[3][:, :], ACT.Copy).then_inc(s["q_ready"], 1)
            act.wait_ge(s["v_in_psum"], 1)
            act.wait_ge(s["va_filled"], 1)
            act.activation(va[:, :, :, 0:A1_HD], ps[4][:, :].rearrange("p (t h d) -> p t h d", t=NT, h=A1_H), ACT.Copy)\
               .then_inc(s["va_ready"], 1)
            for j in range(SETS + 1):
                for kt in range(NT if j < SETS else 2):
                    if j >= 1 and kt == 1:
                        act.wait_ge(s["applied"], NT * j)
                        if j >= 2:
                            act.wait_ge(s["heads_in_psum"], j - 1)
                        act.activation(oS[:, :], OUT[:, :], ACT.Copy).then_inc(s["oS_ready"], 1)
                    if j < SETS:
                        g = j * NT + kt
                        if g >= 2:
                            act.wait_ge(s["applied"], g - 1)
                        for r in range(R):
                            act.wait_ge(s["keyed_in_psum"], R * g + r + 1)
                            act.activation(ex[:, g % 2, r, 0:T - P * kt], ps[2 + r][:, 0:T - P * kt], ACT.Exp, scale=scale)\
                               .then_inc(s["exp_done"], 1)

        @block.gpsimd
        def _(g_):
            need(g_)
            st = Steps(g_, s["pool_step"])
            st.step(g_.memset(va[:, :, :, A1_HD + 1:32], 0.0))
            st.step(g_.memset(va[:, :, :, A1_HD:A1_HD + 1], 1.0))
            g_.memset(mp[:, :, :, :], 0.0).then_inc(s["va_filled"], 1)
            norm_pool(net, s, g_, st)
            g_.wait_ge(s["k_ready"], 1)
            for h in range(2 * R, A1_H):
                g_.tensor_scalar(km[:, h, :], kT[:, :], w("headsum", h, h + 1), 0.0, ALU.mult, ALU.add).then_inc(s["more_km_ready"], 1)
            for g in range(SETS * NT):
                g_.wait_ge(s["exp_done"], R * (g + 1))
                st.link(g_.tensor_scalar(ex[:, g % 2, :, 0:P], ex[:, g % 2, :, 0:P], 3.0e38, 1.0, ALU.min, ALU.mult))
                g_.tensor_tensor(ex[:, g % 2, :, 0:P], ex[:, g % 2, :, 0:P], bc(w("causalT"), R), ALU.mult).then_inc(s["ex_ready"], 1)

        @block.vector
        def _(v_):
            need(v_)
            st = Steps(v_, s["vector_step"])
            norm_vector(net, s, v_, st)
            v_.wait_ge(s["k_ready"], 1)
            for h in range(2 * R):
                v_.tensor_scalar(km[:, h, :], kT[:, :], w("headsum", h, h + 1), None, ALU.mult).then_inc(s["km_ready"], 1)

            def finish(j):
                v_.wait_ge(s["heads_in_psum"], j + 1)
                heads = MISC[:, :].rearrange("p (t r f) -> p t r f", t=NT, r=R)
                st.link(v_.reciprocal(rden[:, j, :, :], heads[:, :, :, A1_HD]))
                for t in range(NT):
                    last = v_.tensor_tensor(cat[:, 32 * j:32 * j + 32, t].rearrange("p (r d) -> p r d", r=R),
                                            heads[:, t, :, 0:A1_HD], bci(rden[:, j, t, :], A1_HD), ALU.mult)
                last.then_inc(s["cat_ready"], 1)

            for j in range(SETS + 1):
                for i in range(NT):
                    if j >= 2 and i == 3:
                        finish(j - 2)
                    for k in range(R if j < SETS else 0):
                        u = (j * NT + i) * R + k
                        t = ORDER[i]
                        n = P * (t + 1)
                        if u >= 2:
                            v_.wait_ge(s["row_max"], u - 1)
                        v_.wait_ge(s["scores_in_psum"], u + 1)
                        v_.tensor_tensor_reduce(junk[:, u % 2, 0:n], ps[u % 2][:, 0:n], w("causal", T - n, T), 1.0, -3.0e38,
                                                ALU.add, ALU.max, mx[:, j, t, k:k + 1]).then_inc(s["row_max"], 1)
                if j < SETS:
                    v_.wait_ge(s["row_max"], (j + 1) * NT * R)
                    if j == 0:
                        v_.wait_ge(s["va_filled"], 1)
                    st.link(v_.tensor_scalar(mp[:, j, :, 0:R], mx[:, j, :, :], -1.0, None, ALU.mult))
                    v_.scalar_tensor_tensor(out=mp[:, j, :, R:2 * R], in0=mx[:, j, :, :], scalar=-1.0, in1=mp[:, j, :, 0:R],
                                            op0=ALU.mult, op1=ALU.subtract).then_inc(s["mp_ready"], 1)
                    v_.wait_ge(s["maxima_in_psum"], j + 1)
                    v_.tensor_copy(mT[:, j % 2, :], MISC[:, :].bitcast(BF16)[:, 0:T]).then_inc(s["mT_ready"], 1)
            finish(SETS - 1)
            v_.wait_ge(s["y_in_psum"], 1)
            st.link(v_.tensor_tensor(net.x[:, :, :], net.x[:, :, :], ps[0][:, :].rearrange("p (t d) -> p t d", t=NT), ALU.add))

    return body




def top2_vector(net, s, v, st, values, sel, top, topi, topf):
    for t in range(NT):
        st.step(v.max(top[:, t, :], values[:, t, :]))
    st.wait()
    for t in range(NT):
        st.step(v.max_index(topi[:, t, :], top[:, t, :], values[:, t, :]))
    st.wait()
    st.link(v.tensor_copy(topf[:, :, :], topi[:, :, :]))
    for i in range(2):
        st.step(v.tensor_tensor(sel[:, i, :, :], net.w("iota8").rearrange("p (t e) -> p t e", t=NT), bci(topf[:, :, i], 8), ALU.is_equal))
    st.wait()


def l1_ffn(net):
    nc, w, ps = net.nc, net.w, net.ps
    E = M1_E
    N = 2 * E

    def body(s, sb, block, need):
        lg = sb("lg", [P, NT, E])
        gate = sb("gate", [P, NT, E])
        mx = sb("mx", [P, NT])
        den = sb("den", [P, NT])
        rden = sb("rden", [P, NT])
        top = sb("top", [P, NT, 8])
        topi = sb("topi", [P, NT, 8], U32)
        topf = sb("topf", [P, NT, 8])
        sel = sb("sel", [P, 2, NT, E])
        selT = sb("selT", [E, 2, T])
        boost = sb("boost", [P, NT, D])
        boostT = sb("boostT", [D, T])
        hT = sb("hT", [P, 2, 2, T])
        eo = sb("eo", [P, 2, NT, D])
        res = sb("res", [P, NT, D])

        @block.tensor
        def _(pe):
            need(pe)
            norm_tensor(net, s, pe, ps[0])
            pe.wait_ge(s["normT_ready"], 1)
            for t in range(NT):
                last = pe.matmul(ps[1][:, E * t:E * t + E], net.xnT[:, tile(t)], w("m1_wg"), start=True, stop=True)
            last.then_inc(s["logits_in_psum"], 1)
            pe.wait_ge(s["sel_ready"], 1)
            for i in range(2):
                for t in range(NT):
                    last = pe.transpose(ps[i][0:E, tile(t)], sel[:, i, t, :], w("ident"))
                last.then_inc(s["selT_in_psum"], 1)
            pe.wait_ge(s["selT_ready"], 2)
            for i in range(2):
                src = net.xnT if i == 0 else boostT
                if i == 1:
                    pe.wait_ge(s["boost_ready"], 1)
                    transpose_tensor(net, s, pe, boost, ps[0], "boostT_in_psum")
                    pe.wait_ge(s["boostT_ready"], 1)
                for t in range(NT):
                    last = pe.matmul(ps[1][:, tile(t)], selT[:, i, tile(t)], w("m1_b2"), start=True, stop=True)
                last.then_inc(s["bias_in_psum"], 1)
                for e in range(E + 1):
                    if e < E:
                        n = i * E + e
                        for c in range(2):
                            if n >= 2:
                                pe.wait_ge(s["hidden_ready"], 2 * (n - 2) + c + 1)
                            pe.matmul(ps[2 + 2 * (n % 2) + c][:, :], w("m1_w1", e * M1_H + c * P, e * M1_H + (c + 1) * P),
                                      src[:, :], start=True, stop=True).then_inc(s["hidden_in_psum"], 1)
                    if e >= 1:
                        n = i * E + e - 1
                        pe.wait_ge(s["hidden_ready"], 2 * (n + 1))
                        if n >= 2:
                            pe.wait_ge(s["added"], n - 1)
                        for t in range(NT):
                            for c in range(2):
                                last = pe.matmul(ps[6 + n % 2][:, tile(t)], hT[:, n % 2, c, tile(t)],
                                                 w("m1_w2", (2 * (e - 1) + c) * D, (2 * (e - 1) + c + 1) * D),
                                                 start=(c == 0), stop=(c == 1))
                        last.then_inc(s["expert_in_psum"], 1)

        @block.scalar
        def _(act):
            need(act)
            norm_scalar(net, s, act, ps[0])
            act.wait_ge(s["logits_shifted"], 1)
            act.activation(gate[:, :, :], lg[:, :, :], ACT.Exp).then_inc(s["gate_exp"], 1)
            for i in range(2):
                act.wait_ge(s["selT_in_psum"], i + 1)
                act.activation(selT[:, i, :], ps[i][0:E, :], ACT.Copy).then_inc(s["selT_ready"], 1)
            for n in range(N):
                if n == E:
                    act.wait_ge(s["boostT_in_psum"], 1)
                    act.activation(boostT[:, :], ps[0][:, :], ACT.Copy).then_inc(s["boostT_ready"], 1)
                for c in range(2):
                    act.wait_ge(s["hidden_in_psum"], 2 * n + c + 1)
                    if n >= 2:
                        act.wait_ge(s["expert_in_psum"], n - 1)
                    b = 2 * (n % E) + c
                    act.activation(hT[:, n % 2, c, :], ps[2 + 2 * (n % 2) + c][:, :], ACT.Relu, bias=w("m1_b1", b, b + 1))\
                       .then_inc(s["hidden_ready"], 1)

        @block.gpsimd
        def _(g):
            need(g)
            st = Steps(g, s["pool_step"])
            norm_pool(net, s, g, st)
            norm_pool(net, s, g, st, tag="out_")

        @block.vector
        def _(v):
            need(v)
            st = Steps(v, s["vector_step"])
            norm_vector(net, s, v, st)
            v.wait_ge(s["logits_in_psum"], 1)
            st.link(v.tensor_tensor(lg[:, :, :], ps[1][:, 0:NT * E].rearrange("p (t e) -> p t e", t=NT), bc(w("m1_bg"), NT), ALU.add))
            st.link(v.tensor_reduce(mx[:, :], lg[:, :, :], AX.X, ALU.max))
            v.tensor_tensor(lg[:, :, :], lg[:, :, :], bci(mx[:, :], E), ALU.subtract).then_inc(s["logits_shifted"], 1)
            v.wait_ge(s["gate_exp"], 1)
            st.link(v.tensor_reduce(den[:, :], gate[:, :, :], AX.X, ALU.add))
            st.link(v.reciprocal(rden[:, :], den[:, :]))
            st.link(v.tensor_tensor(gate[:, :, :], gate[:, :, :], bci(rden[:, :], E), ALU.mult))
            top2_vector(net, s, v, st, gate, sel, top, topi, topf)
            v.sem_inc(s["sel_ready"], 1)
            for i in range(2):
                v.wait_ge(s["bias_in_psum"], i + 1)
                st.link(v.tensor_copy(eo[:, i, :, :], ps[1][:, :].rearrange("p (t d) -> p t d", t=NT)))
                for e in range(E):
                    n = i * E + e
                    v.wait_ge(s["expert_in_psum"], n + 1)
                    if e >= 1:
                        v.wait_ge(s["added"], n)
                    for t in range(NT):
                        last = v.scalar_tensor_tensor(out=eo[:, i, t, :], in0=ps[6 + n % 2][:, tile(t)],
                                                      scalar=sel[:, i, t, e:e + 1], in1=eo[:, i, t, :],
                                                      op0=ALU.mult, op1=ALU.add)
                    last.then_inc(s["added"], 1)
                v.wait_ge(s["added"], E * (i + 1))
                if i == 0:
                    v.scalar_tensor_tensor(out=boost[:, :, :], in0=eo[:, 0, :, :], scalar=0.5, in1=net.xn[:, :, :],
                                           op0=ALU.mult, op1=ALU.add).then_inc(s["boost_ready"], 1)
            for i in range(2):
                for t in range(NT):
                    st.step(v.scalar_tensor_tensor(out=res[:, t, :], in0=eo[:, i, t, :], scalar=top[:, t, i:i + 1],
                                                   in1=(net.xn if i == 0 else res)[:, t, :], op0=ALU.mult, op1=ALU.add))
                st.wait()
            norm_vector(net, s, v, st, src=res, dst=boost, tag="out_")
            v.wait_ge(s["out_norm_ready"], 1)
            st.link(v.tensor_tensor(boost[:, :, :], boost[:, :, :], bc(w("m1_g"), NT), ALU.mult))
            st.link(v.tensor_tensor(boost[:, :, :], boost[:, :, :], bc(w("m1_b"), NT), ALU.add))
            st.link(v.tensor_tensor(net.x[:, :, :], net.x[:, :, :], boost[:, :, :], ALU.add))

    return body



A2_J = T // 32
A2_C = 64 + A2_NB + A2_M


def l2_attn(net):
    nc, w, ps = net.nc, net.w, net.ps
    J, C, GR = A2_J, A2_C, 4
    scale = A2_HD ** -0.5
    seg7 = C // 16

    def body(s, sb, block, need):
        xp = sb("xp", [D, 32 + T])
        qT = sb("qT", [D, T])
        kp = sb("kp", [D, 32 + T])
        t1 = sb("t1", [D, T])
        t2 = sb("t2", [D, T])
        qb = sb("qb", [D, GR, T])
        ktok = sb("ktok", [P, NT, D])
        vtok = sb("vtok", [P, NT, D])
        vall = sb("vall", [C, J, D])
        cs = sb("cs", [D, A2_NB + A2_M])
        vcs = sb("vcs", [P, D])
        qsum = sb("qsum", [D, 1])
        imp = sb("imp", [P, A2_NB])
        top = sb("top", [P, 8])
        topi = sb("topi", [P, 8], U32)
        topf = sb("topf", [P, 8])
        pos = sb("pos", [P, A2_M])
        onehot = sb("onehot", [P, NT, A2_M])
        gl32 = sb("gl32", [32, 3 * J])
        gl = sb("gl", [P, J, 3])
        gm = sb("gm", [P, J])
        gs = sb("gs", [P, J])
        sc = sb("sc", [P, 2, GR, 4, C])
        mx7 = sb("mx7", [P, GR * 4, seg7])
        mx = sb("mx", [P, GR * 4, 3])
        sm7 = sb("sm7", [P, GR * 4, seg7])
        sm = sb("sm", [P, GR * 4, 3])
        zero = sb("zero", [P, GR * 4, 3])
        wt7 = sb("wt7", [P, GR * 4, seg7])
        pT = sb("pT", [C, 2, T])
        r = sb("r", [D, 2, T])
        oT = sb("oT", [D, T])

        @block.tensor
        def _(pe):
            need(pe)
            norm_tensor(net, s, pe, ps[0])
            pe.wait_ge(s["normT_ready"], 1)
            for i, key in enumerate(("a2_wk", "a2_wks", "a2_wq", "a2_wqs")):
                pe.matmul(ps[1 + i][:, :], w(key), net.xnT[:, :], start=True, stop=True).then_inc(s["qk_in_psum"], 1)
            for t in range(NT):
                last = pe.matmul(ps[5][:, tile(t)], net.xnT[:, tile(t)], w("a2_wv"), start=True, stop=True)
            last.then_inc(s["v_in_psum"], 1)
            pe.wait_ge(s["xp_ready"], 1)
            for j in range(J):
                last = pe.matmul(ps[6][0:32, 3 * j:3 * j + 3], net.xnT[:, 32 * j:32 * j + 32], w("a2_wg"), start=True, stop=True)
            last.then_inc(s["gates32_in_psum"], 1)
            pe.wait_ge(s["gates32_ready"], 1)
            pe.matmul(ps[6][:, 0:3 * J], w("fourfold"), gl32[:, :], start=True, stop=True).then_inc(s["gates_in_psum"], 1)
            for q in range(J // 4):
                if q >= 2:
                    pe.wait_ge(s["vwin_ready"], q - 1)
                elif q == 0:
                    pe.wait_ge(s["normT_ready"], 1)
                for j in range(4 * q, 4 * q + 4):
                    last = pe.matmul(ps[(0, 7)[q % 2]][0:64, tile(j % 4)], xp[:, 32 * j:32 * j + 64], w("a2_wv"), start=True, stop=True)
                last.then_inc(s["vwin_in_psum"], 1)
            pe.wait_ge(s["k_ready"], 1)
            for t in range(NT):
                last = pe.transpose(ps[1][:, tile(t)], kp[:, 32 + t * P:32 + (t + 1) * P], w("ident"))
            last.then_inc(s["ktok_in_psum"], 1)
            pe.wait_ge(s["ktok_ready"], 1)
            for t in range(NT):
                pe.matmul(ps[2][:, 0:A2_NB], ktok[:, t, :], net.wck[:, t, :], start=(t == 0), stop=False)
            pe.matmul(ps[2][:, 0:A2_NB], w("a2_pe"), w("a2_wkc"), start=False, stop=True).then_inc(s["ck_in_psum"], 1)
            pe.wait_ge(s["vtok_ready"], 1)
            for t in range(NT):
                pe.matmul(ps[3][64:96, 0:D], net.wcv[:, t, :], vtok[:, t, :], start=(t == 0), stop=False)
            pe.matmul(ps[3][64:96, 0:D], w("a2_wvc"), w("a2_pe"), start=False, stop=True).then_inc(s["cv_in_psum"], 1)
            pe.wait_ge(s["ck_ready"], 1)
            pe.wait_ge(s["qsum_ready"], 1)
            pe.matmul(ps[4][:, 0:A2_NB], qsum[:, 0:1].to_broadcast([D, P]), cs[:, 0:A2_NB], start=True, stop=True)\
              .then_inc(s["importance_in_psum"], 1)
            pe.wait_ge(s["onehot_ready"], 1)
            for t in range(NT):
                last = pe.matmul(ps[5][:, 0:A2_M], ktok[:, t, :], onehot[:, t, :], start=(t == 0), stop=(t == NT - 1))
            last.then_inc(s["selk_in_psum"], 1)
            pe.wait_ge(s["cv_ready"], 1)
            for t in range(NT):
                last = pe.matmul(ps[3][96:96 + A2_M, 0:D], onehot[:, t, :], vtok[:, t, :], start=(t == 0), stop=(t == NT - 1))
            last.then_inc(s["selv_in_psum"], 1)
            pe.wait_ge(s["keys_ready"], 1)
            pe.wait_ge(s["vall_ready"], 1)
            pe.wait_ge(s["gates_ready"], 1)
            pe.wait_ge(s["vwin_ready"], J // 4)

            def scores(j):
                if j >= 2:
                    pe.wait_ge(s["masked"], j - 1)
                pe.wait_ge(s["qb_ready"], j + 1)
                for g in range(4):
                    q = qb[:, j % GR, tile(g)]
                    pe.matmul(ps[j % 2][:, g * C:g * C + 64], q, kp[:, 32 * j:32 * j + 64], start=True, stop=True)
                    last = pe.matmul(ps[j % 2][:, g * C + 64:(g + 1) * C], q, cs[:, :], start=True, stop=True)
                last.then_inc(s["scores_in_psum"], 1)

            def apply(j):
                pe.wait_ge(s["probs_ready"], j // GR + 1)
                if j >= 2:
                    pe.wait_ge(s["pT_ready"], j - 1)
                for g in range(4):
                    last = pe.transpose(ps[2 + j % 2][0:C, tile(g)], sc[:, (j // GR) % 2, j % GR, g, :], w("ident"))
                last.then_inc(s["pT_in_psum"], 1)
                if j >= 1:
                    values(j - 1)

            def values(j):
                pe.wait_ge(s["pT_ready"], j + 1)
                if j >= 2:
                    pe.wait_ge(s["picked"], j - 1)
                pe.matmul(ps[4 + j % 2][:, :], vall[:, j, :], pT[:, j % 2, :], start=True, stop=True)\
                  .then_inc(s["values_in_psum"], 1)

            for q in range(J // GR + 1):
                for j in range(GR * q, min(GR * q + GR, J)):
                    scores(j)
                for j in range(GR * (q - 1) if q else 0, GR * q):
                    apply(j)
            values(J - 1)
            pe.wait_ge(s["o_ready"], J)
            for t in range(NT):
                last = pe.matmul(ps[6][:, tile(t)], oT[:, tile(t)], w("a2_wo"), start=True, stop=True)
            last.then_inc(s["y_in_psum"], 1)

        @block.scalar
        def _(act):
            need(act)
            norm_scalar(net, s, act, ps[0])
            act.wait_ge(s["normT_ready"], 1)
            act.wait_ge(s["pads_ready"], 2)
            act.activation(xp[:, 32:], net.xnT[:, :], ACT.Copy).then_inc(s["xp_ready"], 1)
            act.wait_ge(s["v_in_psum"], 1)
            act.activation(vtok[:, :, :], ps[5][:, :].rearrange("p (t d) -> p t d", t=NT), ACT.Copy).then_inc(s["vtok_ready"], 1)
            for q in range(J // 4):
                act.wait_ge(s["vwin_in_psum"], q + 1)
                act.activation(vall[0:64, 4 * q:4 * q + 4, :], ps[(0, 7)[q % 2]][0:64, :].rearrange("p (j d) -> p j d", j=4), ACT.Copy)\
                   .then_inc(s["vwin_ready"], 1)
            act.wait_ge(s["ktok_in_psum"], 1)
            act.activation(ktok[:, :, :], ps[1][:, :].rearrange("p (t d) -> p t d", t=NT), ACT.Copy).then_inc(s["ktok_ready"], 1)
            act.wait_ge(s["ck_in_psum"], 1)
            act.activation(cs[:, 0:A2_NB], ps[2][:, 0:A2_NB], ACT.Copy).then_inc(s["ck_ready"], 1)
            act.wait_ge(s["cv_in_psum"], 1)
            act.activation(vcs[64:96, :], ps[3][64:96, 0:D], ACT.Copy).then_inc(s["cv_ready"], 1)
            act.wait_ge(s["selk_in_psum"], 1)
            act.activation(cs[:, A2_NB:], ps[5][:, 0:A2_M], ACT.Copy).then_inc(s["keys_ready"], 1)
            act.wait_ge(s["selv_in_psum"], 1)
            act.activation(vcs[96:C, :], ps[3][96:C, 0:D], ACT.Copy).then_inc(s["values_ready"], 1)
            act.wait_ge(s["gates_shifted"], 1)
            act.activation(gl[:, :, :], gl[:, :, :], ACT.Exp).then_inc(s["gates_exp"], 1)
            for j in range(0, J + GR, GR):
                if j < J:
                    act.wait_ge(s["shifted"], j // GR + 1)
                    act.activation(sc[:, (j // GR) % 2, :, :, :], sc[:, (j // GR) % 2, :, :, :], ACT.Exp, scale=scale)\
                       .then_inc(s["exp_ready"], 1)
                if j >= GR:
                    for i in range(j - GR, j):
                        act.wait_ge(s["pT_in_psum"], i + 1)
                        if i >= 2:
                            act.wait_ge(s["values_in_psum"], i - 1)
                        act.activation(pT[:, i % 2, :], ps[2 + i % 2][0:C, :], ACT.Copy).then_inc(s["pT_ready"], 1)

        @block.gpsimd
        def _(g):
            need(g)
            st = Steps(g, s["pool_step"])
            g.memset(xp[:, 0:32], 0.0).then_inc(s["pads_ready"], 1)
            g.memset(kp[:, 0:32], 0.0).then_inc(s["pads_ready"], 1)
            norm_pool(net, s, g, st)
            g.wait_ge(s["q_ready"], 1)
            for j in range(J):
                if j >= GR:
                    g.wait_ge(s["scores_in_psum"], j - GR + 1)
                g.tensor_tensor(qb[:, j % GR, :].rearrange("p (h q) -> p h q", h=A2_H), bc(qT[:, 32 * j:32 * j + 32], A2_H),
                                w("headmask").rearrange("p (h q) -> p h q", h=A2_H), ALU.mult).then_inc(s["qb_ready"], 1)

        @block.vector
        def _(v):
            need(v)
            st = Steps(v, s["vector_step"])
            norm_vector(net, s, v, st)
            for i, dst in enumerate((kp[:, 32:], qT[:, :])):
                v.wait_ge(s["qk_in_psum"], 2 * i + 2)
                if i == 1:
                    v.wait_ge(s["k_ready"], 1)
                st.step(v.tensor_tensor(t1[:, :], ps[1 + 2 * i][:, :], w("rope_c"), ALU.mult))
                st.link(v.tensor_tensor(t2[:, :], ps[2 + 2 * i][:, :], w("rope_s"), ALU.mult))
                v.tensor_tensor(dst, t1[:, :], t2[:, :], ALU.add).then_inc(s["k_ready" if i == 0 else "q_ready"], 1)
            v.wait_ge(s["q_ready"], 1)
            v.tensor_reduce(qsum[:, :], qT[:, :], AX.X, ALU.add).then_inc(s["qsum_ready"], 1)
            v.wait_ge(s["gates32_in_psum"], 1)
            v.tensor_copy(gl32[:, :], ps[6][0:32, 0:3 * J]).then_inc(s["gates32_ready"], 1)
            v.wait_ge(s["gates_in_psum"], 1)
            v.tensor_tensor(gl[:, :, :], ps[6][:, 0:3 * J].rearrange("p (j k) -> p j k", j=J), bc(w("a2_bg"), J), ALU.add)\
             .then_inc(s["gates_ready"], 1)
            v.wait_ge(s["gates_ready"], 1)
            st.link(v.tensor_reduce(gm[:, :], gl[:, :, :], AX.X, ALU.max))
            v.tensor_tensor(gl[:, :, :], gl[:, :, :], bci(gm[:, :], 3), ALU.subtract).then_inc(s["gates_shifted"], 1)
            v.wait_ge(s["importance_in_psum"], 1)
            st.link(v.tensor_copy(imp[:, :], ps[4][:, 0:A2_NB]))
            st.link(v.max(top[:, :], imp[:, :]))
            st.link(v.max_index(topi[:, :], top[:, :], imp[:, :]))
            st.link(v.tensor_copy(topf[:, :], topi[:, :]))
            st.link(v.scalar_tensor_tensor(out=pos[:, :].rearrange("p (k m) -> p k m", k=A2_TOP), in0=bci(topf[:, 0:A2_TOP], A2_SB),
                                           scalar=float(A2_CB), in1=bc(w("iota", 0, A2_SB), A2_TOP), op0=ALU.mult, op1=ALU.add))
            for t in range(NT):
                last = v.tensor_scalar(onehot[:, t, :], pos[:, :], w("tokid")[:, t:t + 1], None, ALU.is_equal)
            last.then_inc(s["onehot_ready"], 1)
            v.wait_ge(s["values_ready"], 1)
            v.tensor_copy(vall[64:C, :, :], bc(vcs[64:C, :], J)).then_inc(s["vall_ready"], 1)
            msel = net.mask2[:, :, 64 + A2_NB:C]
            st.link(v.tensor_tensor(msel, bc(pos[:, :], J), bci(w("query_id"), A2_M), ALU.is_gt))
            st.link(v.tensor_scalar(msel, msel, NEG, None, ALU.mult))
            v.wait_ge(s["gates_exp"], 1)
            st.link(v.tensor_reduce(gs[:, :], gl[:, :, :], AX.X, ALU.add))
            st.link(v.reciprocal(gm[:, :], gs[:, :]))
            st.link(v.tensor_tensor(gl[:, :, :], gl[:, :, :], bci(gm[:, :], 3), ALU.mult))

            def soften(q):
                b = q % 2
                rows7 = sc[:, b, :, :, :].rearrange("p j g (n k) -> p (j g n) k", k=16)
                for j in range(GR * q, GR * q + GR):
                    v.wait_ge(s["scores_in_psum"], j + 1)
                    if q >= 2:
                        v.wait_ge(s["pT_in_psum"], GR * (q - 1))
                    v.tensor_tensor(sc[:, b, j % GR, :, :], ps[j % 2][:, 0:4 * C].rearrange("p (g c) -> p g c", g=4),
                                    bc(net.mask2[:, j, :], 4), ALU.add).then_inc(s["masked"], 1)
                v.wait_ge(s["masked"], GR * (q + 1))
                st.link(v.tensor_reduce(mx7[:, :, :].rearrange("p r n -> p (r n)"), rows7, AX.X, ALU.max))
                segs = ((0, 4), (4, 6), (6, 7))
                for i, (lo, hi) in enumerate(segs):
                    st.step(v.tensor_reduce(mx[:, :, i], mx7[:, :, lo:hi], AX.X, ALU.max))
                st.wait()
                for i, (lo, hi) in enumerate(segs):
                    st.step(v.tensor_scalar(mx7[:, :, lo:hi], bci(mx[:, :, i], hi - lo), -1.0e20, None, ALU.max))
                st.wait()
                v.tensor_tensor(rows7, rows7, bci(mx7[:, :, :].rearrange("p r n -> p (r n)"), 16), ALU.subtract)\
                 .then_inc(s["shifted"], 1)

            def weigh(q):
                b = q % 2
                rows7 = sc[:, b, :, :, :].rearrange("p j g (n k) -> p (j g n) k", k=16)
                segs = ((0, 4), (4, 6), (6, 7))
                v.wait_ge(s["exp_ready"], q + 1)
                st.link(v.tensor_reduce(sm7[:, :, :].rearrange("p r n -> p (r n)"), rows7, AX.X, ALU.add))
                for i, (lo, hi) in enumerate(segs):
                    st.step(v.tensor_reduce(sm[:, :, i], sm7[:, :, lo:hi], AX.X, ALU.add))
                st.wait()
                st.link(v.tensor_scalar(zero[:, :, :], sm[:, :, :], 0.0, None, ALU.is_equal))
                st.link(v.tensor_tensor(sm[:, :, :], sm[:, :, :], zero[:, :, :], ALU.add))
                st.link(v.reciprocal(zero[:, :, :], sm[:, :, :]))
                for i, k in enumerate((2, 0, 1)):
                    lo, hi = segs[i]
                    st.step(v.tensor_tensor(sm[:, :, i].rearrange("p (j g) -> p j g", g=4), zero[:, :, i].rearrange("p (j g) -> p j g", g=4),
                                            bci(gl[:, GR * q:GR * q + GR, k], 4), ALU.mult))
                st.wait()
                for i, (lo, hi) in enumerate(segs):
                    st.step(v.tensor_copy(wt7[:, :, lo:hi], bci(sm[:, :, i], hi - lo)))
                st.wait()
                v.tensor_tensor(rows7, rows7, bci(wt7[:, :, :].rearrange("p r n -> p (r n)"), 16), ALU.mult)\
                 .then_inc(s["probs_ready"], 1)

            def pick(j):
                v.wait_ge(s["values_in_psum"], j + 1)
                if j >= 2:
                    v.wait_ge(s["o_ready"], j - 1)
                v.tensor_tensor(r[:, j % 2, :], ps[4 + j % 2][:, :], w("headmask"), ALU.mult).then_inc(s["picked"], 1)
                v.wait_ge(s["picked"], j + 1)
                v.tensor_reduce(oT[:, 32 * j:32 * j + 32], r[:, j % 2, :].rearrange("p (h q) -> p q h", h=A2_H), AX.X, ALU.add)\
                 .then_inc(s["o_ready"], 1)

            for q in range(J // GR):
                soften(q)
                if q >= 1:
                    for j in range(max(GR * (q - 1) - 1, 0), GR * q - 1):
                        pick(j)
                weigh(q)
            for j in range(J - GR - 1, J):
                pick(j)
            st.link(v.tensor_tensor(net.x[:, :, :], net.x[:, :, :], bc(w("a2_bo"), NT), ALU.add))
            v.wait_ge(s["y_in_psum"], 1)
            st.link(v.tensor_tensor(net.x[:, :, :], net.x[:, :, :], ps[6][:, :].rearrange("p (t d) -> p t d", t=NT), ALU.add))

    return body




def l2_ffn(net):
    nc, w, ps = net.nc, net.w, net.ps
    E = M2_E
    C = E * M2_H // P

    def body(s, sb, block, need):
        lg = sb("lg", [P, NT, E])
        top = sb("top", [P, NT, 8])
        topi = sb("topi", [P, NT, 8], U32)
        topf = sb("topf", [P, NT, 8])
        sel = sb("sel", [P, 2, NT, E])
        g2 = sb("g2", [P, NT, 2])
        den = sb("den", [P, NT])
        rden = sb("rden", [P, NT])
        gate = sb("gate", [P, NT, E])
        gateT = sb("gateT", [E, T])
        h = sb("h", [P, C, T])
        hg = sb("hg", [P, C, T])

        @block.tensor
        def _(pe):
            need(pe)
            norm_tensor(net, s, pe, ps[0])
            pe.wait_ge(s["normT_ready"], 1)
            for t in range(NT):
                last = pe.matmul(ps[1][:, E * t:E * t + E], net.xnT[:, tile(t)], w("m2_wg"), start=True, stop=True)
            last.then_inc(s["logits_in_psum"], 1)
            for c in range(C):
                pe.matmul(ps[2 + c][:, :], w("m2_wd", c * P, (c + 1) * P), net.xnT[:, :], start=True, stop=True)\
                  .then_inc(s["hidden_in_psum"], 1)
            pe.wait_ge(s["gate_ready"], 1)
            for t in range(NT):
                last = pe.transpose(ps[6][0:E, tile(t)], gate[:, t, :], w("ident"))
            last.then_inc(s["gateT_in_psum"], 1)
            pe.wait_ge(s["gateT_ready"], 1)
            for c in range(C):
                pe.wait_ge(s["hidden_ready"], c + 1)
                pe.matmul(ps[2 + c][:, :], w("pairpick", c * P, (c + 1) * P), gateT[:, :], start=True, stop=True)\
                  .then_inc(s["spread_in_psum"], 1)
            pe.wait_ge(s["gated"], C)
            for t in range(NT):
                for c in range(C):
                    pe.matmul(ps[7][:, tile(t)], hg[:, c, tile(t)], w("m2_wu", c * D, (c + 1) * D), start=(c == 0), stop=False)
                last = pe.matmul(ps[7][:, tile(t)], gateT[:, tile(t)], w("m2_bu"), start=False, stop=True)
            last.then_inc(s["y_in_psum"], 1)

        @block.scalar
        def _(act):
            need(act)
            norm_scalar(net, s, act, ps[0])
            for c in range(C):
                act.wait_ge(s["hidden_in_psum"], c + 1)
                act.activation(h[:, c, :], ps[2 + c][:, :], ACT.Relu, bias=w("m2_bd", c, c + 1)).then_inc(s["hidden_ready"], 1)
            act.wait_ge(s["top_shifted"], 1)
            act.activation(g2[:, :, :], g2[:, :, :], ACT.Exp).then_inc(s["top_exp"], 1)
            act.wait_ge(s["gateT_in_psum"], 1)
            act.activation(gateT[:, :], ps[6][0:E, :], ACT.Copy).then_inc(s["gateT_ready"], 1)

        @block.gpsimd
        def _(g):
            need(g)
            norm_pool(net, s, g, Steps(g, s["pool_step"]))

        @block.vector
        def _(v):
            need(v)
            st = Steps(v, s["vector_step"])
            norm_vector(net, s, v, st)
            v.wait_ge(s["logits_in_psum"], 1)
            st.link(v.tensor_copy(lg[:, :, :], ps[1][:, 0:NT * E].rearrange("p (t e) -> p t e", t=NT)))
            top2_vector(net, s, v, st, lg, sel, top, topi, topf)
            v.tensor_tensor(g2[:, :, :], top[:, :, 0:2], bci(top[:, :, 0], 2), ALU.subtract).then_inc(s["top_shifted"], 1)
            v.wait_ge(s["top_exp"], 1)
            st.link(v.tensor_reduce(den[:, :], g2[:, :, :], AX.X, ALU.add))
            st.link(v.reciprocal(rden[:, :], den[:, :]))
            st.link(v.scalar_tensor_tensor(out=g2[:, :, :], in0=g2[:, :, :], scalar=0.5, in1=bci(rden[:, :], 2), op0=ALU.mult, op1=ALU.mult))
            for i in range(2):
                st.step(v.tensor_tensor(sel[:, i, :, :], sel[:, i, :, :], bci(g2[:, :, i], E), ALU.mult))
            st.wait()
            v.tensor_tensor(gate[:, :, :], sel[:, 0, :, :], sel[:, 1, :, :], ALU.add).then_inc(s["gate_ready"], 1)
            for c in range(C):
                v.wait_ge(s["spread_in_psum"], c + 1)
                v.tensor_tensor(hg[:, c, :], h[:, c, :], ps[2 + c][:, :], ALU.mult).then_inc(s["gated"], 1)
            v.wait_ge(s["y_in_psum"], 1)
            st.link(v.tensor_tensor(net.x[:, :, :], net.x[:, :, :], ps[7][:, :].rearrange("p (t d) -> p t d", t=NT), ALU.add))

    return body




def l3_attn(net):
    nc, w, ps = net.nc, net.w, net.ps
    C, NS, R = A3_C, A3_N, A3_R
    N = NS * C
    PAD = A3_K - 1

    def body(s, sb, block, need):
        hn = sb("hn", [P, NT, D])
        hT = sb("hT", [D, T])
        xp = sb("xp", [P, C, PAD + T])
        sg = sb("sg", [P, C, T])
        cv = sb("cv", [P, C, T])
        sgc = sb("sgc", [P, C, T])
        xs = sb("xs", [P, C, T])
        dbc = sb("dbc", [R + 2 * NS, T])
        z, e = cv, sgc
        ln = sb("ln", [P, C, T])
        one = sb("one", [P, C, T])
        d = sb("d", [P, C, T])
        dt = sb("dt", [P, C, T])
        dtx = xp[:, :, PAD:]
        bn = sb("bn", [P, 2, T])
        da = sb("da", [P, 3, T])
        u = sb("u", [P, 3, T])
        h = sb("h", [P, 2, T])
        hc = sb("hc", [P, 2, T])
        yT = ln

        @block.tensor
        def _(pe):
            need(pe)
            norm_tensor(net, s, pe, ps[0], src=hn, tag="inner_")
            pe.wait_ge(s["hT_ready"], 1)
            for c in range(2 * C):
                pe.matmul(ps[1 + c][:, :], w("a3_win", c * P, (c + 1) * P), hT[:, :], start=True, stop=True)\
                  .then_inc(s["proj_in_psum"], 1)
            for c in range(C):
                pe.wait_ge(s["xs_ready"], c + 1)
                last = pe.matmul(ps[5][0:R + 2 * NS, :], w("a3_wx", c * 96, (c + 1) * 96), xs[:, c, :],
                                 start=(c == 0), stop=(c == C - 1))
            last.then_inc(s["dbc_in_psum"], 1)
            pe.wait_ge(s["dbc_ready"], 1)
            for c in range(C):
                pe.matmul(ps[6 + c][:, :], w("a3_wdt", c * P, (c + 1) * P), dbc[0:R, :], start=True, stop=True)\
                  .then_inc(s["dt_in_psum"], 1)
            pe.wait_ge(s["sigmoids_ready"], C)
            for n in range(NS + 1):
                if n < NS:
                    if n >= 2:
                        pe.wait_ge(s["bn_ready"], n - 1)
                    pe.matmul(ps[n % 2][:, :], w("ident", R + n, R + n + 1)[0:96, :].to_broadcast([96, P]), dbc[:, :],
                              start=True, stop=True).then_inc(s["b_in_psum"], 1)
                    if n >= 2:
                        pe.wait_ge(s["hc_ready"], C * (n - 1))
                    pe.matmul(ps[2 + n % 2][:, :], w("ident", R + NS + n, R + NS + n + 1)[0:96, :].to_broadcast([96, P]), dbc[:, :],
                              start=True, stop=True).then_inc(s["c_in_psum"], 1)
                if n >= 1:
                    for c in range(C):
                        i = C * (n - 1) + c
                        pe.wait_ge(s["hc_ready"], i + 1)
                        pe.matmul(ps[4 + c][:, :], w("ident"), hc[:, i % 2, :], start=(n == 1), stop=(n == NS))\
                          .then_inc(s["state_added"], 1)
            pe.wait_ge(s["yT_ready"], C)
            for t in range(NT):
                for c in range(C):
                    last = pe.matmul(ps[0][:, tile(t)], yT[:, c, tile(t)], w("a3_wout", c * D, (c + 1) * D),
                                     start=(c == 0), stop=(c == C - 1))
            last.then_inc(s["y_in_psum"], 1)

        @block.scalar
        def _(act):
            need(act)
            st = Steps(act, s["scalar_step"])
            act.wait_ge(s["inner_normT_in_psum"], 1)
            act.activation(hT[:, :], ps[0][:, :], ACT.Identity, bias=w("a3_b"), scale=w("a3_g")).then_inc(s["hT_ready"], 1)
            for c in range(C):
                act.wait_ge(s["proj_in_psum"], c + 1)
                act.activation(xp[:, c, PAD:], ps[1 + c][:, :], ACT.Identity, bias=w("a3_bin", c, c + 1)).then_inc(s["xp_ready"], 1)
            for c in range(C):
                act.wait_ge(s["proj_in_psum"], C + c + 1)
                act.activation(sg[:, c, :], ps[3 + c][:, :], ACT.Sigmoid, bias=w("a3_bin", C + c, C + c + 1))\
                   .then_inc(s["sigmoids_ready"], 1)
            for c in range(C):
                act.wait_ge(s["conv_ready"], c + 1)
                act.activation(sgc[:, c, :], cv[:, c, :], ACT.Sigmoid).then_inc(s["conv_sigmoid"], 1)
            act.wait_ge(s["dbc_in_psum"], 1)
            act.activation(dbc[:, :], ps[5][0:R + 2 * NS, :], ACT.Copy).then_inc(s["dbc_ready"], 1)
            for c in range(C):
                act.wait_ge(s["dt_in_psum"], c + 1)
                st.link(act.activation(z[:, c, :], ps[6 + c][:, :], ACT.Identity, bias=w("a3_bdt", c, c + 1)))
                st.link(act.activation(e[:, c, :], z[:, c, :], ACT.Abs))
                st.link(act.activation(e[:, c, :], e[:, c, :], ACT.Exp, scale=-1.0))
                act.activation(ln[:, c, :], e[:, c, :], ACT.Ln, bias=1.0).then_inc(s["ln_ready"], 1)
            for i in range(N):
                n, c = divmod(i, C)
                if c == 0:
                    act.wait_ge(s["b_in_psum"], n + 1)
                    if n >= 2:
                        act.wait_ge(s["u_ready"], C * (n - 1))
                    act.activation(bn[:, n % 2, :], ps[n % 2][:, :], ACT.Copy).then_inc(s["bn_ready"], 1)
                if i == 0:
                    act.wait_ge(s["dt_ready"], C)
                if i >= 3:
                    act.wait_ge(s["scanned"], i - 2)
                act.activation(da[:, i % 3, :], dt[:, c, :], ACT.Exp, scale=net.a3[:, c, n:n + 1]).then_inc(s["da_ready"], 1)

        @block.gpsimd
        def _(g):
            need(g)
            st = Steps(g, s["pool_step"])
            g.memset(xp[:, :, 0:PAD], 0.0).then_inc(s["pad_ready"], 1)
            norm_pool(net, s, g, st)
            norm_pool(net, s, g, st, tag="inner_")
            g.wait_ge(s["dtx_ready"], C)
            for i in range(N):
                n, c = divmod(i, C)
                g.wait_ge(s["bn_ready"], n + 1)
                if i >= 3:
                    g.wait_ge(s["scanned"], i - 2)
                g.tensor_tensor(u[:, i % 3, :], dtx[:, c, :], bn[:, n % 2, :], ALU.mult).then_inc(s["u_ready"], 1)

        @block.vector
        def _(v):
            need(v)
            st = Steps(v, s["vector_step"])
            norm_vector(net, s, v, st)
            v.wait_ge(s["norm_ready"], 1)
            norm_vector(net, s, v, st, src=net.xn, dst=hn, tag="inner_")
            v.wait_ge(s["pad_ready"], 1)
            for c in range(C):
                v.wait_ge(s["xp_ready"], c + 1)
                k = A3_K * c
                st.link(v.tensor_scalar(cv[:, c, :], xp[:, c, 0:T], w("a3_cw", k, k + 1), w("a3_cb", c, c + 1), ALU.mult, ALU.add))
                for j in range(1, A3_K):
                    last = v.scalar_tensor_tensor(out=cv[:, c, :], in0=xp[:, c, j:j + T], scalar=w("a3_cw", k + j, k + j + 1),
                                                  in1=cv[:, c, :], op0=ALU.mult, op1=ALU.add)
                    if j < A3_K - 1:
                        st.link(last)
                    else:
                        last.then_inc(s["conv_ready"], 1)
            for c in range(C):
                v.wait_ge(s["conv_ready"], c + 1)
                v.wait_ge(s["conv_sigmoid"], c + 1)
                v.tensor_tensor(xs[:, c, :], cv[:, c, :], sgc[:, c, :], ALU.mult).then_inc(s["xs_ready"], 1)
            for c in range(C):
                v.wait_ge(s["ln_ready"], c + 1)
                st.link(v.tensor_scalar(d[:, c, :], e[:, c, :], 1.0, -1.0, ALU.add, ALU.add))
                st.link(v.tensor_scalar(one[:, c, :], d[:, c, :], 0.0, None, ALU.is_equal))
                st.step(v.tensor_tensor(d[:, c, :], d[:, c, :], one[:, c, :], ALU.add))
                st.link(v.tensor_tensor(ln[:, c, :], ln[:, c, :], one[:, c, :], ALU.add))
                st.step(v.reciprocal(one[:, c, :], d[:, c, :]))
                st.link(v.tensor_tensor(ln[:, c, :], ln[:, c, :], e[:, c, :], ALU.mult))
                st.link(v.tensor_tensor(ln[:, c, :], ln[:, c, :], one[:, c, :], ALU.mult))
                v.scalar_tensor_tensor(out=dt[:, c, :], in0=z[:, c, :], scalar=0.0, in1=ln[:, c, :], op0=ALU.max, op1=ALU.add)\
                 .then_inc(s["dt_ready"], 1)
                v.wait_ge(s["dt_ready"], c + 1)
                v.tensor_tensor(dtx[:, c, :], dt[:, c, :], xs[:, c, :], ALU.mult).then_inc(s["dtx_ready"], 1)
            for i in range(N):
                n, c = divmod(i, C)
                v.wait_ge(s["da_ready"], i + 1)
                v.wait_ge(s["u_ready"], i + 1)
                if i >= 2:
                    v.wait_ge(s["hc_ready"], i - 1)
                v.tensor_tensor_scan(h[:, i % 2, :], da[:, i % 3, :], u[:, i % 3, :], 0.0, ALU.mult, ALU.add).then_inc(s["scanned"], 1)
                v.wait_ge(s["scanned"], i + 1)
                v.wait_ge(s["c_in_psum"], n + 1)
                if i >= 2:
                    v.wait_ge(s["state_added"], i - 1)
                v.tensor_tensor(hc[:, i % 2, :], h[:, i % 2, :], ps[2 + n % 2][:, :], ALU.mult).then_inc(s["hc_ready"], 1)
            v.wait_ge(s["state_added"], N)
            for c in range(C):
                st.link(v.scalar_tensor_tensor(out=yT[:, c, :], in0=xs[:, c, :], scalar=w("a3_d", c, c + 1), in1=ps[4 + c][:, :],
                                               op0=ALU.mult, op1=ALU.add))
                v.tensor_tensor(yT[:, c, :], yT[:, c, :], sg[:, c, :], ALU.mult).then_inc(s["yT_ready"], 1)
            st.link(v.tensor_tensor(net.x[:, :, :], net.x[:, :, :], bc(w("a3_bout"), NT), ALU.add))
            st.link(v.tensor_tensor(net.x[:, :, :], net.x[:, :, :], net.xn[:, :, :], ALU.add))
            v.wait_ge(s["y_in_psum"], 1)
            st.link(v.tensor_tensor(net.x[:, :, :], net.x[:, :, :], ps[0][:, :].rearrange("p (t d) -> p t d", t=NT), ALU.add))

    return body




def l3_xattn(net):
    nc, w, ps = net.nc, net.w, net.ps
    H, M = X3_H, 2 * X3_H
    PER = 6
    BANKS = [(0, 6), (6, 12), (12, 16)]
    N = NT * 2
    scale = X3_SD ** -0.5

    def body(s, sb, block, need):
        qT = sb("qT", [D, T])
        kT = sb("kT", [D, S2])
        km = sb("km", [D, M, S2])
        vt = sb("vt", [S2, D])
        mx = sb("mx", [P, 2, H])
        sc = sb("sc", [P, 4, H, S2])
        den = sb("den", [P, 2, 2, H])
        rden = sb("rden", [P, 2, 2, H])
        co = sb("co", [P, 2, H])
        wT = sb("wT", [S2, 2, 4, P])
        o = sb("o", [P, NT, D])
        oT = sb("oT", [D, T])

        @block.tensor
        def _(pe):
            need(pe)
            pe.matmul(ps[6][:, 0:S2], w("x3_wk"), net.ctxT[:, :], start=True, stop=True).then_inc(s["k_in_psum"], 1)
            pe.matmul(ps[7][0:S2, 0:D], net.ctxT[:, :], w("x3_wv"), start=True, stop=True).then_inc(s["v_in_psum"], 1)
            norm_tensor(net, s, pe, ps[0])
            pe.wait_ge(s["normT_ready"], 1)
            pe.matmul(ps[1][:, :], w("x3_wq"), net.xnT[:, :], start=True, stop=True).then_inc(s["q_in_psum"], 1)
            pe.wait_ge(s["q_ready"], 1)
            pe.wait_ge(s["km_ready"], 1)
            pe.wait_ge(s["v_ready"], 1)

            def scores(i):
                t, half = divmod(i, 2)
                if i >= 2:
                    pe.wait_ge(s["shifted"], i - 1)
                for b, (lo, hi) in enumerate(BANKS):
                    last = pe.matmul(ps[3 * half + b][:, 0:(hi - lo) * S2], qT[:, tile(t)],
                                     km[:, half * H + lo:half * H + hi, :].rearrange("p m k -> p (m k)"), start=True, stop=True)
                last.then_inc(s["scores_in_psum"], 1)

            def apply(t):
                pe.wait_ge(s["weights_ready"], t + 1)
                for g in range(H // 4 + 1):
                    n = 4 * t + g
                    if g < H // 4:
                        if n >= 1:
                            pe.wait_ge(s["wT_ready"], n)
                        for k in range(4):
                            last = pe.transpose(ps[6][0:S2, tile(k)], sc[:, 2 * (t % 2), 4 * g + k, :], w("ident"))
                        last.then_inc(s["wT_in_psum"], 1)
                    if g >= 1:
                        n -= 1
                        pe.wait_ge(s["wT_ready"], n + 1)
                        if g == 1 and t >= 1:
                            pe.wait_ge(s["o_ready"], t)
                        for k in range(4):
                            h = 4 * (g - 1) + k
                            last = pe.matmul(ps[7][:, 8 * h:8 * h + 8], wT[:, n % 2, k, :], vt[:, 8 * h:8 * h + 8], start=True, stop=True)
                        last.then_inc(s["heads_done"], 1)

            for t in range(NT + 1):
                if t < NT:
                    scores(2 * t)
                    scores(2 * t + 1)
                if t >= 1:
                    apply(t - 1)
            pe.wait_ge(s["o_ready"], NT)
            transpose_tensor(net, s, pe, o, ps[0], "oT_in_psum")
            pe.wait_ge(s["oT_ready"], 1)
            for t in range(NT):
                last = pe.matmul(ps[1][:, tile(t)], oT[:, tile(t)], w("x3_wo"), start=True, stop=True)
            last.then_inc(s["y_in_psum"], 1)

        @block.scalar
        def _(act):
            need(act)
            act.wait_ge(s["k_in_psum"], 1)
            act.activation(kT[:, :], ps[6][:, 0:S2], ACT.Identity, bias=w("x3_bk")).then_inc(s["k_ready"], 1)
            norm_scalar(net, s, act, ps[0])
            act.wait_ge(s["q_in_psum"], 1)
            act.activation(qT[:, :], ps[1][:, :], ACT.Identity, bias=w("x3_bq")).then_inc(s["q_ready"], 1)
            for t in range(NT + 1):
                if t < NT:
                    for half in range(2):
                        i = 2 * t + half
                        act.wait_ge(s["shifted"], i + 1)
                        act.activation(sc[:, i % 4, :, :], sc[:, i % 4, :, :], ACT.Exp, scale=scale).then_inc(s["exp_ready"], 1)
                if t >= 1:
                    for n in range(4 * (t - 1), 4 * t):
                        act.wait_ge(s["wT_in_psum"], n + 1)
                        if n >= 2:
                            act.wait_ge(s["heads_done"], n - 1)
                        act.activation(wT[:, n % 2, :, :], ps[6][0:S2, :].rearrange("p (h t) -> p h t", h=4), ACT.Copy)\
                           .then_inc(s["wT_ready"], 1)
            act.wait_ge(s["oT_in_psum"], 1)
            act.activation(oT[:, :], ps[0][:, :], ACT.Copy).then_inc(s["oT_ready"], 1)

        @block.gpsimd
        def _(g):
            need(g)
            norm_pool(net, s, g, Steps(g, s["pool_step"]))

        @block.vector
        def _(v):
            need(v)
            st = Steps(v, s["vector_step"])
            norm_vector(net, s, v, st)
            v.wait_ge(s["v_in_psum"], 1)
            v.tensor_tensor(vt[:, :], ps[7][0:S2, 0:D], w("x3_bv")[0:S2, :], ALU.add).then_inc(s["v_ready"], 1)
            v.wait_ge(s["k_ready"], 1)
            v.tensor_tensor(km[:, :, :], bc(kT[:, :], M), bci(w("submap"), S2), ALU.mult).then_inc(s["km_ready"], 1)

            def soften(i):
                half = i % 2
                v.wait_ge(s["scores_in_psum"], i + 1)
                for b, (lo, hi) in enumerate(BANKS):
                    st.step(v.tensor_reduce(mx[:, half, lo:hi], ps[3 * half + b][:, 0:(hi - lo) * S2].rearrange("p (m k) -> p m k", k=S2),
                                            AX.X, ALU.max))
                st.wait()
                if i >= 4:
                    v.wait_ge(s["wT_in_psum"], 4 * (i // 2 - 1))
                for b, (lo, hi) in enumerate(BANKS):
                    last = v.tensor_tensor(sc[:, i % 4, lo:hi, :], ps[3 * half + b][:, 0:(hi - lo) * S2].rearrange("p (m k) -> p m k", k=S2),
                                           bci(mx[:, half, lo:hi], S2), ALU.subtract)
                last.then_inc(s["shifted"], 1)

            def weigh(t):
                b = t % 2
                for half in range(2):
                    v.wait_ge(s["exp_ready"], 2 * t + half + 1)
                    st.step(v.tensor_reduce(den[:, b, half, :], sc[:, 2 * b + half, :, :], AX.X, ALU.add))
                st.wait()
                st.link(v.reciprocal(rden[:, b, :, :], den[:, b, :, :]))
                st.link(v.scalar_tensor_tensor(out=co[:, b, :], in0=den[:, b, 0, :], scalar=net.neglam[:, 0:1], in1=rden[:, b, 1, :],
                                               op0=ALU.mult, op1=ALU.mult))
                st.link(v.tensor_tensor(sc[:, 2 * b + 1, :, :], sc[:, 2 * b + 1, :, :], bci(co[:, b, :], S2), ALU.mult))
                v.tensor_tensor(sc[:, 2 * b, :, :], sc[:, 2 * b, :, :], sc[:, 2 * b + 1, :, :], ALU.add).then_inc(s["weights_ready"], 1)

            def finish(t):
                v.wait_ge(s["heads_done"], 4 * (t + 1))
                v.scalar_tensor_tensor(out=o[:, t, :].rearrange("p (h d) -> p h d", h=H), in0=ps[7][:, 0:D].rearrange("p (h d) -> p h d", h=H),
                                       scalar=0.8, in1=bci(rden[:, t % 2, 0, :], 8), op0=ALU.mult, op1=ALU.mult)\
                 .then_inc(s["o_ready"], 1)

            for t in range(NT):
                soften(2 * t)
                soften(2 * t + 1)
                if t >= 1:
                    finish(t - 1)
                weigh(t)
            finish(NT - 1)
            st.link(v.tensor_tensor(net.x[:, :, :], net.x[:, :, :], bc(w("x3_bo"), NT), ALU.add))
            v.wait_ge(s["y_in_psum"], 1)
            st.link(v.tensor_tensor(net.x[:, :, :], net.x[:, :, :], ps[1][:, :].rearrange("p (t d) -> p t d", t=NT), ALU.add))

    return body



ROUND = 1.5 * 2.0 ** 23


def quantise(net, v, st, x, n, work, out, mx, back, inv, signal):
    st.link(v.tensor_reduce(mx, x, AX.X, ALU.max, apply_absolute_value=True))
    st.link(v.tensor_scalar(mx, mx, 1e-5, None, ALU.max))
    st.step(v.tensor_scalar(back, mx, 1.0 / 127.0, None, ALU.mult))
    st.link(v.reciprocal(inv, mx))
    st.link(v.tensor_scalar(inv, inv, 127.0, None, ALU.mult))
    st.link(v.tensor_scalar(work, x, inv, ROUND, ALU.mult, ALU.add))
    st.link(v.tensor_scalar(work, work, -ROUND, 127.0, ALU.add, ALU.min))
    v.tensor_scalar(out, work, -128.0, None, ALU.max).then_inc(signal, 1)


def l3_ffn(net):
    nc, w, ps = net.nc, net.w, net.ps
    C = F3_IN // P

    def body(s, sb, block, need):
        work = sb("work", [P, 2, F3_IN])
        xq = sb("xq", [P, NT, D], BF16)
        xqT = sb("xqT", [D, T], BF16)
        mx = sb("mx", [P, NT])
        inv = sb("inv", [P, NT])
        back = sb("back", [P, NT])
        fg = sb("fg", [P, NT])
        fu = sb("fu", [P, NT])
        mx2 = sb("mx2", [P, NT])
        inv2 = sb("inv2", [P, NT])
        back2 = sb("back2", [P, NT])
        fd = sb("fd", [P, NT])
        g = sb("g", [P, 2, F3_IN])
        p = sb("p", [P, 2, F3_IN])
        pq = sb("pq", [P, 2, F3_IN], BF16)
        pT = sb("pT", [P, 2, F3_IN], BF16)

        @block.tensor
        def _(pe):
            need(pe)
            pe.wait_ge(s["x_quantised"], NT)
            bank = ps[0][:, :].bitcast(BF16)
            for t in range(NT):
                last = pe.transpose(bank[:, tile(t)], xq[:, t, :], net.ident16[:, :])
            last.then_inc(s["xqT_in_psum"], 1)
            pe.wait_ge(s["xqT_ready"], 1)

            def up(t):
                if t >= 2:
                    pe.wait_ge(s["products_ready"], t - 1)
                pe.matmul(ps[1 + 2 * (t % 2)][:, :], xqT[:, tile(t)], net.q3[:, 0, :], start=True, stop=True)\
                  .then_inc(s["gate_in_psum"], 1)
                pe.matmul(ps[2 + 2 * (t % 2)][:, :], xqT[:, tile(t)], net.q3[:, 1, :], start=True, stop=True)\
                  .then_inc(s["up_in_psum"], 1)

            def down(t):
                pe.wait_ge(s["p_quantised"], t + 1)
                b = ps[5 + t % 2][:, :].bitcast(BF16)
                if t >= 2:
                    pe.wait_ge(s["pT_ready"], t - 1)
                for c in range(C):
                    last = pe.transpose(b[:, tile(c)], pq[:, t % 2, tile(c)], net.ident16[:, :])
                last.then_inc(s["pT_in_psum"], 1)
                pe.wait_ge(s["pT_ready"], t + 1)
                for c in range(C):
                    last = pe.matmul(ps[7][:, tile(t)], pT[:, t % 2, tile(c)], net.q3[:, 2, tile(c)], start=(c == 0), stop=(c == C - 1))
                last.then_inc(s["y_in_psum"], 1)

            up(0)
            for t in range(NT):
                if t + 1 < NT:
                    up(t + 1)
                down(t)

        @block.scalar
        def _(act):
            need(act)
            act.wait_ge(s["xqT_in_psum"], 1)
            act.activation(xqT[:, :], ps[0][:, :].bitcast(BF16)[:, 0:T], ACT.Copy).then_inc(s["xqT_ready"], 1)
            act.wait_ge(s["factors_ready"], 1)

            def gate(t):
                act.wait_ge(s["gate_in_psum"], t + 1)
                if t >= 2:
                    act.wait_ge(s["products_ready"], t - 1)
                act.activation(g[:, t % 2, :], ps[1 + 2 * (t % 2)][:, :], ACT.Silu, scale=fg[:, t:t + 1]).then_inc(s["gate_ready"], 1)

            gate(0)
            for t in range(NT):
                if t + 1 < NT:
                    gate(t + 1)
                act.wait_ge(s["pT_in_psum"], t + 1)
                if t >= 2:
                    act.wait_ge(s["y_in_psum"], t - 1)
                act.activation(pT[:, t % 2, :], ps[5 + t % 2][:, :].bitcast(BF16)[:, 0:F3_IN], ACT.Copy).then_inc(s["pT_ready"], 1)

        @block.gpsimd
        def _(gp):
            need(gp)
            norm_pool(net, s, gp, Steps(gp, s["pool_step"]))

        @block.vector
        def _(v):
            need(v)
            st = Steps(v, s["vector_step"])
            norm_vector(net, s, v, st)
            v.wait_ge(s["norm_ready"], 1)
            for t in range(NT):
                if t >= 2:
                    v.wait_ge(s["x_quantised"], t - 1)
                quantise(net, v, st, net.xn[:, t, :], D, work[:, t % 2, 0:D], xq[:, t, :], mx[:, t:t + 1], back[:, t:t + 1],
                         inv[:, t:t + 1], s["x_quantised"])
            st.step(v.tensor_scalar(fg[:, :], back[:, :], net.mean3[:, 0:1], None, ALU.mult))
            v.tensor_scalar(fu[:, :], back[:, :], net.mean3[:, 1:2], None, ALU.mult).then_inc(s["factors_ready"], 1)
            v.wait_ge(s["factors_ready"], 1)
            v.wait_ge(s["x_quantised"], NT)
            for t in range(NT):
                v.wait_ge(s["up_in_psum"], t + 1)
                v.wait_ge(s["gate_ready"], t + 1)
                if t >= 2:
                    v.wait_ge(s["p_quantised"], t - 1)
                v.scalar_tensor_tensor(out=p[:, t % 2, :], in0=ps[2 + 2 * (t % 2)][:, :], scalar=fu[:, t:t + 1], in1=g[:, t % 2, :],
                                       op0=ALU.mult, op1=ALU.mult).then_inc(s["products_ready"], 1)
                v.wait_ge(s["products_ready"], t + 1)
                if t >= 2:
                    v.wait_ge(s["pT_in_psum"], t - 1)
                quantise(net, v, st, p[:, t % 2, :], F3_IN, work[:, t % 2, :], pq[:, t % 2, :], mx2[:, t:t + 1], back2[:, t:t + 1],
                         inv2[:, t:t + 1], s["p_quantised"])
            st.link(v.tensor_scalar(fd[:, :], back2[:, :], net.mean3[:, 2:3], None, ALU.mult))
            v.wait_ge(s["y_in_psum"], NT)
            for t in range(NT):
                st.step(v.scalar_tensor_tensor(out=net.x[:, t, :], in0=ps[7][:, tile(t)], scalar=fd[:, t:t + 1], in1=net.x[:, t, :],
                                               op0=ALU.mult, op1=ALU.add))
            st.wait()

    return body




def setup_tables(net, ctx):
    net.y = net.sb("y", [P, NT, D])
    net.mask2 = net.sb("mask2", [P, A2_J, A2_C])
    net.wck = net.sb("wck", [P, NT, A2_NB])
    net.wcv = net.sb("wcv", [P, NT, A2_NB])
    net.a3 = net.sb("a3", [P, A3_C, A3_N])
    net.neglam = net.sb("neglam", [P, 1])
    net.mean3 = net.sb("mean3", [P, 3])
    net.q3 = net.sb("q3", [P, 3, F3_IN], BF16)
    net.ident16 = net.sb("ident16", [P, P], BF16)
    net.pick16 = net.sb("pick16", [P, 4], BF16)
    net.rot = net.sb("rot", [P, F0_L, 2, 2, NT, F0_HD])


def prepare(net, load, need):
    nc, w = net.nc, net.w

    def body(s, sb, block, _):
        la = sb("la", [P, 8])
        lsum = sb("lsum", [P, 2])
        lexp = sb("lexp", [P, 2])
        absum = sb("absum", [P, 3])
        inv = sb("inv", [P, 3])
        work = sb("work", [P, F3_IN])
        F3 = ("f3_wg", "f3_wu", "f3_wd")

        @block.sync
        def _(sp):
            load(sp)

        @block.tensor
        def _(pe):
            need("base")(pe)
            pe.wait_ge(s["absum_ready"], 1)
            pe.matmul(net.ps[0][:, 0:3], w("ones"), absum[:, :], start=True, stop=True).then_inc(s["total_in_psum"], 1)

        @block.scalar
        def _(act):
            st = Steps(act, s["scalar_step"])
            need("base")(act)
            need("tables")(act)
            st.step(act.activation(net.ident16[:, :], w("ident"), ACT.Copy))
            st.step(act.activation(net.pick16[:, :], w("pick"), ACT.Copy))
            st.link(act.activation(net.a3[:, :, :], w("a3_alog").rearrange("p (c n) -> p c n", c=A3_C), ACT.Exp))
            st.link(act.activation(net.a3[:, :, :], net.a3[:, :, :], ACT.Copy, scale=-1.0))
            act.wait_ge(s["lambda_sums"], 1)
            act.activation(lexp[:, :], lsum[:, :], ACT.Exp).then_inc(s["lambda_exp"], 1)
            st.wait()

        @block.vector
        def _(v):
            need("tables")(v)
            st = Steps(v, s["vector_step"])
            half = F0_HD // 2
            for l in range(F0_L):
                for j, (c, n, gain) in enumerate((("rot_q", "rot_qs", f"f0_qs{l}"), ("rot_k", "rot_ks", f"f0_ks{l}"))):
                    co = w(c).rearrange("p (t d) -> p t d", t=NT)
                    si = w(n).rearrange("p (t d) -> p t d", t=NT)
                    st.step(v.tensor_tensor(net.rot[:, l, j, 0], co, bc(w(gain), NT), ALU.mult))
                    st.step(v.tensor_tensor(net.rot[:, l, j, 1, :, 0:half], si[:, :, 0:half], bc(w(gain, half, F0_HD), NT), ALU.mult))
                    st.step(v.tensor_tensor(net.rot[:, l, j, 1, :, half:F0_HD], si[:, :, half:F0_HD], bc(w(gain, 0, half), NT), ALU.mult))
            st.step(v.tensor_copy(net.mask2[:, 0, 0:64], w("win_mask", 0, 64)))
            st.step(v.tensor_copy(net.mask2[:, 1:A2_J, 0:64], bc(w("win_mask", 64, 128), A2_J - 1)))
            st.step(v.tensor_copy(net.mask2[:, :, 64:64 + A2_NB], w("comp_mask").rearrange("p (j n) -> p j n", j=A2_J)))
            for dst, src in ((net.wck, "a2_wkt"), (net.wcv, "a2_wvt")):
                st.step(v.tensor_scalar(dst[:, :, :], w("block_of").rearrange("p (t n) -> p t n", t=NT), w(src), None, ALU.mult))
            st.link(v.tensor_tensor(la[:, :], w("x3_l", 0, 8), w("x3_l", 8, 16), ALU.mult))
            v.tensor_reduce(lsum[:, :], la[:, :].rearrange("p (a b) -> p a b", a=2), AX.X, ALU.add).then_inc(s["lambda_sums"], 1)
            v.wait_ge(s["lambda_exp"], 1)
            st.link(v.tensor_tensor(net.neglam[:, :], lexp[:, 1:2], lexp[:, 0:1], ALU.subtract))
            st.step(v.tensor_scalar(net.neglam[:, :], net.neglam[:, :], -0.2, None, ALU.add))
            for i, k in enumerate(F3):
                last = v.tensor_reduce(absum[:, i:i + 1], w(k), AX.X, ALU.add, apply_absolute_value=True)
            last.then_inc(s["absum_ready"], 1)
            v.wait_ge(s["total_in_psum"], 1)
            st.link(v.tensor_scalar(net.mean3[:, :], net.ps[0][:, 0:3], 1.0 / (D * F3_IN), 1e-5, ALU.mult, ALU.max))
            st.link(v.reciprocal(inv[:, :], net.mean3[:, :]))
            for i, k in enumerate(F3):
                st.link(v.tensor_scalar(work[:, :], w(k), inv[:, i:i + 1], ROUND, ALU.mult, ALU.add))
                st.link(v.tensor_scalar(work[:, :], work[:, :], -ROUND, 1.0, ALU.add, ALU.min))
                st.link(v.tensor_scalar(net.q3[:, i, :], work[:, :], -1.0, None, ALU.max))
            st.wait()

    run_stage(nc, "prepare", body, None, final=True)




def stage_list(net):
    return [
        ("l0_attn", l0_attn),
        ("l0_xattn", lambda n: xattn(n, "x0_wq", "x0_wk", "x0_wv", scale=D ** -0.5)),
        ("l0_ffn", l0_ffn),
        ("l1_attn", l1_attn),
        ("l1_xattn", lambda n: xattn(n, "x1_wq", "x1_wk", "x1_wv", "x1_bq", "x1_bv", "x1_wo", "x1_bo", scale=D ** -0.5)),
        ("l1_ffn", l1_ffn),
        ("l2_attn", l2_attn),
        ("l2_xattn", lambda n: xattn(n, "x2_w", "x2_w", bq="x2_b", relu=True, kd="x2_d", masked=True)),
        ("l2_ffn", l2_ffn),
        ("l3_attn", l3_attn),
        ("l3_xattn", l3_xattn),
        ("l3_ffn", l3_ffn),
    ]


def build(nc, x_in, ctx_in, ctxT_in, mask_in, packed, out, where, pieces, only=None, rows_run=B):
    with ExitStack() as ctx:
        net = Net(nc, ctx, where)
        loaded = {k: ctx.enter_context(nc.semaphore(f"{k}_weights_loaded")) for k in pieces}
        setup_tables(net, ctx)

        with ExitStack() as early:
            net.tables = early.enter_context(nc.sbuf_tensor("table_operands", [P, net.split], F32))

            def load(sp):
                for k, (lo, hi) in pieces.items():
                    to = net.tables[:, lo:hi] if k == "tables" else net.W[:, lo - net.split:hi - net.split]
                    sp.dma_start(to, packed[:, lo:hi]).then_inc(loaded[k], 16)

            def need(*names):
                def wait(eng):
                    for k in names:
                        eng.wait_ge(loaded[k], 16)
                return wait

            prepare(net, load, need)

        with nc.Fori(0, rows_run) as row:
            def enter(s, sb, block, _):
                m8 = sb("m8", [P, S2], mybir.dt.uint8)

                @block.sync
                def _(sp):
                    sp.dma_start(net.x[:, :, :], x_in[bass.ds(row, 1)].rearrange("b (t p) d -> (b p) t d", p=P)).then_inc(s["row_loaded"], 16)
                    sp.dma_start(net.ctxT[:, :], ctxT_in[bass.ds(row, 1)].rearrange("b d k -> (b d) k")).then_inc(s["row_loaded"], 16)
                    sp.dma_start(net.ctxtok[:, :], ctx_in[bass.ds(row, 1)].rearrange("b k d -> (b k) d")).then_inc(s["row_loaded"], 16)
                    sp.dma_start(m8[:, :], mask_in[bass.ds(row, 1)].to_broadcast([P, S2])).then_inc(s["mask_loaded"], 16)
                    sp.wait_ge(s["row_loaded"], 48)

                @block.vector
                def _(v):
                    v.wait_ge(s["mask_loaded"], 16)
                    v.tensor_copy(net.bias[:, :], m8[:, :]).then_inc(s["mask_ready"], 1)
                    v.wait_ge(s["mask_ready"], 1)

            sems = run_stage(nc, "enter", enter, None)
            for k, make in stage_list(net):
                if only is None or k in only:
                    bodies = make(net)
                    for i, body in enumerate(bodies if isinstance(bodies, list) else [bodies]):
                        sems = run_stage(nc, f"{k}{i}", body, need("base", *([k] if k in pieces else [])), before=sems)

            def leave(s, sb, block, _):
                @block.sync
                def _(sp):
                    sp.dma_start(out[bass.ds(row, 1)].rearrange("b (t p) d -> (b p) t d", p=P), net.x[:, :, :]).then_inc(s["row_stored"], 16)
                    sp.wait_ge(s["row_stored"], 16)

            run_stage(nc, "leave", leave, None, before=sems, final=True)


def kernel(**inputs):
    import concourse.bacc as bacc
    from concourse.bass_utils import run_bass_kernel_spmd as run

    a = {k: np.asarray(v) for k, v in inputs.items()}
    packed, where, pieces = pack(a)
    arrays = {
        "x_rows": np.ascontiguousarray(a["x"]),
        "context": np.ascontiguousarray(a["ctx_1024"]),
        "contextT": np.ascontiguousarray(a["ctx_1024"].transpose(0, 2, 1)),
        "mask": np.ascontiguousarray(a["mask_BxS2_bf0"]),
        "packed": packed,
    }
    nc = bacc.Bacc("TRN2", target_bir_lowering=False, num_devices=1)
    args = [nc.dram_tensor(k, v.shape, mybir.dt.from_np(v.dtype), kind="ExternalInput").ap() for k, v in arrays.items()]
    out = nc.dram_tensor("out", (B, T, D), F32, kind="ExternalOutput").ap()
    build(nc, *args, out, where, pieces)
    r = run(nc, [arrays], core_ids=[0])
    return r.results[0]["out"]
```

```python
from contextlib import ExitStack

import numpy as np

import concourse.bass as bass
from concourse import mybir

F32 = mybir.dt.float32
BF16 = mybir.dt.bfloat16
U32 = mybir.dt.uint32
ALU = mybir.AluOpType
ACT = mybir.ActivationFunctionType
AX = mybir.AxisListType

P = 128
B = 4
T = 512
D = 128
NT = T // P
S2 = 77
NEG = -1.0e30
LN_EPS = 1e-5

A0_H, A0_HD, A0_U = 16, 8, 31
F0_H, F0_HD, F0_WIN, F0_L = 8, 64, 64, 2
F0_IN = F0_H * F0_HD
F0_HID = 341
F0_CH = [(0, 128), (128, 128), (256, 85)]
A1_H, A1_HD = 16, 8
M1_E, M1_H = 8, 256
A2_H, A2_HD, A2_CB, A2_SB, A2_TOP, A2_WIN = 16, 8, 16, 8, 2, 32
A2_NB = T // A2_CB
A2_M = A2_SB * A2_TOP
M2_E, M2_H = 8, 64
A3_E, A3_N, A3_R, A3_K = 256, 16, 64, 4
A3_C = A3_E // P
X3_H, X3_SD = 16, 4
F3_IN = 512



def rotary_tables():
    half = np.arange(0, F0_HD, 2, dtype=np.float32)
    inv = (np.float32(1.0) / np.float32(10000.0) ** (half / np.float32(F0_HD))).astype(np.float32)
    t = np.arange(T, dtype=np.float32)
    f = t[:, None] * inv[None, :]
    f = np.concatenate([f, f], -1)
    base = (half + np.float32(0.4 * F0_HD)) / np.float32(1.4 * F0_HD)
    power = (t - T // 2) / np.float32(F0_WIN // 2)
    s = (base[None, :] ** power[:, None]).astype(np.float32)
    s = np.concatenate([s, s], -1)
    sign = np.where(np.arange(F0_HD) < F0_HD // 2, -1.0, 1.0).astype(np.float32)
    c, n = np.cos(f), np.sin(f) * sign
    return [c * s, n * s, c / s, n / s]


def rope_tables():
    i = np.arange(A2_HD // 2, dtype=np.float32)
    inv = (np.float32(1.0) / np.float32(10000.0) ** (i * np.float32(2.0) / np.float32(A2_HD))).astype(np.float32)
    a = np.arange(T, dtype=np.float32)[:, None] * inv[None, :]
    f = np.arange(D)
    pair = (f % A2_HD) // 2
    c, s = np.cos(a)[:, pair].T, np.sin(a)[:, pair].T
    return c, s * np.where(f % 2 == 0, -1.0, 1.0)[:, None]


def tokens(a):
    return a.reshape(NT, P, -1).transpose(1, 0, 2).reshape(P, -1)


def constants():
    p, f = np.arange(P), np.arange(D)
    c = {}
    c["ident"] = np.eye(P)
    c["iota"] = np.broadcast_to(np.arange(T), (P, T))
    c["tokid"] = p[:, None] + P * np.arange(NT)[None, :]
    c["neghalf"] = np.full((P, 32), -0.5)
    c["ones"] = np.ones((P, P))
    c["headsum"] = (f[:, None] // 8 == np.arange(16)[None, :])
    c["headmask"] = np.repeat(f[:, None] // 8 == np.arange(16)[None, :], 32, 1)
    c["quadmask"] = np.repeat(f[:, None] // 8 % 4 == np.arange(4)[None, :], 32, 1)
    c["rowmask"] = (4 * np.arange(4)[None, :, None] + p[:, None, None] // 32 == f[None, None, :] // 8).reshape(P, -1)
    h16 = np.zeros((P, 512))
    h16[:16] = np.repeat(np.eye(16), 32, 1)
    c["diag16"] = h16
    m = np.zeros((P, T))
    m[:, 384:] = np.where(p[None, :] <= p[:, None], 0.0, NEG)
    c["causal"] = m
    c["causalT"] = (p[:, None] <= f[None, :])
    c["quarter"] = (p[:, None] // 32 == np.arange(4)[None, :])
    i = p % 32 // 8
    c["terms"] = -1.0 * np.stack([i == 2, i >= 1, i == 1, i == 1, (i == 0) | (i == 2), i == 0], 1)
    c["halves"] = (p[:, None] // 64 == np.arange(2)[None, :])
    c["parts"] = -1.0 * np.stack([p >= 32, p >= 64], 1)
    c["part_of"] = (p[:, None] % 32 == np.arange(32)[None, :]) & (p[:, None] < 96)
    c["pick"] = (p[:, None] % 4 == np.arange(4)[None, :]) & (p[:, None] < 8)
    shift = np.zeros((P, P)); shift[p[:-1], p[1:]] = 1.0
    carry = np.zeros((P, P)); carry[P - 1, 0] = 1.0
    c["shift"], c["carry"] = shift, carry
    j = np.arange(192)
    ok = (j[None, :] - 64 <= p[:, None]) & (j[None, :] >= p[:, None])
    band = np.where(ok, 0.0, NEG)
    c["band"] = band
    c["iota8"] = np.broadcast_to(np.tile(np.arange(8), NT), (P, 8 * NT))
    c["pairpick"] = np.kron(np.eye(8), np.ones((1, 64)))
    c["fourfold"] = np.tile(np.eye(32), (1, 4))
    c["rot_q"], c["rot_qs"], c["rot_k"], c["rot_ks"] = [tokens(a) for a in rotary_tables()]
    c["rope_c"], c["rope_s"] = rope_tables()
    q = p % 32
    n = np.arange(A2_NB)
    comp = [np.where((n[None, :] + 1) * A2_CB <= 32 * k + q[:, None], 0.0, NEG) for k in range(T // 32)]
    c["comp_mask"] = np.concatenate(comp, 1)
    kk = np.arange(64) - 32
    win = (kk[None, :] <= q[:, None]) & (kk[None, :] > q[:, None] - A2_WIN)
    c["win_mask"] = np.concatenate([np.where(win & (kk[None, :] >= 0), 0.0, NEG), np.where(win, 0.0, NEG)], 1)
    tok = p[:, None] + P * np.arange(NT)[None, :]
    c["block_of"] = (tok[:, :, None] // A2_CB == n[None, None, :]).reshape(P, -1)
    c["query_id"] = q[:, None] + 32 * np.arange(T // 32)[None, :]
    m = np.arange(32)
    c["submap"] = (f[:, None] // 4 == (2 * (m % 16) + m // 16)[None, :])
    return {k: np.ascontiguousarray(v, np.float32) for k, v in c.items()}


def blockdiag(w):
    out = np.zeros((D, D), w.dtype)
    for h in range(w.shape[0]):
        out[8 * h:8 * h + 8, 8 * h:8 * h + 8] = w[h]
    return out


def padded_heads(w):
    out = np.zeros((4, 32, 4, w.shape[1]), w.dtype)
    out[:, :8] = w.reshape(4, 4, 8, -1).transpose(1, 2, 0, 3)
    return out.reshape(P, -1)


def three_times(w):
    out = np.zeros((w.shape[0], w.shape[1] // 8, 32), w.dtype)
    out[:, :, :24] = np.tile(w.reshape(w.shape[0], -1, 8), (1, 1, 3))
    return out.reshape(w.shape[0], -1)


def rows(v):
    return np.broadcast_to(np.asarray(v).reshape(1, -1), (P, np.asarray(v).size))


def column(v):
    v = np.asarray(v)
    n = -(-v.size // P)
    out = np.zeros((n * P,), v.dtype)
    out[:v.size] = v
    return out.reshape(n, P).T


def chunks(w):
    n = -(-w.shape[0] // P)
    out = np.zeros((n * P, w.shape[1]), w.dtype)
    out[:w.shape[0]] = w
    return out.reshape(n, P, -1).transpose(1, 0, 2).reshape(P, -1)


def segments(a):
    c = constants()
    seg = {}
    seg["tables"] = [(k, c[k]) for k in ("rot_q", "rot_qs", "rot_k", "rot_ks", "comp_mask", "win_mask", "block_of")] + [
        ("f3_wg", a["L3_ffn_w_gate"].T), ("f3_wu", a["L3_ffn_w_up"].T), ("f3_wd", chunks(a["L3_ffn_w_down"].T)),
        ("a2_wkt", np.tile(a["L2_attn_wk_comp"], P // A2_CB)[:, None]),
        ("a2_wvt", np.tile(a["L2_attn_wv_comp"], P // A2_CB)[:, None]),
        ("a3_alog", chunks(a["L3_attn_A_log"])),
        ("x3_l", rows(np.concatenate([a["L3_xattn_lambda_q1"], a["L3_xattn_lambda_q2"],
                                      a["L3_xattn_lambda_k1"], a["L3_xattn_lambda_k2"]])))]
    for l in range(F0_L):
        seg["tables"] += [(f"f0_qs{l}", rows(a["L0_ffn_q_scale"][l])), (f"f0_ks{l}", rows(a["L0_ffn_k_scale"][l]))]
    seg["base"] = [(k, c[k]) for k in ("ident", "iota", "tokid", "neghalf", "ones", "headsum", "pick", "part_of")]
    seg["l0_attn"] = [(k, c[k]) for k in ("headmask", "rowmask", "diag16")] + [
        ("a0_wq", a["L0_attn_Wq"]), ("a0_wk", a["L0_attn_Wk"]), ("a0_wv", a["L0_attn_Wv"]), ("a0_wo", a["L0_attn_Wo"]),
        ("a0_bq", column(a["L0_attn_bq"])), ("a0_bk", column(a["L0_attn_bk"])),
        ("a0_bv", rows(a["L0_attn_bv"])), ("a0_bo", rows(a["L0_attn_bo"]))]
    seg["l0_xattn"] = [("x0_wq", a["L0_xattn_Q_W"].T), ("x0_wk", a["L0_xattn_K_W"].T), ("x0_wv", a["L0_xattn_V_W"].T)]
    f0 = [(k, c[k]) for k in ("shift", "carry", "band", "halves")]
    for l in range(F0_L):
        f0 += [(f"f0_wqkv{l}", a["L0_ffn_wqkv"][l]),
               (f"f0_wo{l}", chunks(a["L0_ffn_wo"][l])),
               (f"f0_g{l}", column(a["L0_ffn_ln_g"][l])), (f"f0_b{l}", column(a["L0_ffn_ln_b"][l])),
               (f"f0_w1{l}", a["L0_ffn_w1"][l]),
               (f"f0_b1a{l}", column(a["L0_ffn_b1"][l][:F0_HID])), (f"f0_b1g{l}", column(a["L0_ffn_b1"][l][F0_HID:])),
               (f"f0_w2{l}", chunks(a["L0_ffn_w2"][l])), (f"f0_b2{l}", rows(a["L0_ffn_b2"][l]))]
    seg["l0_ffn"] = f0
    seg["l1_attn"] = [(k, c[k]) for k in ("causal", "causalT")] + [
                      ("a1_terms", c["terms"]), ("quarter", c["quarter"]),
                      ("a1_wq", three_times(blockdiag(a["L1_attn_Wq"]))), ("a1_wk", three_times(blockdiag(a["L1_attn_Wk"]))),
                      ("a1_wv", blockdiag(a["L1_attn_Wv"])), ("a1_wo", a["L1_attn_W_O"])]
    seg["l1_xattn"] = [("x1_wq", a["L1_xattn_Wq"].T), ("x1_wk", a["L1_xattn_Wk"].T), ("x1_wv", a["L1_xattn_Wv"].T),
                       ("x1_wo", a["L1_xattn_Wo"].T), ("x1_bq", column(a["L1_xattn_bq"])),
                       ("x1_bv", rows(a["L1_xattn_bv"])), ("x1_bo", rows(a["L1_xattn_bo"]))]
    seg["l1_ffn"] = [("iota8", c["iota8"]), ("m1_wg", a["L1_ffn_gate_W"]), ("m1_bg", rows(a["L1_ffn_gate_b"])),
                     ("m1_w1", a["L1_ffn_W1"].transpose(1, 0, 2).reshape(D, -1)),
                     ("m1_b1", column(a["L1_ffn_b1"].reshape(-1))),
                     ("m1_w2", chunks(a["L1_ffn_W2"].reshape(-1, D))),
                     ("m1_b2", a["L1_ffn_b2"]),
                     ("m1_g", rows(a["L1_ffn_ln_gamma"])), ("m1_b", rows(a["L1_ffn_ln_beta"]))]
    seg["l2_attn"] = [(k, c[k]) for k in ("rope_c", "rope_s", "query_id", "fourfold", "quadmask")] + [
        ("a2_wq", a["L2_attn_Wq"]), ("a2_wqs", a["L2_attn_Wq"][:, np.arange(D) ^ 1]),
        ("a2_wk", a["L2_attn_Wk"]), ("a2_wks", a["L2_attn_Wk"][:, np.arange(D) ^ 1]),
        ("a2_wv", a["L2_attn_Wv"]), ("a2_wo", a["L2_attn_Wo"]), ("a2_bo", rows(a["L2_attn_bo"])),
        ("a2_wkc", np.broadcast_to(a["L2_attn_wk_comp"][:, None], (A2_CB, A2_NB))),
        ("a2_wvc", np.broadcast_to(a["L2_attn_wv_comp"][:, None], (A2_CB, A2_NB))),
        ("a2_pe", a["L2_attn_pe"]), ("a2_wg", a["L2_attn_Wg"]), ("a2_bg", rows(a["L2_attn_bg"]))]
    seg["l2_xattn"] = [("x2_w", a["L2_xattn_W"].T), ("x2_b", column(a["L2_xattn_b"])), ("x2_d", column(a["L2_xattn_D"]))]
    seg["l2_ffn"] = [("pairpick", c["pairpick"]), ("m2_wg", a["L2_ffn_w_gate"]),
                     ("m2_wd", a["L2_ffn_Wd"].transpose(1, 0, 2).reshape(D, -1)),
                     ("m2_bd", column(a["L2_ffn_bd"].reshape(-1))),
                     ("m2_wu", chunks(a["L2_ffn_Wu"].reshape(-1, D))), ("m2_bu", a["L2_ffn_bu"])]
    seg["l3_attn"] = [("a3_g", column(a["L3_attn_ln_w"])), ("a3_b", column(a["L3_attn_ln_b"])),
                      ("a3_win", a["L3_attn_in_proj_w"]), ("a3_bin", column(a["L3_attn_in_proj_b"])),
                      ("a3_cw", chunks(a["L3_attn_conv_w"])), ("a3_cb", column(a["L3_attn_conv_b"])),
                      ("a3_wx", chunks(a["L3_attn_x_proj_w"][:, np.r_[0:A3_R, np.tile(np.arange(A3_R, A3_R + 2 * A3_N), 3)]])),
                      ("a3_parts", c["parts"]), ("a3_wdt", a["L3_attn_dt_proj_w"]),
                      ("a3_bdt", column(a["L3_attn_dt_proj_b"])),
                      ("a3_d", column(a["L3_attn_D"])), ("a3_wout", chunks(a["L3_attn_out_proj_w"])),
                      ("a3_bout", rows(a["L3_attn_out_proj_b"]))]
    w, b = a["L3_xattn_in_proj_weight"], a["L3_xattn_in_proj_bias"]
    seg["l3_xattn"] = [("submap", c["submap"]), ("x3_wq", w[:D].T), ("x3_wk", w[D:2 * D].T), ("x3_wv", w[2 * D:].T),
                       ("x3_bq", column(b[:D])), ("x3_bk", column(b[D:2 * D])), ("x3_bv", rows(b[2 * D:])),
                       ("x3_wo", padded_heads(a["L3_xattn_out_proj_weight"].T)), ("x3_bo", rows(a["L3_xattn_out_proj_bias"]))]
    return seg


def pack(a):
    seg, where, pieces, parts, at = segments(a), {}, {}, [], 0
    for name, items in seg.items():
        start = at
        for key, v in items:
            v = np.asarray(v)
            where[key] = (at, v.shape[1], v.shape[0])
            full = np.zeros((P, v.shape[1]), np.float32)
            full[:v.shape[0]] = v
            parts.append(full)
            at += v.shape[1]
        pieces[name] = (start, at)
    return np.ascontiguousarray(np.concatenate(parts, 1)), where, pieces




class Sems:

    def __init__(self, nc, stage):
        self.nc, self.stage, self.made, self.stack = nc, stage, {}, ExitStack()

    def __getitem__(self, name):
        if name not in self.made:
            self.made[name] = self.stack.enter_context(self.nc.semaphore(f"{self.stage}_{name}"))
        return self.made[name]

    def clear(self):
        for s in self.made.values():
            self.nc.gpsimd.sem_clear(s)


class Steps:

    def __init__(self, eng, sem):
        self.eng, self.sem, self.n = eng, sem, 0

    def step(self, ins):
        ins.then_inc(self.sem, 1)
        self.n += 1

    def wait(self):
        self.eng.wait_ge(self.sem, self.n)

    def link(self, ins):
        self.step(ins)
        self.wait()


class Net:

    def __init__(self, nc, ctx, where):
        self.nc, self.where, self.ctx = nc, where, ctx
        self.split = where["ident"][0]
        self.W = self.sb("weights", [P, max(at + n for at, n, _ in where.values()) - self.split])
        self.tables = None
        self.x = self.sb("x", [P, NT, D])
        self.xn = self.sb("xn", [P, NT, D])
        self.xnT = self.sb("xnT", [D, T])
        self.ctxT = self.sb("ctxT", [D, S2])
        self.ctxtok = self.sb("ctxtok", [S2, D])
        self.bias = self.sb("maskrow", [P, S2])
        self.bn = self.sb("bn", [P, NT, 6])
        self.mv = self.sb("mv", [P, NT, 2])
        self.vare = self.sb("vare", [P, NT])
        self.rstd = self.sb("rstd", [P, NT])
        self.ps = [ctx.enter_context(nc.psum_tensor(f"bank{i}", [P, 512], F32)) for i in range(8)]

    def sb(self, name, shape, dt=F32):
        return self.ctx.enter_context(self.nc.sbuf_tensor(name, shape, dt))

    def w(self, key, lo=0, hi=None):
        at, n, r = self.where[key]
        held = self.W
        if at < self.split:
            held = self.tables
        else:
            at -= self.split
        return held[0:r, at + lo:at + (n if hi is None else hi)]


def tile(t, n=P):
    return slice(t * n, (t + 1) * n)




def norm_vector(net, s, v, steps, src=None, dst=None, tag=""):
    src, dst = src or net.x, dst or net.xn
    for t in range(NT):
        steps.step(v.bn_stats(net.bn[:, t, :], src[:, t, :]))
    steps.wait()
    for t in range(NT):
        last = v.bn_aggr(net.mv[:, t, :], net.bn[:, t, :])
    last.then_inc(s[tag + "variance_ready"], 1)
    v.wait_ge(s[tag + "variance_ready"], 1)
    v.wait_ge(s[tag + "rstd_ready"], 1)
    for t in range(NT):
        v.tensor_scalar(dst[:, t, :], src[:, t, :], net.mv[:, t, 0:1], net.rstd[:, t:t + 1],
                        ALU.subtract, ALU.mult).then_inc(s[tag + "norm_ready"], 1)


def norm_pool(net, s, g, steps, tag=""):
    g.wait_ge(s[tag + "variance_ready"], 1)
    steps.link(g.tensor_scalar(net.vare[:, :], net.mv[:, :, 1], LN_EPS, 0.0, ALU.add, ALU.add))
    g.tensor_tensor(net.rstd[:, :], net.vare[:, :], net.w("neghalf", 0, NT), ALU.pow).then_inc(s[tag + "rstd_ready"], 1)


def transpose_tensor(net, s, pe, src, bank, signal):
    for t in range(NT):
        last = pe.transpose(bank[:, tile(t)], src[:, t, :], net.w("ident"))
    last.then_inc(s[signal], 1)


def norm_tensor(net, s, pe, bank, src=None, tag=""):
    for t in range(NT):
        pe.wait_ge(s[tag + "norm_ready"], t + 1)
        last = pe.transpose(bank[:, tile(t)], (src or net.xn)[:, t, :], net.w("ident"))
    last.then_inc(s[tag + "normT_in_psum"], 1)


def norm_scalar(net, s, act, bank, tag=""):
    act.wait_ge(s[tag + "normT_in_psum"], 1)
    act.activation(net.xnT[:, :], bank[:, :], ACT.Copy).then_inc(s[tag + "normT_ready"], 1)


def bc(ap, n):
    return ap.unsqueeze(1).to_broadcast([ap.shape[0], n, ap.shape[1]])


def bci(ap, n):
    return ap.unsqueeze(2).to_broadcast([ap.shape[0], ap.shape[1], n])


def run_stage(nc, name, body, need, before=None, final=False):
    if before:
        before.clear()
    s = Sems(nc, name)
    with ExitStack() as ctx:
        def sb(n, shape, dt=F32):
            return ctx.enter_context(nc.sbuf_tensor(f"{name}_{n}", shape, dt))
        with nc.Block(no_gpsimd_drain=True) as block:
            body(s, sb, block, need)
    if before:
        before.stack.close()
    if final:
        s.clear()
        nc.all_engine_barrier()
        s.stack.close()
    return s




def l0_attn(net):
    nc, w, ps = net.nc, net.w, net.ps
    G = 4

    def body(s, sb, block, need):
        qabs = sb("qabs", [D, T])
        kT = sb("kT", [D, T])
        v = sb("v", [P, NT, D])
        qn = sb("qn", [A0_H, T])
        top = sb("top", [A0_H, 32])
        topi = sb("topi", [A0_H, 32], U32)
        topf = sb("topf", [A0_H, 32])
        idxd = sb("idxd", [A0_H, T])
        idxcol = sb("idxcol", [P, G])
        lastkey = sb("lastkey", [P, G])
        onehot = sb("onehot", [P, NT, T])
        onehotT = sb("onehotT", [P, G, T])
        forbid = sb("forbid", [P, G, T])
        xsel = sb("xsel", [D, T])
        qsel = sb("qsel", [D, T])
        a = sb("a", [P, G, T])
        sc = sb("sc", [P, G, T])
        mx = sb("mx", [P, G])
        nmx = sb("nmx", [P, G])
        den = sb("den", [P, G])
        rden = sb("rden", [P, G])
        aT = sb("aT", [P, G, T])
        osel = sb("osel", [P, G, D])
        oT = sb("oT", [D, T])
        scale = A0_HD ** -0.5

        @block.tensor
        def _(pe):
            need(pe)
            norm_tensor(net, s, pe, ps[0])
            pe.wait_ge(s["normT_ready"], 1)
            pe.matmul(ps[1][:, :], w("a0_wq"), net.xnT[:, :], start=True, stop=True).then_inc(s["q_in_psum"], 1)
            pe.matmul(ps[2][:, :], w("a0_wk"), net.xnT[:, :], start=True, stop=True).then_inc(s["k_in_psum"], 1)
            for t in range(NT):
                last = pe.matmul(ps[3][:, tile(t)], net.xnT[:, tile(t)], w("a0_wv"), start=True, stop=True)
            last.then_inc(s["v_in_psum"], 1)
            pe.wait_ge(s["qabs_ready"], 1)
            pe.matmul(ps[4][0:A0_H, :], w("headsum"), qabs[:, :], start=True, stop=True).then_inc(s["qnorm_in_psum"], 1)
            pe.wait_ge(s["idx_ready"], 1)
            pe.matmul(ps[5][:, :], w("ones")[0:A0_H, :], idxd[:, :], start=True, stop=True).then_inc(s["idxrow_in_psum"], 1)
            for g in range(G):
                last = pe.matmul(ps[6][:, g:g + 1], idxd[:, tile(g)], w("ones")[0:A0_H, 0:1], start=True, stop=True)
            last.then_inc(s["idxcol_in_psum"], 1)
            for t in range(NT):
                pe.wait_ge(s["onehot_ready"], t + 1)
                last = pe.matmul(ps[7][:, :], net.xn[:, t, :], onehot[:, t, :], start=(t == 0), stop=(t == NT - 1))
            last.then_inc(s["xsel_in_psum"], 1)
            pe.wait_ge(s["xsel_ready"], 1)
            pe.matmul(ps[1][:, :], w("a0_wq"), xsel[:, :], start=True, stop=True).then_inc(s["qsel_in_psum"], 1)
            pe.wait_ge(s["qsel_ready"], 1)
            pe.wait_ge(s["k_ready"], 1)
            for g in range(G):
                if g >= 2:
                    pe.wait_ge(s["masked_ready"], g - 1)
                if g == 1:
                    pe.wait_ge(s["onehot_ready"], NT)
                pe.matmul(ps[4 + g % 2][:, :], qsel[:, tile(g)], kT[:, :], start=True, stop=True)\
                  .then_inc(s["scores_in_psum"], 1)
            for g in range(G):
                pe.wait_ge(s["probs_ready"], g + 1)
                if g >= 2:
                    pe.wait_ge(s["aT_ready"], g - 1)
                elif g == 1:
                    pe.wait_ge(s["v_ready"], 1)
                for t in range(NT):
                    last = pe.transpose(ps[2 + g % 2][:, tile(t)], a[:, g, tile(t)], w("ident"))
                last.then_inc(s["aT_in_psum"], 1)
            pe.wait_ge(s["v_ready"], 1)
            for g in range(G):
                pe.wait_ge(s["aT_ready"], g + 1)
                for t in range(NT):
                    last = pe.matmul(ps[7][:, tile(g)], aT[:, g, tile(t)], v[:, t, :], start=(t == 0), stop=(t == NT - 1))
                last.then_inc(s["osel_in_psum"], 1)
            for g in range(G):
                pe.wait_ge(s["osel_ready"], g + 1)
                last = pe.matmul(ps[0][:, :], osel[:, g, :], onehotT[:, g, :], start=(g == 0), stop=(g == G - 1))
            last.then_inc(s["out_in_psum"], 1)
            pe.wait_ge(s["oT_ready"], 1)
            for t in range(NT):
                last = pe.matmul(ps[1][:, tile(t)], oT[:, tile(t)], w("a0_wo"), start=True, stop=True)
            last.then_inc(s["y_in_psum"], 1)

        @block.scalar
        def _(act):
            need(act)
            norm_scalar(net, s, act, ps[0])
            act.wait_ge(s["q_in_psum"], 1)
            act.activation(qabs[:, :], ps[1][:, :], ACT.Abs, bias=w("a0_bq")).then_inc(s["qabs_ready"], 1)
            act.wait_ge(s["k_in_psum"], 1)
            act.activation(kT[:, :], ps[2][:, :], ACT.Identity, bias=w("a0_bk")).then_inc(s["k_ready"], 1)
            act.wait_ge(s["xsel_in_psum"], 1)
            act.activation(xsel[:, :], ps[7][:, :], ACT.Copy).then_inc(s["xsel_ready"], 1)
            for g in range(G):
                act.wait_ge(s["max_ready"], g + 1)
                act.activation(a[:, g, :], sc[:, g, :], ACT.Exp, bias=nmx[:, g:g + 1], scale=scale,
                               accum_out=den[:, g:g + 1]).then_inc(s["probs_ready"], 1)
            for g in range(G):
                act.wait_ge(s["aT_in_psum"], g + 1)
                act.activation(aT[:, g, :], ps[2 + g % 2][:, :], ACT.Copy).then_inc(s["aT_ready"], 1)
            act.wait_ge(s["out_in_psum"], 1)
            act.activation(oT[:, :], ps[0][:, :], ACT.Copy).then_inc(s["oT_ready"], 1)

        @block.gpsimd
        def _(g_):
            need(g_)
            norm_pool(net, s, g_, Steps(g_, s["pool_step"]))

        @block.vector
        def _(v_):
            need(v_)
            st = Steps(v_, s["vector_step"])
            norm_vector(net, s, v_, st)
            v_.wait_ge(s["v_in_psum"], 1)
            v_.tensor_tensor(v[:, :, :], ps[3][:, :].rearrange("p (t d) -> p t d", t=NT), bc(w("a0_bv"), NT), ALU.add)\
              .then_inc(s["v_ready"], 1)
            v_.wait_ge(s["qnorm_in_psum"], 1)
            st.link(v_.tensor_copy(qn[:, :], ps[4][0:A0_H, :]))
            for r in range(4):
                e = slice(8 * r, 8 * r + 8)
                st.link(v_.max(top[:, e], qn[:, :]))
                st.link(v_.max_index(topi[:, e], top[:, e], qn[:, :]))
                if r < 3:
                    st.link(v_.match_replace(qn[:, :], top[:, e], qn[:, :], -1.0))
            st.link(v_.tensor_copy(topf[:, :], topi[:, :]))
            st.link(v_.memset(topf[:, A0_U:32], -1.0))
            v_.tensor_tensor(idxd[:, :].rearrange("h (a u) -> h a u", u=32), w("diag16")[0:A0_H, :].rearrange("h (a u) -> h a u", u=32),
                             bc(topf[:, :], A0_H), ALU.mult).then_inc(s["idx_ready"], 1)
            v_.wait_ge(s["idxrow_in_psum"], 1)
            for t in range(NT):
                v_.tensor_scalar(onehot[:, t, :], ps[5][:, :], w("tokid")[:, t:t + 1], None, ALU.is_equal)\
                  .then_inc(s["onehot_ready"], 1)
            v_.wait_ge(s["idxcol_in_psum"], 1)
            st.step(v_.tensor_copy(idxcol[:, :], ps[6][:, 0:G]))
            st.link(v_.tensor_scalar(lastkey[:, :], ps[6][:, 0:G], 0.0, None, ALU.max))
            for g in range(G):
                st.step(v_.tensor_scalar(onehotT[:, g, :], w("iota"), idxcol[:, g:g + 1], None, ALU.is_equal))
                st.step(v_.tensor_scalar(forbid[:, g, :], w("iota"), lastkey[:, g:g + 1], NEG, ALU.is_gt, ALU.mult))
            st.wait()
            v_.wait_ge(s["qsel_in_psum"], 1)
            v_.scalar_tensor_tensor(out=qsel[:, :], in0=ps[1][:, :], scalar=w("a0_bq"), in1=w("headmask"),
                                    op0=ALU.add, op1=ALU.mult).then_inc(s["qsel_ready"], 1)
            for g in range(G):
                v_.wait_ge(s["scores_in_psum"], g + 1)
                v_.tensor_tensor_reduce(sc[:, g, :], ps[4 + g % 2][:, :], forbid[:, g, :], 1.0, -3.0e38,
                                        ALU.add, ALU.max, mx[:, g:g + 1]).then_inc(s["masked_ready"], 1)
                v_.wait_ge(s["masked_ready"], g + 1)
                v_.tensor_scalar(nmx[:, g:g + 1], mx[:, g:g + 1], -scale, None, ALU.mult).then_inc(s["max_ready"], 1)
            v_.wait_ge(s["probs_ready"], G)
            st.link(v_.reciprocal(rden[:, :], den[:, :]))
            v_.wait_ge(s["osel_in_psum"], G)
            for g in range(G):
                v_.scalar_tensor_tensor(out=osel[:, g, :], in0=ps[7][:, tile(g)], scalar=rden[:, g:g + 1],
                                        in1=w("rowmask", g * D, (g + 1) * D), op0=ALU.mult, op1=ALU.mult)\
                  .then_inc(s["osel_ready"], 1)
            st.link(v_.tensor_tensor(net.x[:, :, :], net.x[:, :, :], bc(w("a0_bo"), NT), ALU.add))
            v_.wait_ge(s["y_in_psum"], 1)
            st.link(v_.tensor_tensor(net.x[:, :, :], net.x[:, :, :], ps[1][:, :].rearrange("p (t d) -> p t d", t=NT), ALU.add))

    return body




def xattn(net, wq, wk, wv=None, bq=None, bv=None, wo=None, bo=None, scale=1.0, relu=False, kd=None, masked=False):
    nc, w, ps = net.nc, net.w, net.ps

    def body(s, sb, block, need):
        qT = sb("qT", [D, T])
        kT = sb("kT", [D, S2])
        vt = sb("vt", [S2, D])
        sc = sb("sc", [P, NT, S2])
        a = sb("a", [P, NT, S2])
        mx = sb("mx", [P, NT])
        nmx = sb("nmx", [P, NT])
        den = sb("den", [P, NT])
        rden = sb("rden", [P, NT])
        aT = sb("aT", [S2, T])
        oT = sb("oT", [D, T])
        keep = sb("keep", [P, S2])
        value = vt if wv else net.ctxtok
        scores = ps[4][:, 0:NT * S2].rearrange("p (t k) -> p t k", t=NT)

        @block.tensor
        def _(pe):
            need(pe)
            pe.matmul(ps[1][:, 0:S2], w(wk), net.ctxT[:, :], start=True, stop=True).then_inc(s["k_in_psum"], 1)
            if wv:
                pe.matmul(ps[2][0:S2, 0:D], net.ctxT[:, :], w(wv), start=True, stop=True).then_inc(s["v_in_psum"], 1)
            norm_tensor(net, s, pe, ps[0])
            pe.wait_ge(s["normT_ready"], 1)
            pe.matmul(ps[3][:, :], w(wq), net.xnT[:, :], start=True, stop=True).then_inc(s["q_in_psum"], 1)
            pe.wait_ge(s["q_ready"], 1)
            pe.wait_ge(s["k_ready"], 1)
            for t in range(NT):
                last = pe.matmul(scores[:, t, :], qT[:, tile(t)], kT[:, :], start=True, stop=True)
            last.then_inc(s["scores_in_psum"], 1)
            for t in range(NT):
                pe.wait_ge(s["probs_ready"], t + 1)
                last = pe.transpose(ps[5][0:S2, tile(t)], a[:, t, :], w("ident"))
            last.then_inc(s["aT_in_psum"], 1)
            pe.wait_ge(s["aT_ready"], 1)
            if wv:
                pe.wait_ge(s["v_ready"], 1)
            if wo:
                pe.matmul(ps[6][:, :], value[:, :], aT[:, :], start=True, stop=True).then_inc(s["o_in_psum"], 1)
                pe.wait_ge(s["oT_ready"], 1)
                for t in range(NT):
                    last = pe.matmul(ps[7][:, tile(t)], oT[:, tile(t)], w(wo), start=True, stop=True)
            else:
                for t in range(NT):
                    last = pe.matmul(ps[7][:, tile(t)], aT[:, tile(t)], value[:, :], start=True, stop=True)
            last.then_inc(s["y_in_psum"], 1)

        @block.scalar
        def _(act):
            need(act)
            act.wait_ge(s["k_in_psum"], 1)
            if relu:
                st = Steps(act, s["scalar_step"])
                st.link(act.activation(kT[:, :], ps[1][:, 0:S2], ACT.Relu, bias=w(bq)))
                act.activation(kT[:, :], kT[:, :], ACT.Copy, scale=w(kd)).then_inc(s["k_ready"], 1)
            else:
                act.activation(kT[:, :], ps[1][:, 0:S2], ACT.Copy).then_inc(s["k_ready"], 1)
            norm_scalar(net, s, act, ps[0])
            act.wait_ge(s["q_in_psum"], 1)
            act.activation(qT[:, :], ps[3][:, :], ACT.Relu if relu else ACT.Identity,
                           bias=w(bq) if bq else 0.0).then_inc(s["q_ready"], 1)
            act.wait_ge(s["max_ready"], 1)
            for t in range(NT):
                act.activation(a[:, t, :], sc[:, t, :], ACT.Exp, bias=nmx[:, t:t + 1], scale=scale,
                               accum_out=den[:, t:t + 1]).then_inc(s["probs_ready"], 1)
            act.wait_ge(s["aT_in_psum"], 1)
            act.activation(aT[:, :], ps[5][0:S2, :], ACT.Copy).then_inc(s["aT_ready"], 1)
            if wo:
                act.wait_ge(s["o_in_psum"], 1)
                act.activation(oT[:, :], ps[6][:, :], ACT.Copy).then_inc(s["oT_ready"], 1)

        @block.gpsimd
        def _(g):
            need(g)
            norm_pool(net, s, g, Steps(g, s["pool_step"]))

        @block.vector
        def _(v):
            need(v)
            st = Steps(v, s["vector_step"])
            norm_vector(net, s, v, st)
            if wv:
                v.wait_ge(s["v_in_psum"], 1)
                if bv:
                    v.tensor_tensor(vt[:, :], ps[2][0:S2, 0:D], w(bv)[0:S2, :], ALU.add).then_inc(s["v_ready"], 1)
                else:
                    v.tensor_copy(vt[:, :], ps[2][0:S2, 0:D]).then_inc(s["v_ready"], 1)
            if masked:
                st.link(v.tensor_scalar(keep[:, :], net.bias[:, :], -1.0, 1.0, ALU.mult, ALU.add))
                v.wait_ge(s["scores_in_psum"], 1)
                st.link(v.tensor_tensor(sc[:, :, :], scores, bc(keep[:, :], NT), ALU.mult))
                st.link(v.tensor_scalar(keep[:, :], net.bias[:, :], NEG, None, ALU.mult))
                st.link(v.tensor_tensor(sc[:, :, :], sc[:, :, :], bc(keep[:, :], NT), ALU.add))
            else:
                v.wait_ge(s["scores_in_psum"], 1)
                st.link(v.tensor_copy(sc[:, :, :], scores))
            st.link(v.tensor_reduce(mx[:, :], sc[:, :, :], AX.X, ALU.max))
            v.tensor_scalar(nmx[:, :], mx[:, :], -scale, None, ALU.mult).then_inc(s["max_ready"], 1)
            v.wait_ge(s["probs_ready"], NT)
            st.link(v.reciprocal(rden[:, :], den[:, :]))
            if bo:
                st.link(v.tensor_tensor(net.x[:, :, :], net.x[:, :, :], bc(w(bo), NT), ALU.add))
            v.wait_ge(s["y_in_psum"], 1)
            for t in range(NT):
                st.step(v.scalar_tensor_tensor(out=net.x[:, t, :], in0=ps[7][:, tile(t)], scalar=rden[:, t:t + 1],
                                               in1=net.x[:, t, :], op0=ALU.mult, op1=ALU.add))
            st.wait()

    return body




def shift_tensor(net, s, pe, y, bank):
    halves = bank[:, 0:NT * 64].rearrange("p (t d) -> p t d", t=NT)
    pe.matmul(halves, net.w("shift"), y[:, :, 64:D], start=True, stop=False)
    pe.matmul(halves[:, 1:NT, :], net.w("carry"), y[:, 0:NT - 1, 64:D], start=False, stop=True)\
      .then_inc(s["shift_in_psum"], 1)


def shift_scalar(net, s, act, steps, y, h, bank):
    steps.step(act.activation(h[:, :, 0:64], y[:, :, 0:64], ACT.Copy))
    act.wait_ge(s["shift_in_psum"], 1)
    act.activation(h[:, :, 64:D], bank[:, 0:NT * 64].rearrange("p (t d) -> p t d", t=NT), ACT.Copy)\
       .then_inc(s["shifted_ready"], 1)


def f0_attn(net, l, first):
    nc, w, ps, y = net.nc, net.w, net.ps, net.y
    HB = F0_H // 2
    N = NT * HB

    def body(s, sb, block, need):
        hT = sb("hT", [D, T])
        raw = sb("raw", [P, 2, 2, F0_IN])
        sq = sb("sq", [P, 2, F0_IN])
        ss = sb("ss", [P, 2, NT, F0_H])
        rn = sb("rn", [P, 2, NT, F0_H])
        sq8 = sb("sq8", [P, NT, F0_H])
        cs = sb("cs", [P, 2, F0_IN])
        sn = sb("sn", [P, 2, F0_IN])
        h = sn[:, 0, :].rearrange("p (t d) -> p t d", t=NT)
        rot = sb("rot", [P, 2, 2, F0_IN])
        v = sb("v", [P, NT, F0_IN])
        qT = sb("qT", [P, HB, T])
        kT = sb("kT", [P, 2, HB, T])
        sc = sb("sc", [P, 4, 2, 192])
        a = sb("a", [P, 4, 2, 256])
        mx = sb("mx", [P, N, 2])
        nmx = sb("nmx", [P, N, 2])
        den = sb("den", [P, N, 2])
        rden = sb("rden", [P, N, 2])
        aT = sb("aT", [P, 2, 2, 256])
        oT = raw[:, :, :, :].rearrange("p a b t -> p (a b) t")
        keys = lambda t: slice(64 if t == 0 else 0, 192)

        def turn(pe, t):
            for j in range(2):
                pe.wait_ge(s["rotated"], 2 * t + j + 1)
                if t >= 1:
                    pe.wait_ge(s["qkT_ready"], 2 * t + j - 1)
                for hb in range(HB):
                    last = pe.transpose(ps[j][:, tile(hb)], rot[:, t % 2, j, tile(hb)], w("ident"))
                last.then_inc(s["qkT_in_psum"], 1)

        @block.tensor
        def _(pe):
            need(pe)
            if first:
                pe.wait_ge(s["norm_ready"], NT)
            shift_tensor(net, s, pe, y, ps[0])
            pe.wait_ge(s["shifted_ready"], 1)
            transpose_tensor(net, s, pe, h, ps[1], "hT_in_psum")
            pe.wait_ge(s["hT_ready"], 1)
            for t in range(NT):
                if t >= 2:
                    pe.wait_ge(s["raw_ready"], t - 1)
                for j in range(3):
                    last = pe.matmul(ps[2 + 3 * (t % 2) + j][:, :], hT[:, tile(t)],
                                     w(f"f0_wqkv{l}", j * F0_IN, (j + 1) * F0_IN), start=True, stop=True)
                last.then_inc(s["qkv_in_psum"], 1)
                if t >= 1:
                    turn(pe, t - 1)
            turn(pe, NT - 1)
            pe.wait_ge(s["raw_ready"], NT)
            pe.wait_ge(s["qkT_ready"], 2 * NT)
            for i in range(N + 4):
                if i < N:
                    t, hb = divmod(i, HB)
                    if i >= 2:
                        pe.wait_ge(s["masked_ready"], i - 1)
                    for e in range(2):
                        lo = max(P * t - 64, 0)
                        last = pe.matmul(ps[2 + 2 * (i % 2) + e][:, keys(t)],
                                         qT[:, hb, tile(t)], kT[:, e, hb, lo:P * t + P], start=True, stop=True)
                    last.then_inc(s["scores_in_psum"], 1)
                if 3 <= i < N + 3:
                    j = i - 3
                    t = j // HB
                    pe.wait_ge(s["probs_ready"], j + 1)
                    if j >= 2:
                        pe.wait_ge(s["aT_ready"], j - 1)
                    for e in range(2):
                        for c in range(0 if t else 1, 2):
                            last = pe.transpose(ps[6 + j % 2][:, 256 * e + P * c:256 * e + P * c + P],
                                                a[:, j % 4, e, tile(c)], w("ident"))
                    last.then_inc(s["aT_in_psum"], 1)
                if i >= 4:
                    j = i - 4
                    t, hb = divmod(j, HB)
                    pe.wait_ge(s["aT_ready"], j + 1)
                    if hb == 0 and t >= 2:
                        pe.wait_ge(s["oT_ready"], t - 1)
                    for e in range(2):
                        f = slice((2 * hb + e) * F0_HD, (2 * hb + e + 1) * F0_HD)
                        for c in range(0 if t else 1, 2):
                            last = pe.matmul(ps[t % 2][64 * e:64 * e + 64, tile(hb)], v[:, t - 1 + c, f],
                                             aT[:, j % 2, e, tile(c)], start=(c == (0 if t else 1)), stop=(c == 1))
                    last.then_inc(s["pairs_done"], 1)
            pe.wait_ge(s["oT_ready"], NT)
            for t in range(NT):
                for hb in range(HB):
                    last = pe.matmul(ps[2][:, tile(t)], oT[:, hb, tile(t)], w(f"f0_wo{l}", hb * D, (hb + 1) * D),
                                     start=(hb == 0), stop=(hb == HB - 1))
            last.then_inc(s["y_in_psum"], 1)

        @block.scalar
        def _(act):
            need(act)
            st = Steps(act, s["scalar_step"])
            if first:
                act.wait_ge(s["norm_ready"], NT)
            shift_scalar(net, s, act, st, y, h, ps[0])
            act.wait_ge(s["hT_in_psum"], 1)
            act.activation(hT[:, :], ps[1][:, :], ACT.Copy).then_inc(s["hT_ready"], 1)

            def evac_turned(t):
                act.wait_ge(s["qkT_in_psum"], 2 * t + 1)
                act.activation(qT[:, :, tile(t)], ps[0][:, :].rearrange("p (b t) -> p b t", b=HB), ACT.Copy)\
                   .then_inc(s["qkT_ready"], 1)
                act.wait_ge(s["qkT_in_psum"], 2 * t + 2)
                for e in range(2):
                    last = act.activation(kT[:, e, :, tile(t)], ps[1][:, :].rearrange("p (b t) -> p b t", b=HB), ACT.Copy,
                                          scale=w("halves", e, e + 1))
                last.then_inc(s["qkT_ready"], 1)

            for t in range(NT):
                act.wait_ge(s["qkv_in_psum"], t + 1)
                if t >= 2:
                    act.wait_ge(s["rotated"], 2 * (t - 1))
                for j in range(2):
                    st.step(act.activation(raw[:, t % 2, j, :], ps[2 + 3 * (t % 2) + j][:, :], ACT.Copy))
                    if t >= 1:
                        act.wait_ge(s["squares_summed"], 2 * t + j - 1)
                    act.activation(sq[:, j, :], ps[2 + 3 * (t % 2) + j][:, :], ACT.Square).then_inc(s["squares_ready"], 1)
                act.activation(v[:, t, :], ps[4 + 3 * (t % 2)][:, :], ACT.Copy).then_inc(s["raw_ready"], 1)
                if t >= 1:
                    evac_turned(t - 1)
            evac_turned(NT - 1)
            for i in range(N + 4):
                if i < N:
                    t = i // HB
                    act.wait_ge(s["max_ready"], i + 1)
                    if i >= 4:
                        act.wait_ge(s["aT_in_psum"], i - 3)
                    for e in range(2):
                        k = keys(t)
                        last = act.activation(a[:, i % 4, e, 64 + k.start:256], sc[:, i % 4, e, k], ACT.Exp,
                                              bias=nmx[:, i, e:e + 1], scale=sq8[:, t, 2 * (i % HB) + e:2 * (i % HB) + e + 1],
                                              accum_out=den[:, i, e:e + 1])
                    last.then_inc(s["exp_ready"], 1)
                if 3 <= i < N + 3:
                    j = i - 3
                    act.wait_ge(s["aT_in_psum"], j + 1)
                    if j >= 2:
                        act.wait_ge(s["pairs_done"], j - 1)
                    k = slice(0 if j >= HB else P, 256)
                    act.activation(aT[:, j % 2, :, k], ps[6 + j % 2][:, :].rearrange("p (e k) -> p e k", e=2)[:, :, k],
                                   ACT.Copy).then_inc(s["aT_ready"], 1)
                if i >= 4 and (i - 4) % HB == HB - 1:
                    t = (i - 4) // HB
                    act.wait_ge(s["pairs_done"], HB * (t + 1))
                    act.activation(oT[:, :, tile(t)], ps[t % 2][:, :].rearrange("p (b t) -> p b t", b=HB), ACT.Copy)\
                       .then_inc(s["oT_ready"], 1)

        @block.gpsimd
        def _(g):
            need(g)
            st = Steps(g, s["pool_step"])
            g.memset(a[:, :, :, 0:64], 0.0).then_inc(s["pad_ready"], 1)
            if first:
                norm_pool(net, s, g, st)
            for t in range(NT):
                for j in range(2):
                    if j == 0:
                        g.wait_ge(s["squares_ready"], 2 * t + 1)
                        if t >= 1:
                            g.wait_ge(s["rotated"], 2 * t - 1)
                        g.tensor_tensor(cs[:, 0, :].rearrange("p (h d) -> p h d", h=F0_H), raw[:, t % 2, 0, :].rearrange("p (h d) -> p h d", h=F0_H),
                                        bc(net.rot[:, l, 0, 0, t, :], F0_H), ALU.mult).then_inc(s["cosines_ready"], 1)
                    g.wait_ge(s["squares_summed"], 2 * t + j + 1)
                    st.link(g.tensor_scalar(ss[:, j, t, :], ss[:, j, t, :], 1e-24, 1.0, ALU.max, ALU.mult))
                    g.tensor_tensor(rn[:, j, t, :], ss[:, j, t, :], net.w("neghalf", 0, F0_H), ALU.pow)\
                     .then_inc(s["norms_ready"], 1)

        @block.vector
        def _(v_):
            need(v_)
            st = Steps(v_, s["vector_step"])
            if first:
                norm_vector(net, s, v_, st, dst=y)
            for t in range(NT):
                for j in range(2):
                    src = raw[:, t % 2, j, :].rearrange("p (h d) -> p h d", h=F0_H)
                    co = cs[:, j, :].rearrange("p (h d) -> p h d", h=F0_H)
                    si = sn[:, j, :].rearrange("p (h d) -> p h d", h=F0_H)
                    ro = rot[:, t % 2, j, :].rearrange("p (h d) -> p h d", h=F0_H)
                    C, S = net.rot[:, l, j, 0, t, :], net.rot[:, l, j, 1, t, :]
                    v_.wait_ge(s["squares_ready"], 2 * t + j + 1)
                    v_.tensor_reduce(ss[:, j, t, :], sq[:, j, :].rearrange("p (h d) -> p h d", h=F0_H), AX.X, ALU.add)\
                      .then_inc(s["squares_summed"], 1)
                    if j == 1:
                        st.step(v_.tensor_tensor(co, src, bc(C, F0_H), ALU.mult))
                    st.step(v_.tensor_tensor(si[:, :, 0:32], src[:, :, 32:64], bc(S[:, 0:32], F0_H), ALU.mult))
                    st.link(v_.tensor_tensor(si[:, :, 32:64], src[:, :, 0:32], bc(S[:, 32:64], F0_H), ALU.mult))
                    if t >= 2:
                        v_.wait_ge(s["qkT_in_psum"], 2 * (t - 2) + j + 1)
                    if j == 0:
                        v_.wait_ge(s["cosines_ready"], t + 1)
                        v_.tensor_tensor(ro, co, si, ALU.add).then_inc(s["rotated"], 1)
                    else:
                        st.link(v_.tensor_tensor(co, co, si, ALU.add))
                        v_.wait_ge(s["norms_ready"], 2 * t + 2)
                        v_.tensor_tensor(ro, co, bci(rn[:, 1, t, :], F0_HD), ALU.mult).then_inc(s["rotated"], 1)
            st.link(v_.tensor_scalar(sq8[:, :, :], rn[:, 0, :, :], 8.0, None, ALU.mult))
            v_.wait_ge(s["pad_ready"], 1)
            for i in range(N + 1):
                if i < N:
                    t, hb = divmod(i, HB)
                    v_.wait_ge(s["scores_in_psum"], i + 1)
                    if i >= 4:
                        v_.wait_ge(s["exp_ready"], i - 3)
                    for e in range(2):
                        k = keys(t)
                        last = v_.tensor_tensor_reduce(sc[:, i % 4, e, k], ps[2 + 2 * (i % 2) + e][:, k],
                                                       w("band", k.start, 192), 1.0, -3.0e38, ALU.add, ALU.max,
                                                       mx[:, i, e:e + 1])
                    last.then_inc(s["masked_ready"], 1)
                    v_.wait_ge(s["masked_ready"], i + 1)
                    v_.scalar_tensor_tensor(out=nmx[:, i, :], in0=mx[:, i, :], scalar=-1.0, in1=sq8[:, t, 2 * hb:2 * hb + 2],
                                            op0=ALU.mult, op1=ALU.mult).then_inc(s["max_ready"], 1)
                if i >= 1:
                    j = i - 1
                    k = slice(64 + keys(j // HB).start, 256)
                    v_.wait_ge(s["exp_ready"], j + 1)
                    st.link(v_.reciprocal(rden[:, j, :], den[:, j, :]))
                    for e in range(2):
                        last = v_.tensor_scalar(a[:, j % 4, e, k], a[:, j % 4, e, k], rden[:, j, e:e + 1], None, ALU.mult)
                    last.then_inc(s["probs_ready"], 1)
            v_.wait_ge(s["y_in_psum"], 1)
            st.link(v_.tensor_tensor(y[:, :, :], y[:, :, :], ps[2][:, :].rearrange("p (t d) -> p t d", t=NT), ALU.add))

    return body


def f0_mlp(net, l, last_layer):
    nc, w, ps, y = net.nc, net.w, net.ps, net.y
    C = len(F0_CH)

    def body(s, sb, block, need):
        h = sb("h", [P, NT, D])
        hn = sb("hn", [P, NT, D])
        hT = sb("hT", [D, T])
        gate = sb("gate", [P, C, T])
        u = sb("u", [P, C, T])

        @block.tensor
        def _(pe):
            need(pe)
            shift_tensor(net, s, pe, y, ps[0])
            pe.wait_ge(s["shifted_ready"], 1)
            norm_tensor(net, s, pe, ps[0], src=hn)
            pe.wait_ge(s["hT_ready"], 1)
            for c, (lo, n) in enumerate(F0_CH):
                pe.matmul(ps[4 + c][0:n, :], w(f"f0_w1{l}", F0_HID + lo, F0_HID + lo + n), hT[:, :], start=True, stop=True)\
                  .then_inc(s["gate_in_psum"], 1)
                pe.matmul(ps[1 + c][0:n, :], w(f"f0_w1{l}", lo, lo + n), hT[:, :], start=True, stop=True)\
                  .then_inc(s["up_in_psum"], 1)
            pe.wait_ge(s["u_ready"], C)
            for t in range(NT):
                for c, (_, n) in enumerate(F0_CH):
                    last = pe.matmul(ps[7][:, tile(t)], u[0:n, c, tile(t)], w(f"f0_w2{l}", c * D, (c + 1) * D)[0:n, :],
                                     start=(c == 0), stop=(c == C - 1))
            last.then_inc(s["y_in_psum"], 1)

        @block.scalar
        def _(act):
            need(act)
            shift_scalar(net, s, act, Steps(act, s["scalar_step"]), y, h, ps[0])
            act.wait_ge(s["normT_in_psum"], 1)
            act.activation(hT[:, :], ps[0][:, :], ACT.Identity, bias=w(f"f0_b{l}"), scale=w(f"f0_g{l}")).then_inc(s["hT_ready"], 1)
            for c, (_, n) in enumerate(F0_CH):
                act.wait_ge(s["gate_in_psum"], c + 1)
                act.activation(gate[0:n, c, :], ps[4 + c][0:n, :], ACT.Gelu, bias=w(f"f0_b1g{l}", c, c + 1)[0:n, :])\
                   .then_inc(s["gate_ready"], 1)

        @block.gpsimd
        def _(g):
            need(g)
            norm_pool(net, s, g, Steps(g, s["pool_step"]))

        @block.vector
        def _(v):
            need(v)
            st = Steps(v, s["vector_step"])
            v.wait_ge(s["shifted_ready"], 1)
            norm_vector(net, s, v, st, src=h, dst=hn)
            for c, (_, n) in enumerate(F0_CH):
                v.wait_ge(s["up_in_psum"], c + 1)
                v.wait_ge(s["gate_ready"], c + 1)
                v.scalar_tensor_tensor(out=u[0:n, c, :], in0=ps[1 + c][0:n, :], scalar=w(f"f0_b1a{l}", c, c + 1)[0:n, :],
                                       in1=gate[0:n, c, :], op0=ALU.add, op1=ALU.mult).then_inc(s["u_ready"], 1)
            st.link(v.tensor_tensor(y[:, :, :], y[:, :, :], bc(w(f"f0_b2{l}"), NT), ALU.add))
            v.wait_ge(s["y_in_psum"], 1)
            st.link(v.tensor_tensor(y[:, :, :], y[:, :, :], ps[7][:, :].rearrange("p (t d) -> p t d", t=NT), ALU.add))
            if last_layer:
                st.link(v.tensor_tensor(net.x[:, :, :], net.x[:, :, :], y[:, :, :], ALU.add))

    return body


def l0_ffn(net):
    parts = []
    for l in range(F0_L):
        parts += [f0_attn(net, l, l == 0), f0_mlp(net, l, l == F0_L - 1)]
    return parts




def l1_attn(net):
    nc, w, ps = net.nc, net.w, net.ps
    SETS, R = A1_H // 4, 4
    ORDER = list(range(NT))[::-1]
    scale = A1_HD ** -0.5
    OUT, MISC = ps[6], ps[7]

    def body(s, sb, block, need):
        qa = sb("qa", [P, SETS, T], BF16)
        qb = sb("qb", [P, SETS, T], BF16)
        ka = sb("ka", [P, A1_H, T], BF16)
        kb = sb("kb", [P, A1_H, T], BF16)
        first = sb("first", [P, 2, T], BF16)
        second = sb("second", [P, 2, T], BF16)
        less = sb("less", [P, 2, T])
        kset = sb("kset", [P, 2, T], BF16)
        mT = sb("mT", [32, 2, T], BF16)
        va = sb("va", [P, NT, A1_H, 32])
        junk = less
        mx = sb("mx", [P, SETS, NT, R])
        mp = sb("mp", [P, SETS, NT, 32], BF16)
        ex = sb("ex", [P, 2, R, T])
        oS = sb("oS", [P, T])
        rden = sb("rden", [P, SETS, NT, R])
        cat = sb("cat", [P, D, NT])
        rowgroup = [slice(32 * r, 32 * r + 32) for r in range(R)]

        def pass1_tensor(pe, j, i, k):
            u = (j * NT + i) * R + k
            t = ORDER[i]
            if u >= 2:
                pe.wait_ge(s["row_max"], u - 1)
            pe.matmul(ps[u % 2][:, 0:P * (t + 1)], qa[:, j, tile(t)], ka[:, R * j + k, 0:P * (t + 1)],
                      start=True, stop=True).then_inc(s["scores_in_psum"], 1)

        def maxima_tensor(pe, j):
            pe.wait_ge(s["mp_ready"], j + 1)
            if j >= 2:
                pe.wait_ge(s["cat_ready"], j - 1)
            elif j == 1:
                pe.wait_ge(s["mT_ready"], 1)
            for t in range(NT):
                last = pe.transpose(MISC[0:32, :].bitcast(BF16)[:, tile(t)], mp[:, j, t, :], net.ident16[:, :])
            last.then_inc(s["maxima_in_psum"], 1)

        def apply_tensor(pe, g):
            j, kt = divmod(g, NT)
            pe.wait_ge(s["ex_ready"], g + 1)
            if kt == 0 and j >= 1:
                pe.wait_ge(s["oS_ready"], j)
            for r in range(R):
                last = pe.matmul(OUT[rowgroup[r], P * kt:T], va[:, kt, R * j + r, :], ex[:, g % 2, r, 0:T - P * kt],
                                 start=(kt == 0), stop=(kt == NT - 1))
            last.then_inc(s["applied"], 1)

        def heads_tensor(pe, j):
            pe.wait_ge(s["oS_ready"], j + 1)
            pe.wait_ge(s["mT_ready"], min(j + 2, SETS))
            if j == SETS - 1:
                pe.wait_ge(s["cat_ready"], j)
            for t in range(NT):
                last = pe.transpose(MISC[:, tile(t)], oS[:, tile(t)], w("ident"))
            last.then_inc(s["heads_in_psum"], 1)

        @block.tensor
        def _(pe):
            need(pe)
            norm_tensor(net, s, pe, ps[0])
            pe.wait_ge(s["normT_ready"], 1)

            def project(units):
                for i in units:
                    if i >= 4:
                        pe.wait_ge(s["less_ready"], i - 3)
                    pe.matmul(ps[2 + i % 4][:, :], w(("a1_wq", "a1_wk")[i % 2], tile(i // 2).start, tile(i // 2).stop), net.xnT[:, :],
                              start=True, stop=True).then_inc(s["projected"], 1)

            project(range(0, 4))
            for t in range(NT):
                last = pe.matmul(OUT[:, tile(t)], net.xnT[:, tile(t)], w("a1_wv"), start=True, stop=True)
            last.then_inc(s["v_in_psum"], 1)
            pe.wait_ge(s["a_ready"], 1)
            for i in range(NT):
                for r in range(R):
                    pass1_tensor(pe, 0, i, r)
            maxima_tensor(pe, 0)
            project(range(4, 2 * SETS))
            pe.wait_ge(s["va_ready"], 1)
            pe.wait_ge(s["less_ready"], 2 * SETS)
            for j in range(SETS):
                pe.wait_ge(s["mT_ready"], j + 1)
                pe.wait_ge(s["b_ready"], j + 1)
                if j + 1 < SETS:
                    pe.wait_ge(s["a_ready"], j + 2)
                for kt in range(NT):
                    g = j * NT + kt
                    if kt == 3 and j >= 1:
                        heads_tensor(pe, j - 1)
                    for r in range(R):
                        if g >= 1:
                            pe.wait_ge(s["exp_done"], R * (g - 1) + r + 1)
                        pe.matmul(ps[2 + r][:, 0:T - P * kt], ka[:, R * j + r, tile(kt)], qa[:, j, P * kt:T], start=True, stop=False)
                        pe.matmul(ps[2 + r][:, 0:T - P * kt], kb[:, R * j + r, tile(kt)], qb[:, j, P * kt:T], start=False, stop=False)
                        pe.matmul(ps[2 + r][:, 0:T - P * kt], net.pick16[0:32, r:r + 1].to_broadcast([32, P]), mT[:, j % 2, P * kt:T],
                                  start=False, stop=True).then_inc(s["keyed_in_psum"], 1)
                        if j + 1 < SETS:
                            pass1_tensor(pe, j + 1, kt, r)
                    if g >= 1:
                        apply_tensor(pe, g - 1)
                if j + 1 < SETS:
                    maxima_tensor(pe, j + 1)
            apply_tensor(pe, SETS * NT - 1)
            heads_tensor(pe, SETS - 1)
            pe.wait_ge(s["cat_ready"], SETS)
            for t in range(NT):
                last = pe.matmul(ps[0][:, tile(t)], cat[:, 32 * t:32 * t + 32, :].rearrange("p e c -> p (e c)"),
                                 w("a1_wo"), start=True, stop=True)
            last.then_inc(s["y_in_psum"], 1)

        @block.scalar
        def _(act):
            need(act)
            norm_scalar(net, s, act, ps[0])

            def first_part(i):
                act.wait_ge(s["projected"], i + 1)
                if i >= 2:
                    act.wait_ge(s["less_ready"], i - 1)
                act.activation(first[:, i % 2, :], ps[2 + i % 4][:, :], ACT.Copy).then_inc(s["first_ready"], 1)

            def second_part(i):
                act.wait_ge(s["less_ready"], i + 1)
                if i >= 2:
                    act.wait_ge(s["b_parts"], i - 1)
                act.activation(second[:, i % 2, :], less[:, i % 2, :], ACT.Copy).then_inc(s["second_ready"], 1)

            def parts(units):
                first_part(units[0])
                for i in units[1:]:
                    first_part(i)
                    second_part(i - 1)
                second_part(units[-1])

            parts(range(0, 4))
            act.wait_ge(s["v_in_psum"], 1)
            act.wait_ge(s["va_filled"], 1)
            act.activation(va[:, :, :, 0:A1_HD], OUT[:, :].rearrange("p (t h d) -> p t h d", t=NT, h=A1_H), ACT.Copy)\
               .then_inc(s["va_ready"], 1)
            parts(range(4, 2 * SETS))
            for j in range(SETS + 1):
                for kt in range(NT if j < SETS else 2):
                    if j >= 1 and kt == 1:
                        act.wait_ge(s["applied"], NT * j)
                        if j >= 2:
                            act.wait_ge(s["heads_in_psum"], j - 1)
                        act.activation(oS[:, :], OUT[:, :], ACT.Copy).then_inc(s["oS_ready"], 1)
                    if j < SETS:
                        g = j * NT + kt
                        if g >= 2:
                            act.wait_ge(s["applied"], g - 1)
                        for r in range(R):
                            act.wait_ge(s["keyed_in_psum"], R * g + r + 1)
                            act.activation(ex[:, g % 2, r, 0:T - P * kt], ps[2 + r][:, 0:T - P * kt], ACT.Exp, scale=scale)\
                               .then_inc(s["exp_done"], 1)

        @block.gpsimd
        def _(g_):
            need(g_)
            st = Steps(g_, s["pool_step"])
            st.step(g_.memset(va[:, :, :, A1_HD + 1:32], 0.0))
            st.step(g_.memset(va[:, :, :, A1_HD:A1_HD + 1], 1.0))
            g_.memset(mp[:, :, :, :], 0.0).then_inc(s["va_filled"], 1)
            norm_pool(net, s, g_, st)

        @block.vector
        def _(v_):
            need(v_)
            st = Steps(v_, s["vector_step"])
            norm_vector(net, s, v_, st)

            def a_part(i):
                j, c = i // 2, 3 * (i % 2)
                v_.wait_ge(s["first_ready"], i + 1)
                last = v_.scalar_tensor_tensor(out=(qa[:, j, :], kset[:, 0, :])[i % 2], in0=first[:, i % 2, :], scalar=w("a1_terms", c, c + 1),
                                               in1=ps[2 + i % 4][:, :], op0=ALU.mult, op1=ALU.add)
                st.step(last)
                if i >= 2:
                    v_.wait_ge(s["second_ready"], i - 1)
                v_.scalar_tensor_tensor(out=less[:, i % 2, :], in0=first[:, i % 2, :], scalar=w("a1_terms", c + 1, c + 2),
                                        in1=ps[2 + i % 4][:, :], op0=ALU.mult, op1=ALU.add).then_inc(s["less_ready"], 1)

            def b_part(i):
                j, c = i // 2, 3 * (i % 2)
                v_.wait_ge(s["less_ready"], i + 1)
                v_.wait_ge(s["second_ready"], i + 1)
                v_.scalar_tensor_tensor(out=(qb[:, j, :], kset[:, 1, :])[i % 2], in0=second[:, i % 2, :], scalar=w("a1_terms", c + 2, c + 3),
                                        in1=less[:, i % 2, :], op0=ALU.mult, op1=ALU.add).then_inc(s["b_parts"], 1)
                if i % 2:
                    by_head(kb, 1, j, "b_ready")

            def by_head(dst, which, j, signal):
                st.wait()
                v_.wait_ge(s["b_parts"], 2 * j + 2 * which)
                for r in range(R):
                    last = v_.tensor_scalar(dst[:, R * j + r, :], kset[:, which, :], w("quarter", r, r + 1), None, ALU.mult)
                last.then_inc(s[signal], 1)
                v_.wait_ge(s[signal], j + 1)

            def operands(units):
                for i in units:
                    a_part(i)
                    if i > units[0]:
                        b_part(i - 1)
                    if i % 2:
                        by_head(ka, 0, i // 2, "a_ready")
                b_part(units[-1])

            operands(range(0, 4))

            def finish(j):
                v_.wait_ge(s["heads_in_psum"], j + 1)
                heads = MISC[:, :].rearrange("p (t r f) -> p t r f", t=NT, r=R)
                st.link(v_.reciprocal(rden[:, j, :, :], heads[:, :, :, A1_HD]))
                for t in range(NT):
                    last = v_.tensor_tensor(cat[:, 32 * j:32 * j + 32, t].rearrange("p (r d) -> p r d", r=R),
                                            heads[:, t, :, 0:A1_HD], bci(rden[:, j, t, :], A1_HD), ALU.mult)
                last.then_inc(s["cat_ready"], 1)

            def causal(g):
                v_.wait_ge(s["exp_done"], R * (g + 1))
                v_.scalar_tensor_tensor(out=ex[:, g % 2, :, 0:P], in0=ex[:, g % 2, :, 0:P], scalar=3.0e38, in1=bc(w("causalT"), R),
                                        op0=ALU.min, op1=ALU.mult).then_inc(s["ex_ready"], 1)

            for j in range(SETS + 1):
                for i in range(NT):
                    if j >= 2 and i == 3:
                        finish(j - 2)
                    g = (j - 1) * NT + i
                    if g >= 1:
                        causal(g - 1)
                    for k in range(R if j < SETS else 0):
                        u = (j * NT + i) * R + k
                        t = ORDER[i]
                        n = P * (t + 1)
                        if u >= 2:
                            v_.wait_ge(s["row_max"], u - 1)
                        v_.wait_ge(s["scores_in_psum"], u + 1)
                        v_.tensor_tensor_reduce(junk[:, u % 2, 0:n], ps[u % 2][:, 0:n], w("causal", T - n, T), 1.0, -3.0e38,
                                                ALU.add, ALU.max, mx[:, j, t, k:k + 1]).then_inc(s["row_max"], 1)
                if j < SETS:
                    v_.wait_ge(s["row_max"], (j + 1) * NT * R)
                    if j == 0:
                        v_.wait_ge(s["va_filled"], 1)
                    st.link(v_.tensor_scalar(mp[:, j, :, 0:R], mx[:, j, :, :], -1.0, None, ALU.mult))
                    v_.scalar_tensor_tensor(out=mp[:, j, :, R:2 * R], in0=mx[:, j, :, :], scalar=-1.0, in1=mp[:, j, :, 0:R],
                                            op0=ALU.mult, op1=ALU.subtract).then_inc(s["mp_ready"], 1)
                    v_.wait_ge(s["maxima_in_psum"], j + 1)
                    v_.tensor_copy(mT[:, j % 2, :], MISC[0:32, :].bitcast(BF16)[:, 0:T]).then_inc(s["mT_ready"], 1)
                    if j == 0:
                        operands(range(4, 2 * SETS))
            causal(SETS * NT - 1)
            finish(SETS - 1)
            v_.wait_ge(s["y_in_psum"], 1)
            st.link(v_.tensor_tensor(net.x[:, :, :], net.x[:, :, :], ps[0][:, :].rearrange("p (t d) -> p t d", t=NT), ALU.add))

    return body




def top2_vector(net, s, v, st, values, sel, top, topi, topf):
    for t in range(NT):
        st.step(v.max(top[:, t, :], values[:, t, :]))
    st.wait()
    for t in range(NT):
        st.step(v.max_index(topi[:, t, :], top[:, t, :], values[:, t, :]))
    st.wait()
    st.link(v.tensor_copy(topf[:, :, :], topi[:, :, :]))
    for i in range(2):
        st.step(v.tensor_tensor(sel[:, i, :, :], net.w("iota8").rearrange("p (t e) -> p t e", t=NT), bci(topf[:, :, i], 8), ALU.is_equal))
    st.wait()


def l1_ffn(net):
    nc, w, ps = net.nc, net.w, net.ps
    E = M1_E
    N = 2 * E

    def body(s, sb, block, need):
        lg = sb("lg", [P, NT, E])
        gate = sb("gate", [P, NT, E])
        mx = sb("mx", [P, NT])
        den = sb("den", [P, NT])
        rden = sb("rden", [P, NT])
        top = sb("top", [P, NT, 8])
        topi = sb("topi", [P, NT, 8], U32)
        topf = sb("topf", [P, NT, 8])
        sel = sb("sel", [P, 2, NT, E])
        selT = sb("selT", [E, 2, T])
        boost = sb("boost", [P, NT, D])
        boostT = sb("boostT", [D, T])
        hT = sb("hT", [P, 2, 2, T])
        eo = sb("eo", [P, 2, NT, D])
        res = sb("res", [P, NT, D])

        @block.tensor
        def _(pe):
            need(pe)
            norm_tensor(net, s, pe, ps[0])
            pe.wait_ge(s["normT_ready"], 1)
            for t in range(NT):
                last = pe.matmul(ps[1][:, E * t:E * t + E], net.xnT[:, tile(t)], w("m1_wg"), start=True, stop=True)
            last.then_inc(s["logits_in_psum"], 1)

            def choice():
                pe.wait_ge(s["sel_ready"], 1)
                for i in range(2):
                    for t in range(NT):
                        last = pe.transpose(ps[i][0:E, tile(t)], sel[:, i, t, :], w("ident"))
                    last.then_inc(s["selT_in_psum"], 1)
                pe.wait_ge(s["selT_ready"], 2)

            def bias(i):
                for t in range(NT):
                    last = pe.matmul(ps[1][:, tile(t)], selT[:, i, tile(t)], w("m1_b2"), start=True, stop=True)
                last.then_inc(s["bias_in_psum"], 1)

            for i in range(2):
                src = net.xnT if i == 0 else boostT
                if i == 1:
                    pe.wait_ge(s["boost_ready"], 1)
                    transpose_tensor(net, s, pe, boost, ps[0], "boostT_in_psum")
                    pe.wait_ge(s["boostT_ready"], 1)
                    bias(1)
                for e in range(E + 1):
                    if i == 0 and e == 2:
                        choice()
                        bias(0)
                    if e < E:
                        n = i * E + e
                        for c in range(2):
                            if n >= 2:
                                pe.wait_ge(s["hidden_ready"], 2 * (n - 2) + c + 1)
                            pe.matmul(ps[2 + 2 * (n % 2) + c][:, :], w("m1_w1", e * M1_H + c * P, e * M1_H + (c + 1) * P),
                                      src[:, :], start=True, stop=True).then_inc(s["hidden_in_psum"], 1)
                    if e >= 1:
                        n = i * E + e - 1
                        pe.wait_ge(s["hidden_ready"], 2 * (n + 1))
                        if n >= 2:
                            pe.wait_ge(s["added"], n - 1)
                        for t in range(NT):
                            for c in range(2):
                                last = pe.matmul(ps[6 + n % 2][:, tile(t)], hT[:, n % 2, c, tile(t)],
                                                 w("m1_w2", (2 * (e - 1) + c) * D, (2 * (e - 1) + c + 1) * D),
                                                 start=(c == 0), stop=(c == 1))
                        last.then_inc(s["expert_in_psum"], 1)

        @block.scalar
        def _(act):
            need(act)
            norm_scalar(net, s, act, ps[0])
            for n in range(N):
                if n == 1:
                    act.wait_ge(s["logits_shifted"], 1)
                    act.activation(gate[:, :, :], lg[:, :, :], ACT.Exp).then_inc(s["gate_exp"], 1)
                if n == 2:
                    for i in range(2):
                        act.wait_ge(s["selT_in_psum"], i + 1)
                        act.activation(selT[:, i, :], ps[i][0:E, :], ACT.Copy).then_inc(s["selT_ready"], 1)
                if n == E:
                    act.wait_ge(s["boostT_in_psum"], 1)
                    act.activation(boostT[:, :], ps[0][:, :], ACT.Copy).then_inc(s["boostT_ready"], 1)
                for c in range(2):
                    act.wait_ge(s["hidden_in_psum"], 2 * n + c + 1)
                    if n >= 2:
                        act.wait_ge(s["expert_in_psum"], n - 1)
                    b = 2 * (n % E) + c
                    act.activation(hT[:, n % 2, c, :], ps[2 + 2 * (n % 2) + c][:, :], ACT.Relu, bias=w("m1_b1", b, b + 1))\
                       .then_inc(s["hidden_ready"], 1)

        @block.gpsimd
        def _(g):
            need(g)
            st = Steps(g, s["pool_step"])
            norm_pool(net, s, g, st)
            norm_pool(net, s, g, st, tag="out_")

        @block.vector
        def _(v):
            need(v)
            st = Steps(v, s["vector_step"])
            norm_vector(net, s, v, st)
            v.wait_ge(s["logits_in_psum"], 1)
            st.link(v.tensor_tensor(lg[:, :, :], ps[1][:, 0:NT * E].rearrange("p (t e) -> p t e", t=NT), bc(w("m1_bg"), NT), ALU.add))
            st.link(v.tensor_reduce(mx[:, :], lg[:, :, :], AX.X, ALU.max))
            v.tensor_tensor(lg[:, :, :], lg[:, :, :], bci(mx[:, :], E), ALU.subtract).then_inc(s["logits_shifted"], 1)
            v.wait_ge(s["gate_exp"], 1)
            st.link(v.tensor_reduce(den[:, :], gate[:, :, :], AX.X, ALU.add))
            st.link(v.reciprocal(rden[:, :], den[:, :]))
            st.link(v.tensor_tensor(gate[:, :, :], gate[:, :, :], bci(rden[:, :], E), ALU.mult))
            top2_vector(net, s, v, st, gate, sel, top, topi, topf)
            v.sem_inc(s["sel_ready"], 1)
            for i in range(2):
                v.wait_ge(s["bias_in_psum"], i + 1)
                st.link(v.tensor_copy(eo[:, i, :, :], ps[1][:, :].rearrange("p (t d) -> p t d", t=NT)))
                for e in range(E):
                    n = i * E + e
                    v.wait_ge(s["expert_in_psum"], n + 1)
                    if e >= 1:
                        v.wait_ge(s["added"], n)
                    for t in range(NT):
                        last = v.scalar_tensor_tensor(out=eo[:, i, t, :], in0=ps[6 + n % 2][:, tile(t)],
                                                      scalar=sel[:, i, t, e:e + 1], in1=eo[:, i, t, :],
                                                      op0=ALU.mult, op1=ALU.add)
                    last.then_inc(s["added"], 1)
                v.wait_ge(s["added"], E * (i + 1))
                if i == 0:
                    v.scalar_tensor_tensor(out=boost[:, :, :], in0=eo[:, 0, :, :], scalar=0.5, in1=net.xn[:, :, :],
                                           op0=ALU.mult, op1=ALU.add).then_inc(s["boost_ready"], 1)
            for i in range(2):
                for t in range(NT):
                    st.step(v.scalar_tensor_tensor(out=res[:, t, :], in0=eo[:, i, t, :], scalar=top[:, t, i:i + 1],
                                                   in1=(net.xn if i == 0 else res)[:, t, :], op0=ALU.mult, op1=ALU.add))
                st.wait()
            norm_vector(net, s, v, st, src=res, dst=boost, tag="out_")
            v.wait_ge(s["out_norm_ready"], NT)
            st.link(v.tensor_tensor(boost[:, :, :], boost[:, :, :], bc(w("m1_g"), NT), ALU.mult))
            st.link(v.tensor_tensor(boost[:, :, :], boost[:, :, :], bc(w("m1_b"), NT), ALU.add))
            st.link(v.tensor_tensor(net.x[:, :, :], net.x[:, :, :], boost[:, :, :], ALU.add))

    return body



A2_J = T // 32
A2_C = 64 + A2_NB + A2_M


def l2_attn(net):
    nc, w, ps = net.nc, net.w, net.ps
    J, C, GR = A2_J, A2_C, 4
    scale = A2_HD ** -0.5
    RING = (ps[0], ps[1], ps[6], ps[7])
    seg7 = C // 16

    def body(s, sb, block, need):
        xp = sb("xp", [D, 32 + T])
        qT = sb("qT", [D, T])
        kp = sb("kp", [D, 32 + T])
        t1 = sb("t1", [D, T])
        t2 = sb("t2", [D, T])
        qb = sb("qb", [D, GR, T])
        ktok = sb("ktok", [P, NT, D])
        vtok = sb("vtok", [P, NT, D])
        vall = sb("vall", [C, J, D])
        cs = sb("cs", [D, A2_NB])
        kall = sb("kall", [D, J, C])
        vcs = sb("vcs", [P, D])
        qsum = sb("qsum", [D, 1])
        imp = sb("imp", [P, A2_NB])
        top = sb("top", [P, 8])
        topi = sb("topi", [P, 8], U32)
        topf = sb("topf", [P, 8])
        pos = sb("pos", [P, A2_M])
        onehot = sb("onehot", [P, NT, A2_M])
        gl32 = sb("gl32", [32, 3 * J])
        gl = sb("gl", [P, J, 3])
        gm = sb("gm", [P, J])
        gs = sb("gs", [P, J])
        sc = sb("sc", [P, 2, GR, 4, C])
        mx7 = sb("mx7", [P, GR * 4, seg7])
        mx = sb("mx", [P, GR * 4, 3])
        sm7 = sb("sm7", [P, GR * 4, seg7])
        sm = sb("sm", [P, GR * 4, 3])
        zero = sb("zero", [P, GR * 4, 3])
        wt7 = sb("wt7", [P, 2, GR * 4, seg7])
        pT = sb("pT", [C, 2, T])
        r = sb("r", [D, 2, GR, P])
        oT = sb("oT", [D, T])

        @block.tensor
        def _(pe):
            need(pe)
            norm_tensor(net, s, pe, ps[0])
            pe.wait_ge(s["normT_ready"], 1)
            for i, key in enumerate(("a2_wk", "a2_wks", "a2_wq", "a2_wqs")):
                pe.matmul(ps[1 + i][:, :], w(key), net.xnT[:, :], start=True, stop=True).then_inc(s["qk_in_psum"], 1)
            for t in range(NT):
                last = pe.matmul(ps[5][:, tile(t)], net.xnT[:, tile(t)], w("a2_wv"), start=True, stop=True)
            last.then_inc(s["v_in_psum"], 1)
            pe.wait_ge(s["xp_ready"], 1)
            for j in range(J):
                last = pe.matmul(ps[6][0:32, 3 * j:3 * j + 3], net.xnT[:, 32 * j:32 * j + 32], w("a2_wg"), start=True, stop=True)
            last.then_inc(s["gates32_in_psum"], 1)
            pe.wait_ge(s["k_ready"], 1)
            for t in range(NT):
                last = pe.transpose(ps[1][:, tile(t)], kp[:, 32 + t * P:32 + (t + 1) * P], w("ident"))
            last.then_inc(s["ktok_in_psum"], 1)
            pe.wait_ge(s["ktok_ready"], 1)
            for t in range(NT):
                pe.matmul(ps[2][:, 0:A2_NB], ktok[:, t, :], net.wck[:, t, :], start=(t == 0), stop=False)
            pe.matmul(ps[2][:, 0:A2_NB], w("a2_pe"), w("a2_wkc"), start=False, stop=True).then_inc(s["ck_in_psum"], 1)
            pe.wait_ge(s["ck_ready"], 1)
            pe.wait_ge(s["qsum_ready"], 1)
            pe.matmul(ps[4][:, 0:A2_NB], qsum[:, 0:1].to_broadcast([D, P]), cs[:, :], start=True, stop=True)\
              .then_inc(s["importance_in_psum"], 1)
            pe.wait_ge(s["gates32_ready"], 1)
            pe.matmul(ps[6][:, 0:3 * J], w("fourfold"), gl32[:, :], start=True, stop=True).then_inc(s["gates_in_psum"], 1)
            pe.wait_ge(s["vtok_ready"], 1)
            for t in range(NT):
                pe.matmul(ps[3][64:96, 0:D], net.wcv[:, t, :], vtok[:, t, :], start=(t == 0), stop=False)
            pe.matmul(ps[3][64:96, 0:D], w("a2_wvc"), w("a2_pe"), start=False, stop=True).then_inc(s["cv_in_psum"], 1)
            pe.wait_ge(s["onehot_ready"], 1)
            for t in range(NT):
                last = pe.matmul(ps[5][:, 0:A2_M], ktok[:, t, :], onehot[:, t, :], start=(t == 0), stop=(t == NT - 1))
            last.then_inc(s["selk_in_psum"], 1)
            pe.wait_ge(s["cv_ready"], 1)
            for t in range(NT):
                last = pe.matmul(ps[3][96:96 + A2_M, 0:D], onehot[:, t, :], vtok[:, t, :], start=(t == 0), stop=(t == NT - 1))
            last.then_inc(s["selv_in_psum"], 1)
            pe.wait_ge(s["keys_ready"], 1)
            pe.wait_ge(s["gates_ready"], 1)

            def windows():
                for q in range(J // 4):
                    if q >= 2:
                        pe.wait_ge(s["vwin_ready"], q - 1)
                    for j in range(4 * q, 4 * q + 4):
                        last = pe.matmul(ps[4 + q % 2][0:64, tile(j % 4)], xp[:, 32 * j:32 * j + 64], w("a2_wv"), start=True, stop=True)
                    last.then_inc(s["vwin_in_psum"], 1)

            def scores(j):
                if j >= len(RING):
                    pe.wait_ge(s["masked"], j - len(RING) + 1)
                pe.wait_ge(s["qb_ready"], j + 1)
                for g in range(4):
                    q = qb[:, j % GR, tile(g)]
                    last = pe.matmul(RING[j % len(RING)][:, g * C:(g + 1) * C], q, kall[:, j, :], start=True, stop=True)
                last.then_inc(s["scores_in_psum"], 1)

            def apply(j):
                pe.wait_ge(s["probs_ready"], j // GR + 1)
                if j >= 2:
                    pe.wait_ge(s["pT_ready"], j - 1)
                for g in range(4):
                    last = pe.transpose(ps[2 + j % 2][0:C, tile(g)], sc[:, (j // GR) % 2, j % GR, g, :], w("ident"))
                last.then_inc(s["pT_in_psum"], 1)
                if j >= 1:
                    values(j - 1)

            def values(j):
                pe.wait_ge(s["pT_ready"], j + 1)
                if j == 0:
                    pe.wait_ge(s["vall_ready"], 1)
                    pe.wait_ge(s["vwin_ready"], J // 4)
                q = j // GR
                if q >= 2 and j % GR == 0:
                    pe.wait_ge(s["picked"], q - 1)
                for g in range(4):
                    last = pe.matmul(ps[4 + q % 2][32 * g:32 * g + 32, tile(j % GR)], vall[:, j, 32 * g:32 * g + 32],
                                     pT[:, j % 2, tile(g)], start=True, stop=True)
                last.then_inc(s["values_in_psum"], 1)

            for q in range(J // GR + 1):
                for j in range(GR * q, min(GR * q + GR, J)):
                    scores(j)
                if q == 0:
                    windows()
                for j in range(GR * (q - 1) if q else 0, GR * q):
                    apply(j)
            values(J - 1)
            pe.wait_ge(s["o_ready"], J // GR)
            for t in range(NT):
                last = pe.matmul(ps[6][:, tile(t)], oT[:, tile(t)], w("a2_wo"), start=True, stop=True)
            last.then_inc(s["y_in_psum"], 1)

        @block.scalar
        def _(act):
            need(act)
            st = Steps(act, s["scalar_step"])
            norm_scalar(net, s, act, ps[0])
            act.wait_ge(s["normT_ready"], 1)
            act.wait_ge(s["pads_ready"], 2)
            act.activation(xp[:, 32:], net.xnT[:, :], ACT.Copy).then_inc(s["xp_ready"], 1)
            act.wait_ge(s["v_in_psum"], 1)
            act.activation(vtok[:, :, :], ps[5][:, :].rearrange("p (t d) -> p t d", t=NT), ACT.Copy).then_inc(s["vtok_ready"], 1)
            act.wait_ge(s["ktok_in_psum"], 1)
            act.activation(ktok[:, :, :], ps[1][:, :].rearrange("p (t d) -> p t d", t=NT), ACT.Copy).then_inc(s["ktok_ready"], 1)
            act.wait_ge(s["ck_in_psum"], 1)
            act.activation(cs[:, :], ps[2][:, 0:A2_NB], ACT.Copy).then_inc(s["ck_ready"], 1)
            st.step(act.activation(kall[:, :, 64:64 + A2_NB], bc(ps[2][:, 0:A2_NB], J), ACT.Copy))
            act.wait_ge(s["k_ready"], 1)
            st.step(act.activation(kall[:, 0:J:2, 0:64], kp[:, 0:T].rearrange("p (j k) -> p j k", k=64), ACT.Copy))
            st.step(act.activation(kall[:, 1:J:2, 0:64], kp[:, 32:32 + T].rearrange("p (j k) -> p j k", k=64), ACT.Copy))
            act.wait_ge(s["cv_in_psum"], 1)
            act.activation(vcs[64:96, :], ps[3][64:96, 0:D], ACT.Copy).then_inc(s["cv_ready"], 1)
            act.wait_ge(s["selk_in_psum"], 1)
            act.activation(kall[:, :, 64 + A2_NB:C], bc(ps[5][:, 0:A2_M], J), ACT.Copy).then_inc(s["keys_ready"], 1)
            act.wait_ge(s["selv_in_psum"], 1)
            act.activation(vcs[96:C, :], ps[3][96:C, 0:D], ACT.Copy).then_inc(s["values_ready"], 1)
            act.wait_ge(s["gates_shifted"], 1)
            act.activation(gl[:, :, :], gl[:, :, :], ACT.Exp).then_inc(s["gates_exp"], 1)
            for q in range(J // 4):
                act.wait_ge(s["vwin_in_psum"], q + 1)
                act.activation(vall[0:64, 4 * q:4 * q + 4, :], ps[4 + q % 2][0:64, :].rearrange("p (j d) -> p j d", j=4), ACT.Copy)\
                   .then_inc(s["vwin_ready"], 1)
            def turned(i):
                act.wait_ge(s["pT_in_psum"], i + 1)
                if i >= 2:
                    act.wait_ge(s["values_in_psum"], i - 1)
                act.activation(pT[:, i % 2, :], ps[2 + i % 2][0:C, :], ACT.Copy).then_inc(s["pT_ready"], 1)

            for j in range(0, J + GR, GR):
                if j >= GR:
                    turned(j - GR)
                    turned(j - GR + 1)
                if j < J:
                    act.wait_ge(s["shifted"], j // GR + 1)
                    act.activation(sc[:, (j // GR) % 2, :, :, :], sc[:, (j // GR) % 2, :, :, :], ACT.Exp, scale=scale)\
                       .then_inc(s["exp_ready"], 1)
                if j >= GR:
                    turned(j - GR + 2)
                    turned(j - GR + 3)

        @block.gpsimd
        def _(g):
            need(g)
            st = Steps(g, s["pool_step"])
            g.memset(xp[:, 0:32], 0.0).then_inc(s["pads_ready"], 1)
            g.memset(kp[:, 0:32], 0.0).then_inc(s["pads_ready"], 1)
            norm_pool(net, s, g, st)
            g.wait_ge(s["q_ready"], 1)

            def weighted(q):
                rows7 = sc[:, q % 2, :, :, :].rearrange("p j g (n k) -> p (j g n) k", k=16)
                g.wait_ge(s["weights_ready"], q + 1)
                g.tensor_tensor(rows7, rows7, bci(wt7[:, q % 2, :, :].rearrange("p r n -> p (r n)"), 16), ALU.mult)\
                 .then_inc(s["probs_ready"], 1)

            for j in range(J):
                if j >= 2 * GR and j % GR == 0:
                    weighted(j // GR - 2)
                if j >= GR:
                    g.wait_ge(s["scores_in_psum"], j - GR + 1)
                g.tensor_tensor(qb[:, j % GR, :].rearrange("p (h q) -> p h q", h=A2_H), bc(qT[:, 32 * j:32 * j + 32], A2_H),
                                w("headmask").rearrange("p (h q) -> p h q", h=A2_H), ALU.mult).then_inc(s["qb_ready"], 1)
            weighted(J // GR - 2)
            weighted(J // GR - 1)

        @block.vector
        def _(v):
            need(v)
            st = Steps(v, s["vector_step"])
            norm_vector(net, s, v, st)
            for i, dst in enumerate((kp[:, 32:], qT[:, :])):
                v.wait_ge(s["qk_in_psum"], 2 * i + 2)
                if i == 1:
                    v.wait_ge(s["k_ready"], 1)
                st.step(v.tensor_tensor(t1[:, :], ps[1 + 2 * i][:, :], w("rope_c"), ALU.mult))
                st.link(v.tensor_tensor(t2[:, :], ps[2 + 2 * i][:, :], w("rope_s"), ALU.mult))
                v.tensor_tensor(dst, t1[:, :], t2[:, :], ALU.add).then_inc(s["k_ready" if i == 0 else "q_ready"], 1)
            v.wait_ge(s["q_ready"], 1)
            v.tensor_reduce(qsum[:, :], qT[:, :], AX.X, ALU.add).then_inc(s["qsum_ready"], 1)
            v.wait_ge(s["gates32_in_psum"], 1)
            v.tensor_copy(gl32[:, :], ps[6][0:32, 0:3 * J]).then_inc(s["gates32_ready"], 1)
            v.wait_ge(s["importance_in_psum"], 1)
            st.link(v.tensor_copy(imp[:, :], ps[4][:, 0:A2_NB]))
            st.link(v.max(top[:, :], imp[:, :]))
            st.link(v.max_index(topi[:, :], top[:, :], imp[:, :]))
            st.link(v.tensor_copy(topf[:, :], topi[:, :]))
            st.link(v.scalar_tensor_tensor(out=pos[:, :].rearrange("p (k m) -> p k m", k=A2_TOP), in0=bci(topf[:, 0:A2_TOP], A2_SB),
                                           scalar=float(A2_CB), in1=bc(w("iota", 0, A2_SB), A2_TOP), op0=ALU.mult, op1=ALU.add))
            for t in range(NT):
                last = v.tensor_scalar(onehot[:, t, :], pos[:, :], w("tokid")[:, t:t + 1], None, ALU.is_equal)
            last.then_inc(s["onehot_ready"], 1)
            msel = net.mask2[:, :, 64 + A2_NB:C]
            st.link(v.tensor_tensor(msel, bc(pos[:, :], J), bci(w("query_id"), A2_M), ALU.is_gt))
            st.link(v.tensor_scalar(msel, msel, NEG, None, ALU.mult))
            v.wait_ge(s["gates_in_psum"], 1)
            v.tensor_tensor(gl[:, :, :], ps[6][:, 0:3 * J].rearrange("p (j k) -> p j k", j=J), bc(w("a2_bg"), J), ALU.add)\
             .then_inc(s["gates_ready"], 1)
            v.wait_ge(s["gates_ready"], 1)
            st.link(v.tensor_reduce(gm[:, :], gl[:, :, :], AX.X, ALU.max))
            v.tensor_tensor(gl[:, :, :], gl[:, :, :], bci(gm[:, :], 3), ALU.subtract).then_inc(s["gates_shifted"], 1)
            v.wait_ge(s["gates_exp"], 1)
            st.link(v.tensor_reduce(gs[:, :], gl[:, :, :], AX.X, ALU.add))
            st.link(v.reciprocal(gm[:, :], gs[:, :]))
            st.link(v.tensor_tensor(gl[:, :, :], gl[:, :, :], bci(gm[:, :], 3), ALU.mult))

            def soften(q):
                b = q % 2
                rows7 = sc[:, b, :, :, :].rearrange("p j g (n k) -> p (j g n) k", k=16)
                for j in range(GR * q, GR * q + GR):
                    v.wait_ge(s["scores_in_psum"], j + 1)
                    if q >= 2:
                        v.wait_ge(s["pT_in_psum"], GR * (q - 1))
                    v.tensor_tensor(sc[:, b, j % GR, :, :], RING[j % len(RING)][:, 0:4 * C].rearrange("p (g c) -> p g c", g=4),
                                    bc(net.mask2[:, j, :], 4), ALU.add).then_inc(s["masked"], 1)
                v.wait_ge(s["masked"], GR * (q + 1))
                st.link(v.tensor_reduce(mx7[:, :, :].rearrange("p r n -> p (r n)"), rows7, AX.X, ALU.max))
                segs = ((0, 4), (4, 6), (6, 7))
                for i, (lo, hi) in enumerate(segs):
                    st.step(v.tensor_reduce(mx[:, :, i], mx7[:, :, lo:hi], AX.X, ALU.max))
                st.wait()
                for i, (lo, hi) in enumerate(segs):
                    st.step(v.tensor_scalar(mx7[:, :, lo:hi], bci(mx[:, :, i], hi - lo), -1.0e20, None, ALU.max))
                st.wait()
                v.tensor_tensor(rows7, rows7, bci(mx7[:, :, :].rearrange("p r n -> p (r n)"), 16), ALU.subtract)\
                 .then_inc(s["shifted"], 1)

            def weigh(q):
                b = q % 2
                rows7 = sc[:, b, :, :, :].rearrange("p j g (n k) -> p (j g n) k", k=16)
                segs = ((0, 4), (4, 6), (6, 7))
                v.wait_ge(s["exp_ready"], q + 1)
                st.link(v.tensor_reduce(sm7[:, :, :].rearrange("p r n -> p (r n)"), rows7, AX.X, ALU.add))
                for i, (lo, hi) in enumerate(segs):
                    st.step(v.tensor_reduce(sm[:, :, i], sm7[:, :, lo:hi], AX.X, ALU.add))
                st.wait()
                st.link(v.tensor_scalar(zero[:, :, :], sm[:, :, :], 0.0, None, ALU.is_equal))
                st.link(v.tensor_tensor(sm[:, :, :], sm[:, :, :], zero[:, :, :], ALU.add))
                st.link(v.reciprocal(zero[:, :, :], sm[:, :, :]))
                for i, k in enumerate((2, 0, 1)):
                    lo, hi = segs[i]
                    st.step(v.tensor_tensor(sm[:, :, i].rearrange("p (j g) -> p j g", g=4), zero[:, :, i].rearrange("p (j g) -> p j g", g=4),
                                            bci(gl[:, GR * q:GR * q + GR, k], 4), ALU.mult))
                st.wait()
                if q >= 2:
                    v.wait_ge(s["probs_ready"], q - 1)
                for i, (lo, hi) in enumerate(segs[1:], 1):
                    st.step(v.tensor_copy(wt7[:, b, :, lo:hi], bci(sm[:, :, i], hi - lo)))
                st.wait()
                v.tensor_copy(wt7[:, b, :, 0:4], bci(sm[:, :, 0], 4)).then_inc(s["weights_ready"], 1)

            def pick(q):
                v.wait_ge(s["values_in_psum"], GR * (q + 1))
                if q >= 2:
                    v.wait_ge(s["o_ready"], q - 1)
                v.tensor_tensor(r[:, q % 2, :, :], ps[4 + q % 2][:, :].rearrange("p (j c) -> p j c", j=GR),
                                bc(w("quadmask"), GR), ALU.mult).then_inc(s["picked"], 1)
                v.wait_ge(s["picked"], q + 1)
                v.tensor_reduce(oT[:, P * q:P * (q + 1)].rearrange("p (j q) -> p j q", j=GR),
                                r[:, q % 2, :, :].rearrange("p j (h q) -> p j q h", h=4), AX.X, ALU.add)\
                 .then_inc(s["o_ready"], 1)

            for q in range(J // GR):
                soften(q)
                if q == 0:
                    v.wait_ge(s["values_ready"], 1)
                    v.tensor_copy(vall[64:C, :, :], bc(vcs[64:C, :], J)).then_inc(s["vall_ready"], 1)
                if q >= 2:
                    pick(q - 2)
                weigh(q)
            pick(J // GR - 2)
            pick(J // GR - 1)
            st.link(v.tensor_tensor(net.x[:, :, :], net.x[:, :, :], bc(w("a2_bo"), NT), ALU.add))
            v.wait_ge(s["y_in_psum"], 1)
            st.link(v.tensor_tensor(net.x[:, :, :], net.x[:, :, :], ps[6][:, :].rearrange("p (t d) -> p t d", t=NT), ALU.add))

    return body




def l2_ffn(net):
    nc, w, ps = net.nc, net.w, net.ps
    E = M2_E
    C = E * M2_H // P

    def body(s, sb, block, need):
        lg = sb("lg", [P, NT, E])
        top = sb("top", [P, NT, 8])
        topi = sb("topi", [P, NT, 8], U32)
        topf = sb("topf", [P, NT, 8])
        sel = sb("sel", [P, 2, NT, E])
        g2 = sb("g2", [P, NT, 2])
        den = sb("den", [P, NT])
        rden = sb("rden", [P, NT])
        gate = sb("gate", [P, NT, E])
        gateT = sb("gateT", [E, T])
        h = sb("h", [P, C, T])
        hg = sb("hg", [P, C, T])

        @block.tensor
        def _(pe):
            need(pe)
            norm_tensor(net, s, pe, ps[0])
            pe.wait_ge(s["normT_ready"], 1)
            for t in range(NT):
                last = pe.matmul(ps[1][:, E * t:E * t + E], net.xnT[:, tile(t)], w("m2_wg"), start=True, stop=True)
            last.then_inc(s["logits_in_psum"], 1)
            for c in range(C):
                pe.matmul(ps[2 + c][:, :], w("m2_wd", c * P, (c + 1) * P), net.xnT[:, :], start=True, stop=True)\
                  .then_inc(s["hidden_in_psum"], 1)
            pe.wait_ge(s["gate_ready"], 1)
            for t in range(NT):
                last = pe.transpose(ps[6][0:E, tile(t)], gate[:, t, :], w("ident"))
            last.then_inc(s["gateT_in_psum"], 1)
            pe.wait_ge(s["gateT_ready"], 1)
            for c in range(C):
                pe.wait_ge(s["hidden_ready"], c + 1)
                pe.matmul(ps[2 + c][:, :], w("pairpick", c * P, (c + 1) * P), gateT[:, :], start=True, stop=True)\
                  .then_inc(s["spread_in_psum"], 1)
            pe.wait_ge(s["gated"], C)
            for t in range(NT):
                for c in range(C):
                    pe.matmul(ps[7][:, tile(t)], hg[:, c, tile(t)], w("m2_wu", c * D, (c + 1) * D), start=(c == 0), stop=False)
                last = pe.matmul(ps[7][:, tile(t)], gateT[:, tile(t)], w("m2_bu"), start=False, stop=True)
            last.then_inc(s["y_in_psum"], 1)

        @block.scalar
        def _(act):
            need(act)
            norm_scalar(net, s, act, ps[0])
            for c in range(C):
                act.wait_ge(s["hidden_in_psum"], c + 1)
                act.activation(h[:, c, :], ps[2 + c][:, :], ACT.Relu, bias=w("m2_bd", c, c + 1)).then_inc(s["hidden_ready"], 1)
            act.wait_ge(s["top_shifted"], 1)
            act.activation(g2[:, :, :], g2[:, :, :], ACT.Exp).then_inc(s["top_exp"], 1)
            act.wait_ge(s["gateT_in_psum"], 1)
            act.activation(gateT[:, :], ps[6][0:E, :], ACT.Copy).then_inc(s["gateT_ready"], 1)

        @block.gpsimd
        def _(g):
            need(g)
            norm_pool(net, s, g, Steps(g, s["pool_step"]))

        @block.vector
        def _(v):
            need(v)
            st = Steps(v, s["vector_step"])
            norm_vector(net, s, v, st)
            v.wait_ge(s["logits_in_psum"], 1)
            st.link(v.tensor_copy(lg[:, :, :], ps[1][:, 0:NT * E].rearrange("p (t e) -> p t e", t=NT)))
            top2_vector(net, s, v, st, lg, sel, top, topi, topf)
            v.tensor_tensor(g2[:, :, :], top[:, :, 0:2], bci(top[:, :, 0], 2), ALU.subtract).then_inc(s["top_shifted"], 1)
            v.wait_ge(s["top_exp"], 1)
            st.link(v.tensor_reduce(den[:, :], g2[:, :, :], AX.X, ALU.add))
            st.link(v.reciprocal(rden[:, :], den[:, :]))
            st.link(v.scalar_tensor_tensor(out=g2[:, :, :], in0=g2[:, :, :], scalar=0.5, in1=bci(rden[:, :], 2), op0=ALU.mult, op1=ALU.mult))
            for i in range(2):
                st.step(v.tensor_tensor(sel[:, i, :, :], sel[:, i, :, :], bci(g2[:, :, i], E), ALU.mult))
            st.wait()
            v.tensor_tensor(gate[:, :, :], sel[:, 0, :, :], sel[:, 1, :, :], ALU.add).then_inc(s["gate_ready"], 1)
            for c in range(C):
                v.wait_ge(s["spread_in_psum"], c + 1)
                v.tensor_tensor(hg[:, c, :], h[:, c, :], ps[2 + c][:, :], ALU.mult).then_inc(s["gated"], 1)
            v.wait_ge(s["y_in_psum"], 1)
            st.link(v.tensor_tensor(net.x[:, :, :], net.x[:, :, :], ps[7][:, :].rearrange("p (t d) -> p t d", t=NT), ALU.add))

    return body




def l3_attn(net):
    nc, w, ps = net.nc, net.w, net.ps
    C, NS, R = A3_C, A3_N, A3_R
    N = NS * C
    PAD = A3_K - 1

    def body(s, sb, block, need):
        hn = sb("hn", [P, NT, D])
        hT = sb("hT", [D, T])
        xp = sb("xp", [P, C, PAD + T])
        sg = sb("sg", [P, C, T])
        cv = sb("cv", [P, C, T])
        sgc = sb("sgc", [P, C, T])
        xs = sb("xs", [P, C, T])
        dbc = sb("dbc", [R, T])
        bc3 = sb("bc3", [96, T])
        part = sb("part", [96, T], BF16)
        parts = sb("parts", [96, T], BF16)
        z, e = cv, sgc
        ln = sb("ln", [P, C, T])
        d = sb("d", [P, C, T])
        dt = sb("dt", [P, C, T])
        dtx = xp[:, :, PAD:]
        bn = sb("bn", [P, 2, T])
        da = sb("da", [P, 3, T])
        u = sb("u", [P, 3, T])
        h = sb("h", [P, 2, T])
        hc = sb("hc", [P, 2, T])
        yT = ln

        @block.tensor
        def _(pe):
            need(pe)
            norm_tensor(net, s, pe, ps[0], src=hn, tag="inner_")
            pe.wait_ge(s["hT_ready"], 1)
            for c in range(2 * C):
                pe.matmul(ps[1 + c][:, :], w("a3_win", c * P, (c + 1) * P), hT[:, :], start=True, stop=True)\
                  .then_inc(s["proj_in_psum"], 1)
            for c in range(C):
                pe.wait_ge(s["xs_ready"], c + 1)
                last = pe.matmul(ps[5][0:R, :], w("a3_wx", c * 160, c * 160 + R), xs[:, c, :],
                                 start=(c == 0), stop=(c == C - 1))
            last.then_inc(s["dbc_in_psum"], 1)
            pe.wait_ge(s["xp_ready"], 1)
            for c in range(C):
                last = pe.matmul(ps[1][0:96, :], w("a3_wx", c * 160 + R, (c + 1) * 160), xs[:, c, :],
                                 start=(c == 0), stop=(c == C - 1))
            last.then_inc(s["bc_in_psum"], 1)
            pe.wait_ge(s["dbc_ready"], 1)
            for c in range(C):
                pe.matmul(ps[6 + c][:, :], w("a3_wdt", c * P, (c + 1) * P), dbc[0:R, :], start=True, stop=True)\
                  .then_inc(s["dt_in_psum"], 1)
            pe.wait_ge(s["sigmoids_ready"], C)
            pe.wait_ge(s["parts_ready"], 1)
            for n in range(NS + 1):
                if n < NS:
                    if n >= 2:
                        pe.wait_ge(s["bn_ready"], n - 1)
                    pe.matmul(ps[n % 2][:, :], net.part16[0:96, n:n + 1].to_broadcast([96, P]), parts[:, :],
                              start=True, stop=True).then_inc(s["b_in_psum"], 1)
                    if n >= 2:
                        pe.wait_ge(s["hc_ready"], C * (n - 1))
                    pe.matmul(ps[2 + n % 2][:, :], net.part16[0:96, NS + n:NS + n + 1].to_broadcast([96, P]), parts[:, :],
                              start=True, stop=True).then_inc(s["c_in_psum"], 1)
                if n >= 1:
                    for c in range(C):
                        i = C * (n - 1) + c
                        pe.wait_ge(s["hc_ready"], i + 1)
                        pe.matmul(ps[4 + c][:, :], w("ident"), hc[:, i % 2, :], start=(n == 1), stop=(n == NS))\
                          .then_inc(s["state_added"], 1)
            pe.wait_ge(s["yT_ready"], C)
            for t in range(NT):
                for c in range(C):
                    last = pe.matmul(ps[0][:, tile(t)], yT[:, c, tile(t)], w("a3_wout", c * D, (c + 1) * D),
                                     start=(c == 0), stop=(c == C - 1))
            last.then_inc(s["y_in_psum"], 1)

        @block.scalar
        def _(act):
            need(act)
            st = Steps(act, s["scalar_step"])
            act.wait_ge(s["inner_normT_in_psum"], 1)
            act.activation(hT[:, :], ps[0][:, :], ACT.Identity, bias=w("a3_b"), scale=w("a3_g")).then_inc(s["hT_ready"], 1)
            for c in range(C):
                act.wait_ge(s["proj_in_psum"], c + 1)
                act.activation(xp[:, c, PAD:], ps[1 + c][:, :], ACT.Identity, bias=w("a3_bin", c, c + 1)).then_inc(s["xp_ready"], 1)
            for c in range(C):
                act.wait_ge(s["proj_in_psum"], C + c + 1)
                act.activation(sg[:, c, :], ps[3 + c][:, :], ACT.Sigmoid, bias=w("a3_bin", C + c, C + c + 1))\
                   .then_inc(s["sigmoids_ready"], 1)
            for c in range(C):
                act.wait_ge(s["conv_ready"], c + 1)
                act.activation(sgc[:, c, :], cv[:, c, :], ACT.Sigmoid).then_inc(s["conv_sigmoid"], 1)
            act.wait_ge(s["dbc_in_psum"], 1)
            act.activation(dbc[:, :], ps[5][0:R, :], ACT.Copy).then_inc(s["dbc_ready"], 1)
            act.wait_ge(s["dt_in_psum"], C)
            for c in range(C):
                st.step(act.activation(z[:, c, :], ps[6 + c][:, :], ACT.Identity, bias=w("a3_bdt", c, c + 1)))
            for c in range(C):
                st.step(act.activation(e[:, c, :], ps[6 + c][:, :], ACT.Abs, bias=w("a3_bdt", c, c + 1)))
            st.wait()
            for c in range(C):
                act.activation(e[:, c, :], e[:, c, :], ACT.Exp, scale=-1.0).then_inc(s["e_ready"], 1)
            act.wait_ge(s["e_ready"], C)
            for c in range(C):
                act.activation(ln[:, c, :], e[:, c, :], ACT.Ln, bias=1.0).then_inc(s["ln_ready"], 1)
            for i in range(N):
                n, c = divmod(i, C)
                if c == 0:
                    act.wait_ge(s["b_in_psum"], n + 1)
                    if n >= 2:
                        act.wait_ge(s["u_ready"], C * (n - 1))
                    act.activation(bn[:, n % 2, :], ps[n % 2][:, :], ACT.Copy).then_inc(s["bn_ready"], 1)
                if i == 0:
                    act.wait_ge(s["dt_ready"], C)
                if i >= 3:
                    act.wait_ge(s["scanned"], i - 2)
                act.activation(da[:, i % 3, :], dt[:, c, :], ACT.Exp, scale=net.a3[:, c, n:n + 1]).then_inc(s["da_ready"], 1)

        @block.gpsimd
        def _(g):
            need(g)
            st = Steps(g, s["pool_step"])
            g.memset(xp[:, :, 0:PAD], 0.0).then_inc(s["pad_ready"], 1)
            norm_pool(net, s, g, st)
            norm_pool(net, s, g, st, tag="inner_")
            g.wait_ge(s["dtx_ready"], C)
            for i in range(N):
                n, c = divmod(i, C)
                g.wait_ge(s["bn_ready"], n + 1)
                if i >= 3:
                    g.wait_ge(s["scanned"], i - 2)
                g.tensor_tensor(u[:, i % 3, :], dtx[:, c, :], bn[:, n % 2, :], ALU.mult).then_inc(s["u_ready"], 1)

        @block.vector
        def _(v):
            need(v)
            st = Steps(v, s["vector_step"])
            norm_vector(net, s, v, st)
            v.wait_ge(s["norm_ready"], NT)
            norm_vector(net, s, v, st, src=net.xn, dst=hn, tag="inner_")
            v.wait_ge(s["pad_ready"], 1)
            for c in range(C):
                v.wait_ge(s["xp_ready"], c + 1)
                k = A3_K * c
                st.link(v.tensor_scalar(cv[:, c, :], xp[:, c, 0:T], w("a3_cw", k, k + 1), w("a3_cb", c, c + 1), ALU.mult, ALU.add))
                for j in range(1, A3_K):
                    last = v.scalar_tensor_tensor(out=cv[:, c, :], in0=xp[:, c, j:j + T], scalar=w("a3_cw", k + j, k + j + 1),
                                                  in1=cv[:, c, :], op0=ALU.mult, op1=ALU.add)
                    if j < A3_K - 1:
                        st.link(last)
                    else:
                        last.then_inc(s["conv_ready"], 1)
            for c in range(C):
                v.wait_ge(s["conv_ready"], c + 1)
                v.wait_ge(s["conv_sigmoid"], c + 1)
                v.tensor_tensor(xs[:, c, :], cv[:, c, :], sgc[:, c, :], ALU.mult).then_inc(s["xs_ready"], 1)
            v.wait_ge(s["bc_in_psum"], 1)
            st.step(v.tensor_copy(bc3[:, :], ps[1][0:96, :]))
            st.link(v.tensor_copy(part[:, :], ps[1][0:96, :]))
            st.link(v.scalar_tensor_tensor(out=bc3[:, :], in0=part[:, :], scalar=w("a3_parts", 0, 1)[0:96, :], in1=bc3[:, :],
                                           op0=ALU.mult, op1=ALU.add))
            st.link(v.tensor_copy(part[:, :], bc3[:, :]))
            v.scalar_tensor_tensor(out=parts[:, :], in0=part[:, :], scalar=w("a3_parts", 1, 2)[0:96, :], in1=bc3[:, :],
                                   op0=ALU.mult, op1=ALU.add).then_inc(s["parts_ready"], 1)
            for c in range(C):
                v.wait_ge(s["e_ready"], c + 1)
                st.link(v.tensor_scalar(d[:, c, :], e[:, c, :], 1.0, -1.0, ALU.add, ALU.add))
                st.link(v.tensor_tensor(d[:, c, :], e[:, c, :], d[:, c, :], ALU.subtract))
            for c in range(C):
                v.wait_ge(s["ln_ready"], c + 1)
                st.link(v.tensor_tensor(ln[:, c, :], ln[:, c, :], d[:, c, :], ALU.add))
                v.scalar_tensor_tensor(out=dt[:, c, :], in0=z[:, c, :], scalar=0.0, in1=ln[:, c, :], op0=ALU.max, op1=ALU.add)\
                 .then_inc(s["dt_ready"], 1)
                v.wait_ge(s["dt_ready"], c + 1)
                v.tensor_tensor(dtx[:, c, :], dt[:, c, :], xs[:, c, :], ALU.mult).then_inc(s["dtx_ready"], 1)
            for i in range(N):
                n, c = divmod(i, C)
                v.wait_ge(s["da_ready"], i + 1)
                v.wait_ge(s["u_ready"], i + 1)
                if i >= 2:
                    v.wait_ge(s["hc_ready"], i - 1)
                v.tensor_tensor_scan(h[:, i % 2, :], da[:, i % 3, :], u[:, i % 3, :], 0.0, ALU.mult, ALU.add).then_inc(s["scanned"], 1)
                v.wait_ge(s["scanned"], i + 1)
                v.wait_ge(s["c_in_psum"], n + 1)
                if i >= 2:
                    v.wait_ge(s["state_added"], i - 1)
                v.tensor_tensor(hc[:, i % 2, :], h[:, i % 2, :], ps[2 + n % 2][:, :], ALU.mult).then_inc(s["hc_ready"], 1)
            v.wait_ge(s["state_added"], N)
            for c in range(C):
                st.link(v.scalar_tensor_tensor(out=yT[:, c, :], in0=xs[:, c, :], scalar=w("a3_d", c, c + 1), in1=ps[4 + c][:, :],
                                               op0=ALU.mult, op1=ALU.add))
                v.tensor_tensor(yT[:, c, :], yT[:, c, :], sg[:, c, :], ALU.mult).then_inc(s["yT_ready"], 1)
            st.link(v.tensor_tensor(net.x[:, :, :], net.x[:, :, :], bc(w("a3_bout"), NT), ALU.add))
            st.link(v.tensor_tensor(net.x[:, :, :], net.x[:, :, :], net.xn[:, :, :], ALU.add))
            v.wait_ge(s["y_in_psum"], 1)
            st.link(v.tensor_tensor(net.x[:, :, :], net.x[:, :, :], ps[0][:, :].rearrange("p (t d) -> p t d", t=NT), ALU.add))

    return body




def l3_xattn(net):
    nc, w, ps = net.nc, net.w, net.ps
    H, M = X3_H, 2 * X3_H
    PER = 6
    BANKS = [(0, 6), (6, 12), (12, 16)]
    RING = 5
    LAG = 2
    scale = X3_SD ** -0.5

    def body(s, sb, block, need):
        qT = sb("qT", [D, T])
        kT = sb("kT", [D, S2])
        km = sb("km", [D, M, S2])
        va = sb("va", [S2, H, 32])
        mx = sb("mx", [P, 2, H])
        sc = sb("sc", [P, 6, H, S2])
        den = sb("den", [P, 3, 2, H])
        rden = sb("rden", [P, 3, 2, H])
        co = sb("co", [P, 3, H])
        wT = sb("wT", [S2, 2, 4, P])
        o = sb("o", [P, NT, T])

        @block.tensor
        def _(pe):
            need(pe)
            pe.matmul(ps[6][:, 0:S2], w("x3_wk"), net.ctxT[:, :], start=True, stop=True).then_inc(s["k_in_psum"], 1)
            pe.matmul(ps[7][0:S2, 0:D], net.ctxT[:, :], w("x3_wv"), start=True, stop=True).then_inc(s["v_in_psum"], 1)
            norm_tensor(net, s, pe, ps[0])
            pe.wait_ge(s["normT_ready"], 1)
            pe.matmul(ps[1][:, :], w("x3_wq"), net.xnT[:, :], start=True, stop=True).then_inc(s["q_in_psum"], 1)
            pe.wait_ge(s["q_ready"], 1)
            pe.wait_ge(s["km_ready"], 1)
            pe.wait_ge(s["v_ready"], 1)

            def scores(i):
                t, half = divmod(i, 2)
                for b, (lo, hi) in enumerate(BANKS):
                    u = 3 * i + b
                    if u >= RING:
                        pe.wait_ge(s["shifted"], u - RING + 1)
                    pe.matmul(ps[u % RING][:, 0:(hi - lo) * S2], qT[:, tile(t)],
                              km[:, half * H + lo:half * H + hi, :].rearrange("p m k -> p (m k)"), start=True, stop=True)\
                      .then_inc(s["scores_in_psum"], 1)

            def apply(t):
                pe.wait_ge(s["weights_ready"], t + 1)
                for g in range(H // 4 + 1):
                    n = 4 * t + g
                    if g < H // 4:
                        if n >= 2:
                            pe.wait_ge(s["wT_ready"], n - 1)
                        for k in range(4):
                            last = pe.transpose(ps[5 + n % 2][0:S2, tile(k)], sc[:, 2 * (t % 3), 4 * g + k, :], w("ident"))
                        last.then_inc(s["wT_in_psum"], 1)
                    if g >= 1:
                        n -= 1
                        pe.wait_ge(s["wT_ready"], n + 1)
                        if g == 1 and t >= 1:
                            pe.wait_ge(s["o_ready"], t)
                        for k in range(4):
                            last = pe.matmul(ps[7][32 * k:32 * k + 32, tile(g - 1)], va[:, 4 * (g - 1) + k, :], wT[:, n % 2, k, :],
                                             start=True, stop=True)
                        last.then_inc(s["heads_done"], 1)

            for t in range(NT + LAG):
                if t < NT:
                    scores(2 * t)
                    scores(2 * t + 1)
                if t >= LAG:
                    apply(t - LAG)
            for t in range(NT):
                pe.wait_ge(s["o_ready"], t + 1)
                for g in range(4):
                    last = pe.matmul(ps[1][:, tile(t)], o[:, t, tile(g)], w("x3_wo", g * D, (g + 1) * D), start=(g == 0), stop=(g == 3))
            last.then_inc(s["y_in_psum"], 1)

        @block.scalar
        def _(act):
            need(act)
            act.wait_ge(s["k_in_psum"], 1)
            act.activation(kT[:, :], ps[6][:, 0:S2], ACT.Identity, bias=w("x3_bk")).then_inc(s["k_ready"], 1)
            norm_scalar(net, s, act, ps[0])
            act.wait_ge(s["q_in_psum"], 1)
            act.activation(qT[:, :], ps[1][:, :], ACT.Identity, bias=w("x3_bq")).then_inc(s["q_ready"], 1)
            for t in range(NT + LAG):
                if t < NT:
                    for half in range(2):
                        i = 2 * t + half
                        act.wait_ge(s["shifted"], 3 * (i + 1))
                        act.activation(sc[:, i % 6, :, :], sc[:, i % 6, :, :], ACT.Exp, scale=scale).then_inc(s["exp_ready"], 1)
                if t >= LAG:
                    for n in range(4 * (t - LAG), 4 * (t - LAG) + 4):
                        act.wait_ge(s["wT_in_psum"], n + 1)
                        if n >= 2:
                            act.wait_ge(s["heads_done"], n - 1)
                        act.activation(wT[:, n % 2, :, :], ps[5 + n % 2][0:S2, :].rearrange("p (h t) -> p h t", h=4), ACT.Copy)\
                           .then_inc(s["wT_ready"], 1)
                    act.wait_ge(s["heads_done"], 4 * (t - LAG) + 4)
                    act.activation(o[:, t - LAG, :], ps[7][:, :], ACT.Copy, scale=0.8).then_inc(s["o_ready"], 1)

        @block.gpsimd
        def _(g):
            need(g)
            st = Steps(g, s["pool_step"])
            g.memset(va[:, :, :], 0.0).then_inc(s["va_zeroed"], 1)
            norm_pool(net, s, g, st)
            for t in range(NT):
                b = t % 3
                g.wait_ge(s["factors_ready"], t + 1)
                st.step(g.tensor_tensor(sc[:, 2 * b + 1, :, :], sc[:, 2 * b + 1, :, :], bci(co[:, b, :], S2), ALU.mult))
                st.link(g.tensor_tensor(sc[:, 2 * b, :, :], sc[:, 2 * b, :, :], bci(rden[:, b, 0, :], S2), ALU.mult))
                g.tensor_tensor(sc[:, 2 * b, :, :], sc[:, 2 * b, :, :], sc[:, 2 * b + 1, :, :], ALU.add).then_inc(s["weights_ready"], 1)

        @block.vector
        def _(v):
            need(v)
            st = Steps(v, s["vector_step"])
            norm_vector(net, s, v, st)
            v.wait_ge(s["v_in_psum"], 1)
            v.wait_ge(s["va_zeroed"], 1)
            v.tensor_tensor(va[:, :, 0:8], ps[7][0:S2, 0:D].rearrange("p (h d) -> p h d", h=H),
                            w("x3_bv")[0:S2, :].rearrange("p (h d) -> p h d", h=H), ALU.add).then_inc(s["v_ready"], 1)
            v.wait_ge(s["k_ready"], 1)
            v.tensor_tensor(km[:, :, :], bc(kT[:, :], M), bci(w("submap"), S2), ALU.mult).then_inc(s["km_ready"], 1)

            def soften(i):
                half = i % 2
                for b, (lo, hi) in enumerate(BANKS):
                    v.wait_ge(s["scores_in_psum"], 3 * i + b + 1)
                    st.step(v.tensor_reduce(mx[:, half, lo:hi], ps[(3 * i + b) % RING][:, 0:(hi - lo) * S2].rearrange("p (m k) -> p m k", k=S2),
                                            AX.X, ALU.max))
                st.wait()
                if i >= 6:
                    v.wait_ge(s["wT_in_psum"], 4 * (i // 2 - 2))
                for b, (lo, hi) in enumerate(BANKS):
                    v.tensor_tensor(sc[:, i % 6, lo:hi, :], ps[(3 * i + b) % RING][:, 0:(hi - lo) * S2].rearrange("p (m k) -> p m k", k=S2),
                                    bci(mx[:, half, lo:hi], S2), ALU.subtract).then_inc(s["shifted"], 1)

            def weigh(t):
                b = t % 3
                for half in range(2):
                    v.wait_ge(s["exp_ready"], 2 * t + half + 1)
                    st.step(v.tensor_reduce(den[:, b, half, :], sc[:, 2 * b + half, :, :], AX.X, ALU.add))
                st.wait()
                if t >= 3:
                    v.wait_ge(s["weights_ready"], t - 2)
                st.link(v.reciprocal(rden[:, b, :, :], den[:, b, :, :]))
                v.tensor_scalar(co[:, b, :], rden[:, b, 1, :], net.neglam[:, 0:1], None, ALU.mult).then_inc(s["factors_ready"], 1)

            for t in range(NT):
                soften(2 * t)
                soften(2 * t + 1)
                weigh(t)
            st.link(v.tensor_tensor(net.x[:, :, :], net.x[:, :, :], bc(w("x3_bo"), NT), ALU.add))
            v.wait_ge(s["y_in_psum"], 1)
            st.link(v.tensor_tensor(net.x[:, :, :], net.x[:, :, :], ps[1][:, :].rearrange("p (t d) -> p t d", t=NT), ALU.add))

    return body



ROUND = 1.5 * 2.0 ** 23


def quantise(net, v, st, x, n, work, out, mx, back, inv, signal):
    st.link(v.tensor_reduce(mx, x, AX.X, ALU.max, apply_absolute_value=True))
    st.link(v.tensor_scalar(mx, mx, 1e-5, None, ALU.max))
    st.step(v.tensor_scalar(back, mx, 1.0 / 127.0, None, ALU.mult))
    st.link(v.reciprocal(inv, mx))
    st.link(v.tensor_scalar(inv, inv, 127.0, None, ALU.mult))
    st.link(v.tensor_scalar(work, x, inv, ROUND, ALU.mult, ALU.add))
    st.link(v.tensor_scalar(work, work, -ROUND, 127.0, ALU.add, ALU.min))
    v.tensor_scalar(out, work, -128.0, None, ALU.max).then_inc(signal, 1)


def l3_ffn(net):
    nc, w, ps = net.nc, net.w, net.ps
    C = F3_IN // P

    def body(s, sb, block, need):
        work = sb("work", [P, 2, F3_IN])
        xq = sb("xq", [P, NT, D], BF16)
        xqT = sb("xqT", [D, T], BF16)
        mx = sb("mx", [P, NT])
        inv = sb("inv", [P, NT])
        back = sb("back", [P, NT])
        fg = sb("fg", [P, NT])
        fu = sb("fu", [P, NT])
        mx2 = sb("mx2", [P, NT])
        inv2 = sb("inv2", [P, NT])
        back2 = sb("back2", [P, NT])
        fd = sb("fd", [P, NT])
        g = sb("g", [P, 2, F3_IN])
        p = sb("p", [P, 2, F3_IN])
        pq = sb("pq", [P, 2, F3_IN], BF16)
        pT = sb("pT", [P, 2, F3_IN], BF16)

        @block.tensor
        def _(pe):
            need(pe)
            pe.wait_ge(s["x_quantised"], NT)
            bank = ps[0][:, :].bitcast(BF16)
            for t in range(NT):
                last = pe.transpose(bank[:, tile(t)], xq[:, t, :], net.ident16[:, :])
            last.then_inc(s["xqT_in_psum"], 1)
            pe.wait_ge(s["xqT_ready"], 1)

            def up(t):
                if t >= 2:
                    pe.wait_ge(s["products_ready"], t - 1)
                pe.matmul(ps[1 + 2 * (t % 2)][:, :], xqT[:, tile(t)], net.q3[:, 0, :], start=True, stop=True)\
                  .then_inc(s["gate_in_psum"], 1)
                pe.matmul(ps[2 + 2 * (t % 2)][:, :], xqT[:, tile(t)], net.q3[:, 1, :], start=True, stop=True)\
                  .then_inc(s["up_in_psum"], 1)

            def down(t):
                pe.wait_ge(s["p_quantised"], t + 1)
                b = ps[5 + t % 2][:, :].bitcast(BF16)
                if t >= 2:
                    pe.wait_ge(s["pT_ready"], t - 1)
                for c in range(C):
                    last = pe.transpose(b[:, tile(c)], pq[:, t % 2, tile(c)], net.ident16[:, :])
                last.then_inc(s["pT_in_psum"], 1)
                pe.wait_ge(s["pT_ready"], t + 1)
                for c in range(C):
                    last = pe.matmul(ps[7][:, tile(t)], pT[:, t % 2, tile(c)], net.q3[:, 2, tile(c)], start=(c == 0), stop=(c == C - 1))
                last.then_inc(s["y_in_psum"], 1)

            up(0)
            for t in range(NT):
                if t + 1 < NT:
                    up(t + 1)
                down(t)

        @block.scalar
        def _(act):
            need(act)
            act.wait_ge(s["xqT_in_psum"], 1)
            act.activation(xqT[:, :], ps[0][:, :].bitcast(BF16)[:, 0:T], ACT.Copy).then_inc(s["xqT_ready"], 1)
            act.wait_ge(s["factors_ready"], 1)

            def gate(t):
                act.wait_ge(s["gate_in_psum"], t + 1)
                if t >= 2:
                    act.wait_ge(s["products_ready"], t - 1)
                act.activation(g[:, t % 2, :], ps[1 + 2 * (t % 2)][:, :], ACT.Silu, scale=fg[:, t:t + 1]).then_inc(s["gate_ready"], 1)

            gate(0)
            for t in range(NT):
                if t + 1 < NT:
                    gate(t + 1)
                act.wait_ge(s["pT_in_psum"], t + 1)
                if t >= 2:
                    act.wait_ge(s["y_in_psum"], t - 1)
                act.activation(pT[:, t % 2, :], ps[5 + t % 2][:, :].bitcast(BF16)[:, 0:F3_IN], ACT.Copy).then_inc(s["pT_ready"], 1)

        @block.gpsimd
        def _(gp):
            need(gp)
            norm_pool(net, s, gp, Steps(gp, s["pool_step"]))

        @block.vector
        def _(v):
            need(v)
            st = Steps(v, s["vector_step"])
            norm_vector(net, s, v, st)
            v.wait_ge(s["norm_ready"], NT)
            for t in range(NT):
                if t >= 2:
                    v.wait_ge(s["x_quantised"], t - 1)
                quantise(net, v, st, net.xn[:, t, :], D, work[:, t % 2, 0:D], xq[:, t, :], mx[:, t:t + 1], back[:, t:t + 1],
                         inv[:, t:t + 1], s["x_quantised"])
            st.step(v.tensor_scalar(fg[:, :], back[:, :], net.mean3[:, 0:1], None, ALU.mult))
            v.tensor_scalar(fu[:, :], back[:, :], net.mean3[:, 1:2], None, ALU.mult).then_inc(s["factors_ready"], 1)
            v.wait_ge(s["factors_ready"], 1)
            v.wait_ge(s["x_quantised"], NT)
            for t in range(NT):
                v.wait_ge(s["up_in_psum"], t + 1)
                v.wait_ge(s["gate_ready"], t + 1)
                if t >= 2:
                    v.wait_ge(s["p_quantised"], t - 1)
                v.scalar_tensor_tensor(out=p[:, t % 2, :], in0=ps[2 + 2 * (t % 2)][:, :], scalar=fu[:, t:t + 1], in1=g[:, t % 2, :],
                                       op0=ALU.mult, op1=ALU.mult).then_inc(s["products_ready"], 1)
                v.wait_ge(s["products_ready"], t + 1)
                if t >= 2:
                    v.wait_ge(s["pT_in_psum"], t - 1)
                quantise(net, v, st, p[:, t % 2, :], F3_IN, work[:, t % 2, :], pq[:, t % 2, :], mx2[:, t:t + 1], back2[:, t:t + 1],
                         inv2[:, t:t + 1], s["p_quantised"])
            st.link(v.tensor_scalar(fd[:, :], back2[:, :], net.mean3[:, 2:3], None, ALU.mult))
            v.wait_ge(s["y_in_psum"], NT)
            for t in range(NT):
                st.step(v.scalar_tensor_tensor(out=net.x[:, t, :], in0=ps[7][:, tile(t)], scalar=fd[:, t:t + 1], in1=net.x[:, t, :],
                                               op0=ALU.mult, op1=ALU.add))
            st.wait()

    return body




def setup_tables(net, ctx):
    net.y = net.sb("y", [P, NT, D])
    net.mask2 = net.sb("mask2", [P, A2_J, A2_C])
    net.wck = net.sb("wck", [P, NT, A2_NB])
    net.wcv = net.sb("wcv", [P, NT, A2_NB])
    net.a3 = net.sb("a3", [P, A3_C, A3_N])
    net.neglam = net.sb("neglam", [P, 1])
    net.mean3 = net.sb("mean3", [P, 3])
    net.q3 = net.sb("q3", [P, 3, F3_IN], BF16)
    net.ident16 = net.sb("ident16", [P, P], BF16)
    net.pick16 = net.sb("pick16", [P, 4], BF16)
    net.part16 = net.sb("part16", [P, 32], BF16)
    net.rot = net.sb("rot", [P, F0_L, 2, 2, NT, F0_HD])


def prepare(net, load, need):
    nc, w = net.nc, net.w

    def body(s, sb, block, _):
        la = sb("la", [P, 8])
        lsum = sb("lsum", [P, 2])
        lexp = sb("lexp", [P, 2])
        absum = sb("absum", [P, 3])
        inv = sb("inv", [P, 3])
        work = sb("work", [P, F3_IN])
        F3 = ("f3_wg", "f3_wu", "f3_wd")

        @block.sync
        def _(sp):
            load(sp)

        @block.tensor
        def _(pe):
            need("base")(pe)
            pe.wait_ge(s["absum_ready"], 1)
            pe.matmul(net.ps[0][:, 0:3], w("ones"), absum[:, :], start=True, stop=True).then_inc(s["total_in_psum"], 1)

        @block.scalar
        def _(act):
            st = Steps(act, s["scalar_step"])
            need("base")(act)
            need("tables")(act)
            st.step(act.activation(net.ident16[:, :], w("ident"), ACT.Copy))
            st.step(act.activation(net.pick16[:, :], w("pick"), ACT.Copy))
            st.step(act.activation(net.part16[:, :], w("part_of"), ACT.Copy))
            st.link(act.activation(net.a3[:, :, :], w("a3_alog").rearrange("p (c n) -> p c n", c=A3_C), ACT.Exp))
            st.link(act.activation(net.a3[:, :, :], net.a3[:, :, :], ACT.Copy, scale=-1.0))
            act.wait_ge(s["lambda_sums"], 1)
            act.activation(lexp[:, :], lsum[:, :], ACT.Exp).then_inc(s["lambda_exp"], 1)
            st.wait()

        @block.vector
        def _(v):
            need("tables")(v)
            st = Steps(v, s["vector_step"])
            half = F0_HD // 2
            for l in range(F0_L):
                for j, (c, n, gain) in enumerate((("rot_q", "rot_qs", f"f0_qs{l}"), ("rot_k", "rot_ks", f"f0_ks{l}"))):
                    co = w(c).rearrange("p (t d) -> p t d", t=NT)
                    si = w(n).rearrange("p (t d) -> p t d", t=NT)
                    st.step(v.tensor_tensor(net.rot[:, l, j, 0], co, bc(w(gain), NT), ALU.mult))
                    st.step(v.tensor_tensor(net.rot[:, l, j, 1, :, 0:half], si[:, :, 0:half], bc(w(gain, half, F0_HD), NT), ALU.mult))
                    st.step(v.tensor_tensor(net.rot[:, l, j, 1, :, half:F0_HD], si[:, :, half:F0_HD], bc(w(gain, 0, half), NT), ALU.mult))
            st.step(v.tensor_copy(net.mask2[:, 0, 0:64], w("win_mask", 0, 64)))
            st.step(v.tensor_copy(net.mask2[:, 1:A2_J, 0:64], bc(w("win_mask", 64, 128), A2_J - 1)))
            st.step(v.tensor_copy(net.mask2[:, :, 64:64 + A2_NB], w("comp_mask").rearrange("p (j n) -> p j n", j=A2_J)))
            for dst, src in ((net.wck, "a2_wkt"), (net.wcv, "a2_wvt")):
                st.step(v.tensor_scalar(dst[:, :, :], w("block_of").rearrange("p (t n) -> p t n", t=NT), w(src), None, ALU.mult))
            st.link(v.tensor_tensor(la[:, :], w("x3_l", 0, 8), w("x3_l", 8, 16), ALU.mult))
            v.tensor_reduce(lsum[:, :], la[:, :].rearrange("p (a b) -> p a b", a=2), AX.X, ALU.add).then_inc(s["lambda_sums"], 1)
            v.wait_ge(s["lambda_exp"], 1)
            st.link(v.tensor_tensor(net.neglam[:, :], lexp[:, 1:2], lexp[:, 0:1], ALU.subtract))
            st.step(v.tensor_scalar(net.neglam[:, :], net.neglam[:, :], -0.2, None, ALU.add))
            for i, k in enumerate(F3):
                last = v.tensor_reduce(absum[:, i:i + 1], w(k), AX.X, ALU.add, apply_absolute_value=True)
            last.then_inc(s["absum_ready"], 1)
            v.wait_ge(s["total_in_psum"], 1)
            st.link(v.tensor_scalar(net.mean3[:, :], net.ps[0][:, 0:3], 1.0 / (D * F3_IN), 1e-5, ALU.mult, ALU.max))
            st.link(v.reciprocal(inv[:, :], net.mean3[:, :]))
            for i, k in enumerate(F3):
                st.link(v.tensor_scalar(work[:, :], w(k), inv[:, i:i + 1], ROUND, ALU.mult, ALU.add))
                st.link(v.tensor_scalar(work[:, :], work[:, :], -ROUND, 1.0, ALU.add, ALU.min))
                st.link(v.tensor_scalar(net.q3[:, i, :], work[:, :], -1.0, None, ALU.max))
            st.wait()

    run_stage(nc, "prepare", body, None, final=True)




def stage_list(net):
    return [
        ("l0_attn", l0_attn),
        ("l0_xattn", lambda n: xattn(n, "x0_wq", "x0_wk", "x0_wv", scale=D ** -0.5)),
        ("l0_ffn", l0_ffn),
        ("l1_attn", l1_attn),
        ("l1_xattn", lambda n: xattn(n, "x1_wq", "x1_wk", "x1_wv", "x1_bq", "x1_bv", "x1_wo", "x1_bo", scale=D ** -0.5)),
        ("l1_ffn", l1_ffn),
        ("l2_attn", l2_attn),
        ("l2_xattn", lambda n: xattn(n, "x2_w", "x2_w", bq="x2_b", relu=True, kd="x2_d", masked=True)),
        ("l2_ffn", l2_ffn),
        ("l3_attn", l3_attn),
        ("l3_xattn", l3_xattn),
        ("l3_ffn", l3_ffn),
    ]


def build(nc, x_in, ctx_in, ctxT_in, mask_in, packed, out, where, pieces, only=None, rows_run=B):
    with ExitStack() as ctx:
        net = Net(nc, ctx, where)
        loaded = {k: ctx.enter_context(nc.semaphore(f"{k}_weights_loaded")) for k in pieces}
        setup_tables(net, ctx)

        with ExitStack() as early:
            net.tables = early.enter_context(nc.sbuf_tensor("table_operands", [P, net.split], F32))

            def load(sp):
                for k, (lo, hi) in pieces.items():
                    to = net.tables[:, lo:hi] if k == "tables" else net.W[:, lo - net.split:hi - net.split]
                    sp.dma_start(to, packed[:, lo:hi]).then_inc(loaded[k], 16)

            def need(*names):
                def wait(eng):
                    for k in names:
                        eng.wait_ge(loaded[k], 16)
                return wait

            prepare(net, load, need)

        with nc.Fori(0, rows_run) as row:
            def enter(s, sb, block, _):
                m8 = sb("m8", [P, S2], mybir.dt.uint8)

                @block.sync
                def _(sp):
                    sp.dma_start(net.x[:, :, :], x_in[bass.ds(row, 1)].rearrange("b (t p) d -> (b p) t d", p=P)).then_inc(s["row_loaded"], 16)
                    sp.dma_start(net.ctxT[:, :], ctxT_in[bass.ds(row, 1)].rearrange("b d k -> (b d) k")).then_inc(s["row_loaded"], 16)
                    sp.dma_start(net.ctxtok[:, :], ctx_in[bass.ds(row, 1)].rearrange("b k d -> (b k) d")).then_inc(s["row_loaded"], 16)
                    sp.dma_start(m8[:, :], mask_in[bass.ds(row, 1)].to_broadcast([P, S2])).then_inc(s["mask_loaded"], 16)
                    sp.wait_ge(s["row_loaded"], 48)

                @block.vector
                def _(v):
                    v.wait_ge(s["mask_loaded"], 16)
                    v.tensor_copy(net.bias[:, :], m8[:, :]).then_inc(s["mask_ready"], 1)
                    v.wait_ge(s["mask_ready"], 1)

            sems = run_stage(nc, "enter", enter, None)
            for k, make in stage_list(net):
                if only is None or k in only:
                    bodies = make(net)
                    for i, body in enumerate(bodies if isinstance(bodies, list) else [bodies]):
                        sems = run_stage(nc, f"{k}{i}", body, need("base", *([k] if k in pieces else [])), before=sems)

            def leave(s, sb, block, _):
                @block.sync
                def _(sp):
                    sp.dma_start(out[bass.ds(row, 1)].rearrange("b (t p) d -> (b p) t d", p=P), net.x[:, :, :]).then_inc(s["row_stored"], 16)
                    sp.wait_ge(s["row_stored"], 16)

            run_stage(nc, "leave", leave, None, before=sems, final=True)


def kernel(**inputs):
    import concourse.bacc as bacc
    from concourse.bass_utils import run_bass_kernel_spmd as run

    a = {k: np.asarray(v) for k, v in inputs.items()}
    packed, where, pieces = pack(a)
    arrays = {
        "x_rows": np.ascontiguousarray(a["x"]),
        "context": np.ascontiguousarray(a["ctx_1024"]),
        "contextT": np.ascontiguousarray(a["ctx_1024"].transpose(0, 2, 1)),
        "mask": np.ascontiguousarray(a["mask_BxS2_bf0"]),
        "packed": packed,
    }
    nc = bacc.Bacc("TRN2", target_bir_lowering=False, num_devices=1)
    args = [nc.dram_tensor(k, v.shape, mybir.dt.from_np(v.dtype), kind="ExternalInput").ap() for k, v in arrays.items()]
    out = nc.dram_tensor("out", (B, T, D), F32, kind="ExternalOutput").ap()
    build(nc, *args, out, where, pieces)
    r = run(nc, [arrays], core_ids=[0])
    return r.results[0]["out"]
```
